# Optimizing a Trainium2 kernel written in Bass

```python
import numpy as np
import jax
import jax.numpy as jnp

def _softmax(x, axis=-1):
    return jax.nn.softmax(x, axis=axis)

def _gelu(x):
    return jax.nn.gelu(x, approximate=True)

def _silu(x):
    return jax.nn.silu(x)

def _sigmoid(x):
    return jax.nn.sigmoid(x)

def _layernorm(x, axis=-1, eps=1e-05):
    m = jnp.mean(x, axis=axis, keepdims=True)
    v = jnp.var(x, axis=axis, keepdims=True)
    return (x - m) / jnp.sqrt(v + eps)

def _scatter_add(tgt, idx, src, axis=0):
    return tgt.at[idx].add(src)

def _segment_sum(src, seg, n):
    return jax.ops.segment_sum(src, seg, n)
kernel_name = 'mk_macaron_d1_jaxref_r8_a5039a'

def setup_inputs(seed: int=0):
    np.random.seed(seed)
    _w = jnp.asarray

    def _L0_attn_setup():
        import jax, jax.numpy as jnp
        import numpy as np
        EPS = 1e-06

        def rmsnorm(x, w):
            return x * jax.lax.rsqrt(jnp.mean(x * x, axis=-1, keepdims=True) + EPS) * w

        def rope(x, freqs):
            xr = x.reshape(x.shape[:-1] + (-1, 2))
            c, s = (jnp.cos(freqs), jnp.sin(freqs))
            x0, x1 = (xr[..., 0], xr[..., 1])
            return jnp.stack([x0 * c - x1 * s, x0 * s + x1 * c], axis=-1).reshape(x.shape)
        B_, L, D = (2, 256, 256)
        Din, H, P, N = (512, 64, 64, 128)
        key = jax.random.key(seed)
        ks = jax.random.split(key, 10)
        sd = lambda fan: 1.0 / np.sqrt(fan)
        f32 = jnp.float32
        return {'x': jax.random.normal(ks[0], (B_, L, D), f32), 'Wx': (jax.random.normal(ks[1], (Din, D)) * sd(D)).astype(f32), 'Wz': (jax.random.normal(ks[2], (Din, D)) * sd(D)).astype(f32), 'WB': (jax.random.normal(ks[3], (H * N, D)) * sd(D)).astype(f32), 'WC': (jax.random.normal(ks[4], (H * N, D)) * sd(D)).astype(f32), 'Wdt': jax.random.uniform(ks[5], (H, D), f32, -0.0001, 0.0001), 'Wlam': (jax.random.normal(ks[6], (H, D)) * sd(D)).astype(f32), 'Wth': (jax.random.normal(ks[7], (H * (N // 2), D)) * sd(D)).astype(f32), 'A_log': jnp.log(jnp.linspace(1.0, N, H)).astype(f32), 'Bn_w': jnp.ones((N,), f32), 'Cn_w': jnp.ones((N,), f32), 'B_bias': jnp.ones((H, N), f32), 'C_bias': jnp.ones((H, N), f32), 'Wout': (jax.random.normal(ks[8], (D, Din)) * sd(Din)).astype(f32)}
    _L0_attn_in = _L0_attn_setup()

    def _L0_ffn_setup():
        import jax, jax.numpy as jnp
        import numpy as np
        TOP_K = 8
        key = jax.random.key(seed)
        ks = jax.random.split(key, 5)
        B, S, H, I, E = (1, 256, 256, 96, 64)
        scale = 0.02
        return {'hidden_states': jax.random.normal(ks[0], (B, S, H), jnp.float32), 'Wr': jax.random.normal(ks[1], (E, H), jnp.float32) * scale, 'Wg': jax.random.normal(ks[2], (E, H, I), jnp.float32) * scale, 'Wu': jax.random.normal(ks[3], (E, H, I), jnp.float32) * scale, 'Wd': jax.random.normal(ks[4], (E, I, H), jnp.float32) * scale}
    _L0_ffn_in = _L0_ffn_setup()
    _d = {'L0_attn_x': _L0_attn_in['x'], 'L0_attn_Wx': _L0_attn_in['Wx'], 'L0_attn_Wz': _L0_attn_in['Wz'], 'L0_attn_WB': _L0_attn_in['WB'], 'L0_attn_WC': _L0_attn_in['WC'], 'L0_attn_Wdt': _L0_attn_in['Wdt'], 'L0_attn_Wlam': _L0_attn_in['Wlam'], 'L0_attn_Wth': _L0_attn_in['Wth'], 'L0_attn_A_log': _L0_attn_in['A_log'], 'L0_attn_Bn_w': _L0_attn_in['Bn_w'], 'L0_attn_Cn_w': _L0_attn_in['Cn_w'], 'L0_attn_B_bias': _L0_attn_in['B_bias'], 'L0_attn_C_bias': _L0_attn_in['C_bias'], 'L0_attn_Wout': _L0_attn_in['Wout'], 'L0_ffn_Wr': _L0_ffn_in['Wr'], 'L0_ffn_Wg': _L0_ffn_in['Wg'], 'L0_ffn_Wu': _L0_ffn_in['Wu'], 'L0_ffn_Wd': _L0_ffn_in['Wd']}
    _x0 = _d['L0_attn_x']
    _d['L0_attn_x'] = jax.random.normal(jax.random.fold_in(jax.random.key(seed), 1), (4, 512, 256), dtype=_x0.dtype)
    del _x0
    return _d

def reference(L0_attn_x, L0_attn_Wx, L0_attn_Wz, L0_attn_WB, L0_attn_WC, L0_attn_Wdt, L0_attn_Wlam, L0_attn_Wth, L0_attn_A_log, L0_attn_Bn_w, L0_attn_Cn_w, L0_attn_B_bias, L0_attn_C_bias, L0_attn_Wout, L0_ffn_Wr, L0_ffn_Wg, L0_ffn_Wu, L0_ffn_Wd):

    def _L0_attn_ref(x, Wx, Wz, WB, WC, Wdt, Wlam, Wth, A_log, Bn_w, Cn_w, B_bias, C_bias, Wout):
        import jax, jax.numpy as jnp
        import numpy as np
        EPS = 1e-06

        def rmsnorm(x, w):
            return x * jax.lax.rsqrt(jnp.mean(x * x, axis=-1, keepdims=True) + EPS) * w

        def rope(x, freqs):
            xr = x.reshape(x.shape[:-1] + (-1, 2))
            c, s = (jnp.cos(freqs), jnp.sin(freqs))
            x0, x1 = (xr[..., 0], xr[..., 1])
            return jnp.stack([x0 * c - x1 * s, x0 * s + x1 * c], axis=-1).reshape(x.shape)
        B_, L, D = x.shape
        H = A_log.shape[0]
        N = B_bias.shape[1]
        Din = Wx.shape[0]
        P = Din // H
        xp = x @ Wx.T
        z = x @ Wz.T
        Bm = (x @ WB.T).reshape(B_, L, H, N)
        Cm = (x @ WC.T).reshape(B_, L, H, N)
        Bm = rmsnorm(Bm, Bn_w) + B_bias
        Cm = rmsnorm(Cm, Cn_w) + C_bias
        dt = jax.nn.softplus(x @ Wdt.T)
        lam = jax.nn.sigmoid(x @ Wlam.T)
        theta = (x @ Wth.T).reshape(B_, L, H, N // 2)
        theta_cumsum = jnp.cumsum(theta * dt[..., None], axis=1)
        Bm = rope(Bm, theta_cumsum)
        Cm = rope(Cm, theta_cumsum)
        xh = xp.reshape(B_, L, H, P)
        A = -jnp.exp(A_log)
        alpha = jnp.exp(dt * A)
        beta = (1.0 - lam) * dt * alpha
        gamma = lam * dt

        def step(carry, inputs):
            h, B_prev, x_prev = carry
            Bt, Ct, xt, at, bt, gt = inputs
            h = at[..., None, None] * h + jnp.einsum('bh,bhn,bhp->bhnp', bt, B_prev, x_prev) + jnp.einsum('bh,bhn,bhp->bhnp', gt, Bt, xt)
            yt = jnp.einsum('bhn,bhnp->bhp', Ct, h)
            return ((h, Bt, xt), yt)
        h0 = jnp.zeros((B_, H, N, P), x.dtype)
        carry0 = (h0, jnp.zeros((B_, H, N), x.dtype), jnp.zeros((B_, H, P), x.dtype))
        seq = (Bm.transpose(1, 0, 2, 3), Cm.transpose(1, 0, 2, 3), xh.transpose(1, 0, 2, 3), alpha.transpose(1, 0, 2), beta.transpose(1, 0, 2), gamma.transpose(1, 0, 2))
        _, ys = jax.lax.scan(step, carry0, seq)
        y = ys.transpose(1, 0, 2, 3).reshape(B_, L, H * P)
        y = y * jax.nn.silu(z)
        return y @ Wout.T

    def _L0_ffn_ref(hidden_states, Wr, Wg, Wu, Wd):
        import jax, jax.numpy as jnp
        import numpy as np
        TOP_K = 8
        B, S, H = hidden_states.shape
        E = Wr.shape[0]
        T = B * S
        x = hidden_states.reshape(T, H)
        logits = jnp.einsum('th,eh->te', x, Wr)
        probs = jax.nn.softmax(logits.astype(jnp.float32), axis=-1)
        w, idx = jax.lax.top_k(probs, TOP_K)
        w = w / jnp.sum(w, axis=-1, keepdims=True)
        w = w.astype(x.dtype)
        combine = jnp.zeros((T, E), x.dtype).at[jnp.arange(T)[:, None], idx].add(w)
        gate = jnp.einsum('th,ehi->eti', x, Wg)
        up = jnp.einsum('th,ehi->eti', x, Wu)
        h = jax.nn.silu(gate) * up
        out = jnp.einsum('eti,eih,te->th', h, Wd, combine)
        return out.reshape(B, S, H)
    x = L0_attn_x
    x = x + 0.5 * _L0_ffn_ref(_layernorm(x, axis=-1), L0_ffn_Wr, L0_ffn_Wg, L0_ffn_Wu, L0_ffn_Wd)
    x = x + _L0_attn_ref(_layernorm(x, axis=-1), L0_attn_Wx, L0_attn_Wz, L0_attn_WB, L0_attn_WC, L0_attn_Wdt, L0_attn_Wlam, L0_attn_Wth, L0_attn_A_log, L0_attn_Bn_w, L0_attn_Cn_w, L0_attn_B_bias, L0_attn_C_bias, L0_attn_Wout)
    x = x + 0.5 * _L0_ffn_ref(_layernorm(x, axis=-1), L0_ffn_Wr, L0_ffn_Wg, L0_ffn_Wu, L0_ffn_Wd)
    return x

_drawn_inputs = setup_inputs


def setup_inputs(seed=0):
    import zlib

    import numpy as np

    out = dict(_drawn_inputs(seed))
    spreads = {'L0_attn_Bn_w': (1.0, 0.6),
     'L0_attn_Cn_w': (1.0, 0.6),
     'L0_attn_B_bias': (1.0, 0.2),
     'L0_attn_C_bias': (1.0, 0.2)}
    factors = {'L0_attn_Wdt': 64.0,
     'L0_attn_Wth': 3.48,
     'L0_ffn_Wr': 8.0,
     'L0_ffn_Wg': 8.0,
     'L0_ffn_Wu': 8.0,
     'L0_ffn_Wd': 8.0}
    for name, (base, spread) in spreads.items():
        noise = np.random.default_rng([zlib.crc32(name.encode()), seed]).standard_normal(out[name].shape)
        drawn = base * np.exp(spread * noise) if base else spread * noise
        out[name] = jnp.asarray(drawn.astype(out[name].dtype))
    for name, factor in factors.items():
        out[name] = (out[name] * factor).astype(out[name].dtype)
    return out
```

```python
from contextlib import ExitStack

import numpy as np
import concourse.bass as bass
from concourse import mybir

F32 = mybir.dt.float32
F32R = mybir.dt.float32r
ALU = mybir.AluOpType
ACT = mybir.ActivationFunctionType
AX_X = mybir.AxisListType.X

P = 128
BATCH, SEQ, D = 4, 512, 256
KD = D // P
NE, NI, TOPK = 64, 96, 8
GE = 4
GT = GE * NI // P
NG = NE // GE
GW = 3 * GT * D
PIECE = GW // GT
NT = NG * GT
TT = SEQ // P
LAG = 2
NH, HP, NS = 64, 8, 128
NP = NH // 2
CL = 64
NC = SEQ // CL
DIN = NH * HP
KI = DIN // P
UN = 4
PW = 2 * HP
ROWW = 2 * SEQ + NC
BCW, THW = 4 * KD * P, KD * P
EPS_LN, EPS_NORM = 1e-5, 1e-6
MAGIC = 12582912.0
TWO_PI = 6.283185


class Event:
    unit = 1

    def __init__(self, all_events, ctx, nc, name, ahead=0):
        self.sem, self.ahead = ctx.enter_context(nc.semaphore(name)), 1 + ahead
        all_events.append(self)

    def give_ahead(self, eng):
        eng.sem_inc(self.sem, self.ahead)

    def wait(self, eng, count):
        if isinstance(count, int) and count + self.ahead <= 1:
            return
        eng.wait_ge(self.sem, count * self.unit + self.ahead)

    def hold(self, eng, count):
        self.wait(eng, count)
        eng.nop(nofuse=True)

    def mark(self, ins):
        ins.then_inc(self.sem, self.unit)


class Arrival(Event):
    unit = 16


def split_matmul(e, dst, pairs, start, stop):
    n, c, ins = len(pairs) * 3, 0, None
    for (ah, al), (mh, ml) in pairs:
        for a, m in ((ah, mh), (al, mh), (ah, ml)):
            ins = e.matmul(dst, a, m, start=start and c == 0, stop=stop and c == n - 1,
                           skip_group_check=not (start and stop))
            c += 1
    return ins


def build(nc, x_in, w_ffn, w_router, w_bc, w_th, w_x, w_z, w_dtl, w_dth, a_log, w_out, bias_in, norm_w_in,
          sel_ffn_in, ident_in, cst_in, out):
    with ExitStack() as ctx:
        events = []

        def ev(name, ahead=0):
            return Event(events, ctx, nc, name, ahead)

        def arr(name):
            return Arrival(events, ctx, nc, name)

        def sb_in(c):
            return lambda name, shape, dt=F32: c.enter_context(nc.sbuf_tensor(name, shape, dt))

        bank = [ctx.enter_context(nc.psum_tensor(f"bank{i}", [P, SEQ], F32)) for i in range(8)]

        sb = sb_in(ctx)
        xT = sb("xT", [P, KD, SEQ])
        xn = sb("xn", [P, KD, SEQ + 2])
        xh, xl = sb("xh", [P, KD, SEQ], F32R), sb("xl", [P, KD, SEQ], F32R)
        xc, sq = sb("xc", [P, KD, SEQ]), sb("sq", [P, KD, SEQ])
        std, rstd = sb("std", [P, SEQ]), sb("rstd", [P, SEQ])
        eps_ln, eps_nm, magic, half_pi = (sb(n, [P, 1]) for n in ("eps_ln", "eps_nm", "magic", "half_pi"))
        mean_w = sb("mean_w", [P, P])
        zero_w = sb("zero_w", [P, P], F32R)
        ident = sb("ident", [P, P])
        wr_sb = sb("wr_sb", [P, KD, NE])
        CST = {}
        at_col = 0
        for n, w in (("shift_mask", SEQ), ("diag_mask", SEQ), ("last_row", 1), ("head_mask", 32 * (NC - 1)),
                     ("chunk_mask", P), ("row_sel", P), ("one_hot", 4 * 8)):
            CST[n] = (at_col, w)
            at_col += w
        cst = sb("cst", [P, at_col])
        constant = lambda n: cst[:, CST[n][0]:CST[n][0] + CST[n][1]]
        row_sel = sb("row_sel", [P, P], F32R)
        sel = sb("sel", [2 * GE, GT, P], F32R)

        with ExitStack() as ffn_ctx:
            sb = sb_in(ffn_ctx)
            sel_raw = sb("sel_raw", [2 * GE, GT, P])
            lmax, wsum, wrec = sb("lmax", [P, TT]), sb("wsum", [P, TT]), sb("wrec", [P, TT])
            lg, ex, rest, wsel, comb = (sb(n, [P, TT, NE]) for n in ("lg", "ex", "rest", "wsel", "comb"))
            top = sb("top", [P, TT, TOPK])
            comb_h, comb_l = sb("comb_h", [NE, SEQ], F32R), sb("comb_l", [NE, SEQ], F32R)
            comb_rows = [sb(f"comb_rows{i}", [2 * GE, SEQ], F32R) for i in range(2)]
            w_raw = [sb(f"w_raw{i}", [P, GW]) for i in range(2)]
            w_hi = [sb(f"w_hi{i}", [P, GW], F32R) for i in range(2)]
            w_lo = [sb(f"w_lo{i}", [P, GW], F32R) for i in range(2)]
            sg, h1, hf = ([sb(f"{n}{i}", [P, SEQ]) for i in range(2)] for n in ("sg", "h1_", "hf"))
            h_hi = [sb(f"h_hi{i}", [P, SEQ], F32R) for i in range(3)]
            h_lo = [sb(f"h_lo{i}", [P, SEQ], F32R) for i in range(3)]
        comb_dram = nc.dram_tensor("comb_dram", [NE, 2, SEQ], F32R, kind="Internal").ap().bitcast(F32)

        attn_ctx = ctx
        sb = sb_in(attn_ctx)
        xbc = [sb(f"xbc{i}", [P, 4, SEQ]) for i in range(4)]
        rot = [sb(f"rot{i}", [P, 4, SEQ]) for i in range(2)]
        tmp = sb("tmp", [P, 4, SEQ])
        sn, cs = ([sb(f"{n}{i}", [P, SEQ]) for i in range(2)] for n in ("sn", "cs"))
        ths, turns, rnd, nfr = (sb(n, [P, SEQ]) for n in ("ths", "turns", "rnd", "nfr"))
        sqt = sb("sqt", [P, 4, SEQ])
        sqs = sb("sqs", [P, 2, SEQ])
        btr = sb("btr", [P, 2, SEQ])
        x1, x2 = sb("x1", [P, NH, TT, HP]), sb("x2", [P, NH, TT, HP])
        x1p = [sb(f"x1p{i}", [P, P]) for i in range(4)]
        x2p = [sb(f"x2p{i}", [P, P]) for i in range(4)]
        xwp = [sb(f"xwp{i}", [P, P]) for i in range(2)]
        st_in = sb("st_in", [P, 32 * NC])
        st = sb("st", [P, 32 * NC])
        ysb = sb("ysb", [P, TT, DIN])
        decay_t = sb("decay_t", [P, NC, NP, 2])
        rows = sb("rows", [P, ROWW], F32R)
        rrow = sb("rrow", [P, 4, SEQ], F32R)
        wb_raw, th_raw = ([sb(f"{n}{i}", [P, w]) for i in range(2)] for n, w in (("wb_raw", BCW), ("th_raw", THW)))
        wb_hi, wb_lo = ([sb(f"{n}{i}", [P, BCW], F32R) for i in range(2)] for n in ("wb_hi", "wb_lo"))
        th_hi, th_lo = ([sb(f"{n}{i}", [P, THW], F32R) for i in range(2)] for n in ("th_hi", "th_lo"))
        wx_sb = xbc[3][:, 0:KD, :]
        wz_sb = xbc[0][:, 0:KD, :]
        wo_sb = xbc[0][:, KD:, :].rearrange("p a b -> p (a b)").rearrange("p (f m) -> p f m", f=KI)
        wdtl_sb, wdth_sb = sb("wdtl_sb", [P, KD, 2 * NH]), sb("wdth_sb", [P, KD, NH])
        neg_a = sb("neg_a", [NH, 1])
        bias = sb("bias", [P, NP, 4])
        norm_w = sb("norm_w", [P, 4])
        stdr = sb("stdr", [8, SEQ])
        rc_in, rc, rc_hi, rc_lo = sb("rc_in", [P, 32]), sb("rc", [P, 32]), sb("rc_hi", [P, 32], F32R), sb("rc_lo", [P, 32], F32R)
        dks = [xc[:, i, :] for i in range(2)]
        m1, m2 = sq[:, 0, :], sq[:, 1, :]
        ytmp = sb("ytmp", [CL, SEQ])
        ones = std[:, :]
        cum = rstd
        afr = ths
        dth = rot[0][0:NH, 0, :]
        alpha = rot[0][0:NH, 1, :]
        alpha0 = rot[0][0:NH, 2, :]
        dect = rot[0][0:NH, 3, :]
        hrow = sqt[0:NH, 0:3, :].rearrange("p a b -> p (a b)")[:, 0:ROWW]
        dtk = tmp[:, 0, :].rearrange("p (s t n) -> p s t n", s=2, t=TT)
        lamk = tmp[:, 1, :].rearrange("p (s t n) -> p s t n", s=2, t=TT)
        gam = tmp[:, 2, 0:TT * NH].rearrange("p (t n) -> p t n", t=TT)
        oml = tmp[:, 2, TT * NH:].rearrange("p (t n) -> p t n", t=TT)
        dlt = tmp[:, 3, 0:TT * NH].rearrange("p (t n) -> p t n", t=TT)
        coef = tmp[:, 3, TT * NH:].rearrange("p (t n) -> p t n", t=TT)
        hrow_hi = rows[0:NH, :]
        hrow_lo = rrow[0:NH, :, :].rearrange("p a b -> p (a b)")[:, 0:ROWW]
        silu_z = rot[0]
        gated = rot[1]
        row_dram = nc.dram_tensor("row_dram", [NP, 4, ROWW], F32R, kind="Internal").ap().bitcast(F32)
        rr_dram = [nc.dram_tensor(f"rr_dram{i}", [2, 8, SEQ], F32R, kind="Internal").ap().bitcast(F32) for i in range(2)]

        a_const, a_x, a_out = arr("a_const"), arr("a_x"), arr("a_out")
        a_wraw = [arr(f"a_wraw{i}") for i in range(2)]
        a_combw, a_comb = arr("a_combw"), [arr(f"a_comb{i}") for i in range(2)]
        e_init, e_phase = ev("e_init"), ev("e_phase")
        e_mean, e_xc, e_sq, e_var, e_std, e_rstd, e_xn, e_xh, e_xl = (
            ev(n) for n in "e_mean e_xc e_sq e_var e_std e_rstd e_xn e_xh e_xl".split())
        e_lg, e_sub, e_ex, e_chain, e_comb, e_ct, e_ch, e_cl = (
            ev(n) for n in "e_lg e_sub e_ex e_chain e_comb e_ct e_ch e_cl".split())
        e_hz = ev("e_hz")
        e_g, e_u, e_cb, e_down = ev("e_g"), ev("e_u"), ev("e_cb", 2 * GT), ev("e_down")
        e_silu, e_h1, e_h = ev("e_silu", 2), ev("e_h1", 2), ev("e_h", 2)
        e_hh, e_hl = ev("e_hh", LAG), ev("e_hl", LAG)
        e_wA, e_wP = ev("e_wA"), ev("e_wP")

        PHASES = 3

        def end_phase(e, n):
            e_phase.mark(e.drain())
            e_phase.hold(e, 5 * (n + 1))

        def ln_pe(e, r):
            for k in range(KD):
                ins = e.matmul(bank[2][:, :], mean_w[:, :], xT[:, k, :], start=k == 0, stop=k == KD - 1)
            e_mean.mark(ins)
            e_sq.wait(e, r + 1)
            for k in range(KD):
                ins = e.matmul(bank[3][:, :], mean_w[:, :], sq[:, k, :], start=k == 0, stop=k == KD - 1)
            e_var.mark(ins)

        def ln_dve(e, r):
            e_mean.wait(e, r + 1)
            for k in range(KD):
                ins = e.tensor_tensor(xc[:, k, :], xT[:, k, :], bank[2][:, :], ALU.subtract)
            e_xc.mark(ins)
            e_std.wait(e, r + 1)
            e_rstd.mark(e.reciprocal(rstd[:, :], std[:, :]))
            e_rstd.wait(e, r + 1)
            for k in range(KD):
                e_xn.mark(e.tensor_tensor(xn[:, k, 0:SEQ], xc[:, k, :], rstd[:, :], ALU.mult))
            for k in range(KD):
                e_xh.wait(e, KD * r + k + 1)
                e_xl.mark(e.tensor_tensor(xl[:, k, :], xn[:, k, 0:SEQ], xh[:, k, :].bitcast(F32), ALU.subtract))

        def ln_act(e, r):
            e_xc.wait(e, r + 1)
            e_sq.mark(e.activation(sq[:, :, :], xc[:, :, :], ACT.Square))
            e_var.wait(e, r + 1)
            e_std.mark(e.activation(std[:, :], bank[3][:, :], ACT.Sqrt, bias=eps_ln[:, 0:1]))
            for k in range(KD):
                e_xn.wait(e, KD * r + k + 1)
                e_xh.mark(e.activation(xh[:, k, :], xn[:, k, 0:SEQ], ACT.Copy))

        lgb, ctb = bank[4], bank[5]

        def router_pe(e, f, r):
            e_xn.wait(e, KD * (r + 1))
            for t in range(TT):
                for k in range(KD):
                    ins = e.matmul(lgb[:, t * NE:(t + 1) * NE], xn[:, k, t * P:(t + 1) * P], wr_sb[:, k, :],
                                   start=k == 0, stop=k == KD - 1)
            e_lg.mark(ins)
            e_comb.hold(e, f + 1)
            for t in range(TT):
                ins = e.transpose(ctb[0:NE, t * P:(t + 1) * P], comb[:, t, :], ident[:, :])
            e_ct.mark(ins)

        CHAIN = 9

        def router_dve(e, f):
            n = [0]

            def step(ins):
                e_chain.mark(ins)
                n[0] += 1
                e_chain.hold(e, f * CHAIN + n[0])

            logits = lgb[:, 0:TT * NE].rearrange("p (t n) -> p t n", t=TT)
            wide = lambda a: a[:, :].unsqueeze(2).to_broadcast([P, TT, NE])
            e_lg.wait(e, f + 1)
            step(e.tensor_reduce(lmax[:, :], logits, AX_X, ALU.max))
            e_sub.mark(e.tensor_tensor(lg[:, :, :], logits, wide(lmax), ALU.subtract))
            e_ex.hold(e, f + 1)
            for t in range(TT):
                ins = e.max(top[:, t, :], ex[:, t, :])
            step(ins)
            for t in range(TT):
                step(e.match_replace(rest[:, t, :], top[:, t, :], ex[:, t, :], -1.0))
            step(e.scalar_tensor_tensor(wsel[:, :, :], rest[:, :, :], 0.0, ex[:, :, :], ALU.is_lt, ALU.mult))
            step(e.tensor_reduce(wsum[:, :], wsel[:, :, :], AX_X, ALU.add))
            step(e.reciprocal(wrec[:, :], wsum[:, :]))
            assert n[0] == CHAIN
            e_comb.mark(e.tensor_tensor(comb[:, :, :], wsel[:, :, :], wide(wrec), ALU.mult))
            e_ch.wait(e, f + 1)
            e_cl.mark(e.tensor_tensor(comb_l[:, :], ctb[0:NE, :], comb_h[:, :].bitcast(F32), ALU.subtract))

        def router_act(e, f):
            e_sub.wait(e, f + 1)
            e_ex.mark(e.activation(ex[:, :, :], lg[:, :, :], ACT.Exp))
            e_ct.wait(e, f + 1)
            e_ch.mark(e.activation(comb_h[:, :], ctb[0:NE, :], ACT.Copy))

        def router_sp(e, f):
            e_ch.hold(e, f + 1)
            a_combw.mark(e.dma_start(comb_dram[:, 0, :], comb_h[:, :].bitcast(F32)))
            e_cl.hold(e, f + 1)
            a_combw.mark(e.dma_start(comb_dram[:, 1, :], comb_l[:, :].bitcast(F32)))
            a_combw.hold(e, 2 * (f + 1))

        DOWNS = NT + LAG
        SPLITS = NG * GT

        wg = lambda w, k, i: w[:, k * GT * P + i * P:k * GT * P + (i + 1) * P]
        wu = lambda w, k, i: wg(w, KD + k, i)
        wd = lambda w, i, m: w[:, 2 * KD * GT * P + i * D + m * P:2 * KD * GT * P + i * D + (m + 1) * P]
        piece = lambda w, i: w[:, i * PIECE:(i + 1) * PIECE]

        def each_group(e, f, body):
            with e.Fori(0, NG // 2 - 1) as it:
                for g in range(2):
                    body(g, f * NG + it * 2 + g, it, False)
            for g in range(2):
                body(g, f * NG + NG - 2 + g, NG // 2 - 1, True)

        def ffn_pe(e, f):
            e_hz.wait(e, f + 1)
            for m in range(KD):
                e.matmul(bank[m][:, :], zero_w[:, :], xh[:, 0, :], start=True, stop=False, skip_group_check=True)

            def down(i):
                for m in range(KD):
                    ins = split_matmul(e, bank[m][:, :],
                                       [((wd(w_hi[i // GT], i % GT, m), wd(w_lo[i // GT], i % GT, m)),
                                         (h_hi[i % 3][:, :], h_lo[i % 3][:, :]))], False, False)
                e_down.mark(ins)

            def group(g, G, it, last):
                for i in range(GT):
                    T = G * GT + i
                    s = (g * GT + i) % 2
                    if i == 0:
                        e_wP.wait(e, GT * G + 2)
                    if i == LAG:
                        e_wP.wait(e, GT * G + 3)
                    e_silu.wait(e, T + 1 - 2)
                    e_g.mark(split_matmul(e, bank[2 + s][:, :],
                                          [((wg(w_hi[g], k, i), wg(w_lo[g], k, i)), (xh[:, k, :], xl[:, k, :]))
                                           for k in range(KD)], True, True))
                    e_h1.wait(e, T + 1 - 2)
                    e_u.mark(split_matmul(e, bank[4 + s][:, :],
                                          [((wu(w_hi[g], k, i), wu(w_lo[g], k, i)), (xh[:, k, :], xl[:, k, :]))
                                           for k in range(KD)], True, True))
                    if i == 0:
                        a_comb[g].wait(e, f * (NG // 2) + it + 1)
                    e_h.wait(e, T + 1 - 2)
                    e_cb.mark(e.matmul(bank[6 + s][:, :], sel[:, i, :], comb_rows[g][:, :], start=True, stop=True))
                    e_hl.wait(e, T + 1 - LAG)
                    down((g * GT + i - LAG) % (2 * GT))

            each_group(e, f, group)
            for j in range(LAG):
                e_hl.wait(e, (f + 1) * NT - LAG + j + 1)
                down(2 * GT - LAG + j)

        def ffn_act(e, f):
            a_wraw[0].wait(e, f * (NG // 2) + 1)
            for i in range(GT):
                e_wA.mark(e.activation(piece(w_hi[0], i), piece(w_raw[0], i), ACT.Copy))

            def group(g, G, it, last):
                for i in range(GT):
                    T = G * GT + i
                    s = (g * GT + i) % 2
                    tau = (it * 2 + g) * GT + i
                    e_g.wait(e, T + 1)
                    e_h1.wait(e, T + 1 - 2)
                    e_silu.mark(e.activation(sg[s][:, :], bank[2 + s][:, :], ACT.Silu))
                    e_h.wait(e, T + 1)
                    e_down.wait(e, f * DOWNS + tau)
                    e_hh.mark(e.activation(h_hi[(g * GT + i) % 3][:, :], hf[s][:, :], ACT.Copy))
                    if last and g:
                        continue
                    nx = 1 - g
                    a_wraw[nx].wait(e, f * (NG // 2) + it + 1 + g)
                    if i < 2:
                        e_u.wait(e, GT * G)
                    else:
                        e_down.wait(e, f * DOWNS + (it * 2 + g) * GT + LAG)
                    e_wA.mark(e.activation(piece(w_hi[nx], i), piece(w_raw[nx], i), ACT.Copy))

            each_group(e, f, group)

        def ffn_pool(e, f):
            def lo(s, i):
                e_wP.mark(e.tensor_tensor(piece(w_lo[s], i), piece(w_raw[s], i), piece(w_hi[s], i).bitcast(F32), ALU.subtract))

            for i in range(GT):
                e_wA.wait(e, f * SPLITS + i + 1)
                lo(0, i)

            def group(g, G, it, last):
                if not (last and g):
                    for i in range(GT):
                        e_wA.wait(e, GT * (G + 1) + i + 1)
                        lo(1 - g, i)

            each_group(e, f, group)

        def ffn_start_dve(e, f):
            for m in range(KD):
                for i in range(GT - LAG, GT):
                    e.memset(wd(w_hi[1], i, m).bitcast(F32), 0.0)
                    e.memset(wd(w_lo[1], i, m).bitcast(F32), 0.0)
            for sl in range(3 - LAG, 3):
                e.memset(h_hi[sl][:, :].bitcast(F32), 0.0)
                ins = e.memset(h_lo[sl][:, :].bitcast(F32), 0.0)
            e_hz.mark(ins)

        def ffn_dve(e, f):
            def group(g, G, it, last):
                for i in range(GT):
                    T = G * GT + i
                    s = (g * GT + i) % 2
                    e_silu.wait(e, T + 1)
                    e_u.wait(e, T + 1)
                    e_h1.mark(e.tensor_tensor(h1[s][:, :], sg[s][:, :], bank[4 + s][:, :], ALU.mult))
                    e_cb.wait(e, T + 1)
                    e_h1.wait(e, T + 1)
                    e_h.mark(e.tensor_tensor(hf[s][:, :], h1[s][:, :], bank[6 + s][:, :], ALU.mult))
                    e_hh.wait(e, T + 1)
                    e_hl.mark(e.tensor_tensor(h_lo[(g * GT + i) % 3][:, :], hf[s][:, :],
                                              h_hi[(g * GT + i) % 3][:, :].bitcast(F32), ALU.subtract))

            each_group(e, f, group)
            e_down.wait(e, (f + 1) * DOWNS)
            for m in range(KD):
                e.scalar_tensor_tensor(xT[:, m, :], bank[m][:, :], 0.5, xT[:, m, :], ALU.mult, ALU.add)

        def ffn_load_sp(e, f):
            for g in range(2):
                a_wraw[g].mark(e.dma_start(w_raw[g][:, :], w_ffn[g]))

        def ffn_sp(e, f):
            def group(g, G, it, last):
                e_cb.wait(e, GT * (G - 1))
                n = it * 2 + g
                src = comb_dram[n * GE:(n + 1) * GE] if last else comb_dram[bass.ds(n * GE, GE), :, :]
                a_comb[g].mark(e.dma_start(comb_rows[g][:, :].bitcast(F32), src.rearrange("n h t -> (n h) t")))
                if not last:
                    e_wP.wait(e, GT * (G + 1))
                    a_wraw[g].mark(e.dma_start(w_raw[g][:, :], w_ffn[bass.ds(n + 2, 1), :, :].rearrange("a p c -> (a p) c")))

            each_group(e, f, group)

        a_r1, a_r2, a_roww = arr("a_r1"), arr("a_r2"), arr("a_roww")
        a_rows, a_rr = [arr(f"a_rows{i}") for i in range(4)], [arr(f"a_rr{i}") for i in range(2)]
        a_wb, a_th = [arr(f"a_wb{i}") for i in range(2)], [arr(f"a_th{i}") for i in range(2)]
        a_aw, a_tw = arr("a_aw"), arr("a_tw")
        e_bA, e_bP, e_tA, e_tP = ev("e_bA"), ev("e_bP"), ev("e_tA"), ev("e_tP")
        e_th, e_dtb, e_ths, e_tu, e_cum = ev("e_th", 1), ev("e_dtb"), ev("e_ths"), ev("e_tu"), ev("e_cum")
        e_rnd, e_nfr, e_afr, e_cs = ev("e_rnd"), ev("e_nfr"), ev("e_afr"), ev("e_cs")
        e_rB, e_rC, e_aB, e_xb, e_xcc = ev("e_rB"), ev("e_rC", 2), ev("e_aB"), ev("e_xb"), ev("e_xcc")
        e_t, e_R, e_D, e_xw, e_xp = ev("e_t", 6), ev("e_R"), ev("e_D"), ev("e_xw"), ev("e_xp")
        e_G, e_M, e_bte, e_bt = ev("e_G"), ev("e_M", 1), ev("e_bte"), ev("e_bt", 4)
        e_S, e_sm, e_H, e_Y, e_yev = ev("e_S", 1), ev("e_sm"), ev("e_H", 2), ev("e_Y", 3), ev("e_yev")
        e_pj, e_X, e_sqs, e_ssm, e_sr = ev("e_pj", 4), ev("e_X", 2), ev("e_sqs", 2), ev("e_ssm", 2), ev("e_sr")
        e_rl, e_p1, e_p2, e_p3, e_p4, e_p5, e_pc = (ev(n) for n in "e_rl e_p1 e_p2 e_p3 e_p4 e_p5 e_pc".split())
        e_z, e_sz, e_yT, e_gt, e_o = (ev(n) for n in "e_z e_sz e_yT e_gt e_o".split())
        W = [bank[4], bank[5], bank[6], bank[7]]
        XBANK = [bank[0], bank[1]]
        SSB, YB = bank[2], bank[3]
        pair_w = lambda w, i, k: w[:, (i * KD + k) * P:(i * KD + k + 1) * P]
        xpair = [(xh[:, k, :], xl[:, k, :]) for k in range(KD)]
        y4 = lambda a: a.rearrange("p (k h d) -> p k h d", k=NC, h=2 * UN)

        def prep_pe(e, b):
            a_aw.wait(e, 6 * (b + 1))
            for k in range(KD):
                ins = e.matmul(W[0][0:NH, :], wdth_sb[:, k, :], xn[:, k, 0:SEQ], start=k == 0, stop=k == KD - 1)
            for s in range(2):
                for t in range(TT):
                    for k in range(KD):
                        ins = e.matmul(W[1 + s][:, t * P:(t + 1) * P], xn[:, k, t * P + s:(t + 1) * P + s], wdtl_sb[:, k, :],
                                       start=k == 0, stop=k == KD - 1)
            e_p1.mark(ins)
            for t in range(TT):
                for k in range(KD):
                    ins = e.matmul(bank[t][:, :], xn[:, k, t * P:(t + 1) * P], wx_sb[:, k, :], start=k == 0, stop=k == KD - 1)
            e_p2.mark(ins)
            e_p4.hold(e, b + 1)
            for k in range(NC):
                ins = e.matmul(W[3][CL:P, k * CL:(k + 1) * CL], dect[:, k * CL:(k + 1) * CL], ident[0:NH, 0:NH],
                               start=True, stop=True)
            e_p5.mark(ins)

        def prep_act(e, b):
            e_p1.wait(e, b + 1)
            parts = ((sp_e[0:NH, 0, :], W[0][0:NH, :]), (tok(sp_e, 1), steps_of(0)), (tok(sp_e, 2), steps_of(1)))
            for s in range(2):
                ins = e.activation(lamk[:, s], tail_of(s), ACT.Sigmoid)
            e_p3.mark(ins)
            for o, i in parts:
                ins = e.activation(o, i, ACT.Abs)
            e_pc.mark(ins)
            e_pc.wait(e, 6 * b + 1)
            e.activation(hm(sp_e), hm(sp_e), ACT.Exp, scale=-1.0)
            e_pc.mark(e.activation(tm(sp_e), tm(sp_e), ACT.Exp, scale=-1.0))
            e_pu.wait(e, b + 1)
            e.activation(hm(sp_l), hm(sp_u), ACT.Ln)
            e_pc.mark(e.activation(tm(sp_l), tm(sp_u), ACT.Ln))
            e_pc.mark(e.activation(neg_a[:, :], neg_a[:, :], ACT.Exp))
            e_pc.wait(e, 6 * b + 4)
            e_pc.mark(e.activation(neg_a[:, :], neg_a[:, :], ACT.Copy, scale=-1.0))
            e_pc.wait(e, 6 * b + 5)
            e_p6.wait(e, b + 1)
            e_pc.mark(e.activation(alpha, dth, ACT.Exp, scale=neg_a[:, 0:1]))
            e_p4.wait(e, b + 1)
            e_p3.mark(e.activation(hrow_hi[:, :], hrow, ACT.Copy))
            e_p5.wait(e, b + 1)
            src = W[3][CL:P, :].rearrange("p (k a q) -> p k q a", k=NC, a=2)
            e_p3.mark(e.activation(decay_t[CL:P, :, :, :], src, ACT.Copy))

        e_pd, e_pu, e_p6 = ev("e_pd"), ev("e_pu"), ev("e_p6")
        sp_e, sp_u, sp_l = sqt[:, 0:2, :], sqt[:, 2:4, :], xbc[1][:, 0:2, :]
        hm, tm = (lambda a: a[0:NH, 0, :]), (lambda a: a[:, 1, :])
        tok = lambda a, s: a[:, 1, (s - 1) * TT * NH:s * TT * NH].rearrange("p (t n) -> p t n", t=TT)
        steps_of = lambda s: W[1 + s][:, :].rearrange("p (t n) -> p t n", t=TT)[:, :, 0:NH]
        tail_of = lambda s: W[1 + s][:, :].rearrange("p (t n) -> p t n", t=TT)[:, :, NH:]

        def prep_dve(e, b):
            n = [0]
            STEPS = 10

            def step(ins):
                e_pd.mark(ins)
                n[0] += 1
                e_pd.wait(e, b * STEPS + n[0])

            starts = lambda a: a.rearrange("p (k c) -> p k c", k=NC)[:, :, 0:1]
            e.memset(st_in[:, :], 0.0)
            e.memset(ones, 1.0)
            e_pc.wait(e, 6 * b + 2)
            for part in (hm, tm):
                ins = e.tensor_scalar(part(sp_u), part(sp_e), 1.0, None, ALU.add)
            e_pu.mark(ins)
            e_pu.wait(e, b + 1)
            for part in (hm, tm):
                ins = e.scalar_tensor_tensor(part(sp_e), part(sp_u), 1.0, part(sp_e), ALU.subtract, ALU.subtract)
            step(ins)
            e_pc.wait(e, 6 * b + 3)
            for part in (hm, tm):
                ins = e.tensor_tensor(part(sp_l), part(sp_l), part(sp_e), ALU.subtract)
            step(ins)
            e_p6.mark(e.scalar_tensor_tensor(dth, W[0][0:NH, :], 0.0, sp_l[0:NH, 0, :], ALU.max, ALU.add))
            for s in range(2):
                ins = e.scalar_tensor_tensor(dtk[:, s], steps_of(s), 0.0, tok(sp_l, s + 1), ALU.max, ALU.add)
            step(ins)
            e_pc.wait(e, 6 * b + 6)
            step(e.tensor_copy(alpha0, alpha))
            step(e.memset(starts(alpha0), 0.0))
            step(e.tensor_tensor(alpha, alpha, alpha0, ALU.subtract))
            step(e.tensor_tensor_scan(dect, alpha0, alpha, 0.0, ALU.mult, ALU.add))
            e.tensor_copy(hrow[:, 0:SEQ], dth)
            e.tensor_copy(hrow[:, SEQ:2 * SEQ], alpha0)
            e.memset(hrow[:, 2 * SEQ:2 * SEQ + 1], 0.0)
            ends = dect.rearrange("p (k c) -> p k c", k=NC)[:, 0:NC - 1, CL - 1]
            e_p4.mark(e.tensor_copy(hrow[:, 2 * SEQ + 1:ROWW], ends))
            e_p3.wait(e, 3 * b + 1)
            e.tensor_tensor(gam, lamk[:, 0], dtk[:, 0], ALU.mult)
            step(e.tensor_scalar(oml, lamk[:, 1], -1.0, 1.0, ALU.mult, ALU.add))
            step(e.tensor_tensor(dlt, oml, dtk[:, 1], ALU.mult))
            step(e.tensor_tensor(coef, gam, dlt, ALU.add))
            assert n[0] == STEPS
            e_p2.wait(e, b + 1)
            wide = lambda a, t: a[:, t, :].unsqueeze(2).to_broadcast([P, NH, HP])
            for t in range(TT):
                src = bank[t][:, :].rearrange("p (n d) -> p n d", n=NH)
                e.tensor_tensor(x1[:, :, t, :], src, wide(coef, t), ALU.mult)
                ins = e.tensor_tensor(x2[:, :, t, :], src, wide(gam, t), ALU.mult)
            e_p3.wait(e, 3 * b + 2)
            e_p4b.mark(e.tensor_tensor(hrow_lo[:, :], hrow, hrow_hi[:, :].bitcast(F32), ALU.subtract))

        e_p4b = ev("e_p4b")

        def attn_load_sp(e, b):
            for dst, src in ((wx_sb, w_x), (wdtl_sb, w_dtl), (wdth_sb, w_dth),
                             (bias, bias_in), (norm_w, norm_w_in), (neg_a, a_log)):
                a_aw.mark(e.dma_start(dst[:], src))
            for s in range(2):
                a_th[s].mark(e.dma_start(th_raw[s][:, :], w_th[s]))
                a_wb[s].mark(e.dma_start(wb_raw[s][:, :], w_bc[s]))

        def prep_sp(e, b):
            for hl, src, evt in ((0, hrow_hi, (e_p3, 3 * b + 2)), (1, hrow_lo, (e_p4b, b + 1))):
                evt[0].hold(e, evt[1])
                src = src[:, :].bitcast(F32)
                for a in range(2):
                    r = slice(a * NP, (a + 1) * NP)
                    a_roww.mark(e.dma_start(row_dram[:, 2 * a + hl, 0:SEQ], src[r, 0:SEQ]))
                    a_roww.mark(e.dma_start(row_dram[:, 2 * a + hl, 2 * SEQ:ROWW], src[r, 2 * SEQ:ROWW]))
                    for kp in range(2):
                        dst = row_dram[:, 2 * kp + hl, SEQ + a * (SEQ // 2):SEQ + (a + 1) * (SEQ // 2)]
                        s4 = src[r, SEQ:2 * SEQ].rearrange("p (t k c) -> p t k c", t=TT, k=2)
                        a_roww.mark(e.dma_start(dst.rearrange("q (t c) -> q t c", t=TT), s4[:, :, kp, :]))
            a_roww.hold(e, 16 * (b + 1))
            for j in range(2):
                a_rows[j].mark(e.dma_start(rows[32 * j:32 * j + 4, :].bitcast(F32), row_dram[j]))

        def T_pe(e, m, j):
            e_tP.wait(e, m + 1)
            e_bt.wait(e, 2 * (m - 2))
            e_th.mark(split_matmul(e, W[2][:, :], [((pair_w(th_hi[j % 2], 0, k), pair_w(th_lo[j % 2], 0, k)), xpair[k])
                                                   for k in range(KD)], True, True))
            e_H.wait(e, m - 2)
            r = slice(32 * (j % 4), 32 * (j % 4) + 4)
            e_dtb.mark(e.matmul(W[3][:, :], row_sel[r, :], rows[r, 0:SEQ], start=True, stop=True))

        def T_dve1(e, m, j):
            e_ths.wait(e, m + 1)
            e_dtb.wait(e, m + 1)
            e_tu.mark(e.tensor_tensor(turns[:, :], ths[:, :], W[3][:, :], ALU.mult))
            e_tu.wait(e, m + 1)
            e_cum.mark(e.tensor_tensor_scan(cum[:, :], ones, turns[:, :], 0.0, ALU.mult, ALU.add))

        def T_dve2(e, m, j):
            e_rnd.wait(e, m + 1)
            e_cs.wait(e, m)
            e_cum.wait(e, m + 1)
            e_nfr.mark(e.scalar_tensor_tensor(nfr[:, :], rnd[:, :], MAGIC, cum[:, :], ALU.subtract, ALU.subtract))

        def T_act1(e, m, j):
            e_th.wait(e, m + 1)
            e_tu.wait(e, m)
            e_ths.mark(e.activation(ths[:, :], W[2][:, :], ACT.Copy, scale=float(1 / (2 * np.pi))))

        def T_act2(e, m, j):
            e_cum.wait(e, m + 1)
            e_nfr.wait(e, m)
            e_rnd.mark(e.activation(rnd[:, :], cum[:, :], ACT.Identity, bias=magic[:, 0:1]))

        def T_act3(e, m, j):
            e_nfr.wait(e, m + 1)
            e_t.wait(e, 2 * (m - 1))
            e_afr.mark(e.activation(afr[:, :], nfr[:, :], ACT.Abs))
            e.activation(sn[j % 2][:, :], nfr[:, :], ACT.Sin, scale=-TWO_PI)
            e_afr.wait(e, m + 1)
            e_cs.mark(e.activation(cs[j % 2][:, :], afr[:, :], ACT.Sin, scale=-TWO_PI, bias=half_pi[:, 0:1]))

        def A_pe(e, m, j, parts=range(4)):
            if parts[0] == 0:
                e_bP.wait(e, m + 1)
            for i in parts:
                e_X.wait(e, 4 * m + i - 1)
                e_pj.mark(split_matmul(e, XBANK[i % 2][:, :],
                                       [((pair_w(wb_hi[j % 2], i, k), pair_w(wb_lo[j % 2], i, k)), xpair[k])
                                        for k in range(KD)], True, True))

        def ss_pe(e, m, j):
            if j % 2 == 0:
                e_sr.wait(e, m // 2 if isinstance(m, int) else m >> 1)
            for ty in range(2):
                e_sqs.wait(e, 2 * m + ty + 1)
                c = (j % 2) * 2 + ty
                e_ssm.mark(e.matmul(SSB[0:8, :], constant("one_hot")[:, 8 * c:8 * c + 8], sqs[:, ty, :],
                                    start=c == 0, stop=c == 3, skip_group_check=True))

        def A_act(e, m, j, parts=range(4)):
            if parts[0] == 0:
                e_t.wait(e, 2 * (m - 3))
            for i in parts:
                e_pj.wait(e, 4 * m + i + 1)
                e.activation(xbc[j % 4][:, i, :], XBANK[i % 2][:, :], ACT.Copy)
                if i % 2 == 0:
                    e_sqs.wait(e, 2 * (m - 1) + i // 2 + 1)
                e_X.mark(e.activation(sqt[:, i, :], XBANK[i % 2][:, :], ACT.Square))

        def A_pool(e, m, types=range(2)):
            for ty in types:
                e_X.wait(e, 4 * m + 2 * ty + 2)
                e_ssm.wait(e, 2 * (m - 1) + ty + 1)
                e_sqs.mark(e.tensor_tensor(sqs[:, ty, :], sqt[:, 2 * ty, :], sqt[:, 2 * ty + 1, :], ALU.add))

        def split_act(e, s, m, evA, free, arrival, raw, hi, n):
            arrival[s].wait(e, n)
            free()
            evA.mark(e.activation(hi[s][:, :], raw[s][:, :], ACT.Copy))

        def sb_act(e, m, j, cnt):
            a_wb[j % 2].wait(e, cnt)
            e_pj.wait(e, 4 * (m - 1))
            e_bA.mark(e.activation(wb_hi[j % 2][:, :], wb_raw[j % 2][:, :], ACT.Copy))

        def sb_pool(e, m, j):
            e_bA.wait(e, m + 1)
            e_bP.mark(e.tensor_tensor(wb_lo[j % 2][:, :], wb_raw[j % 2][:, :], wb_hi[j % 2][:, :].bitcast(F32), ALU.subtract))

        def st_act(e, m, j, cnt):
            a_th[j % 2].wait(e, cnt)
            e_th.wait(e, m - 1)
            e_tA.mark(e.activation(th_hi[j % 2][:, :], th_raw[j % 2][:, :], ACT.Copy))

        def st_pool(e, m, j):
            e_tA.wait(e, m + 1)
            e_tP.mark(e.tensor_tensor(th_lo[j % 2][:, :], th_raw[j % 2][:, :], th_hi[j % 2][:, :].bitcast(F32), ALU.subtract))

        def R_act(e, gm):
            e_ssm.wait(e, 4 * (gm + 1))
            a_r1.wait(e, gm)
            e_sr.mark(e.activation(stdr[:, :], SSB[0:8, :], ACT.Sqrt, scale=1.0 / NS, bias=eps_nm[0:8, 0:1]))

        def R_dve(e, gm):
            a_r1.wait(e, gm + 1)
            a_r2.wait(e, 2 * gm)
            e_rc.mark(e.reciprocal(rc[:, :], rc_in[:, :]))
            e_rc.wait(e, 2 * gm + 1)
            e_rc.mark(e.tensor_copy(rc_hi[:, :], rc[:, :]))
            e_rc.wait(e, 2 * gm + 2)
            e_rl.mark(e.tensor_tensor(rc_lo[:, :], rc[:, :], rc_hi[:, :].bitcast(F32), ALU.subtract))

        e_rc = ev("e_rc")

        def R_sp(e, gm, par, cnt):
            e_sr.hold(e, gm + 1)
            e_rl.hold(e, gm)
            a_r1.mark(e.dma_start(rc_in[:, :], stdr[:, :].rearrange("r (c w) -> r c w", w=32)))
            e_rl.hold(e, gm + 1)
            for hl, src in ((0, rc_hi), (1, rc_lo)):
                dst = rr_dram[par][hl].rearrange("r (c w) -> (r c) w", w=32)
                a_r2.mark(e.dma_start(dst, src[:, :].bitcast(F32)))
            a_r2.hold(e, 2 * (gm + 1))
            e_rC.hold(e, 2 * (gm - 1))
            for a in range(2):
                src = rr_dram[par].rearrange("h (g a) t -> a h g t", a=2)[a]
                a_rr[par].mark(e.dma_start(rrow[32 * par + 2 * a:32 * par + 2 * a + 2, :, :].bitcast(F32), src))

        def F_pe(e, n, j, cnt):
            par = (j // 2) % 2
            if j % 2 == 0:
                a_rr[par].wait(e, 2 * cnt)
            e_M.wait(e, n - 1)
            r = slice(32 * par, 32 * par + 4)
            for ty, evt in ((0, e_rB), (1, e_rC)):
                evt.mark(e.matmul(W[ty][:, :], row_sel[r, :], rrow[r, (j % 2) * 2 + ty, :], start=True, stop=True))

        def F_pe2(e, n, j, with_T):
            e_ths.wait(e, n + 2 if with_T else n + 1)
            r = slice(32 * j, 32 * j + 4)
            e_aB.mark(e.matmul(W[2][:, :], row_sel[r, :], rows[r, SEQ:2 * SEQ], start=True, stop=True))

        def F_dve1(e, n, j):
            e_X.wait(e, 4 * (n + 1))
            for ty, src, dst in ((0, e_rB, e_xb), (1, e_rC, e_xcc)):
                src.wait(e, n + 1)
                for i in (2 * ty, 2 * ty + 1):
                    ins = e.scalar_tensor_tensor(xbc[j][:, i, :], xbc[j][:, i, :], norm_w[:, i:i + 1], W[ty][:, :], ALU.mult, ALU.mult)
                dst.mark(ins)

        def F_dve2(e, n, j):
            p2, dk = j % 2, dks[j % 2]
            e_aB.wait(e, n + 1)
            e_M.wait(e, n - 1)
            e_D.mark(e.tensor_tensor_scan(dk, constant("shift_mask"), W[2][:, :], 0.0, ALU.add, ALU.mult))
            e_D.wait(e, n + 1)
            e_xp.wait(e, n + 1)
            e_S.wait(e, n - 1)
            dend = dk.rearrange("p (c w) -> p c w", w=CL)[:, :, CL - 1:CL].to_broadcast([P, 2 * TT, PW])
            e_xw.mark(e.scalar_tensor_tensor(xwp[p2][:, :].rearrange("p (c w) -> p c w", w=PW), dend, constant("last_row"),
                                             x1p[j][:, :].rearrange("p (c w) -> p c w", w=PW), ALU.add, ALU.mult))

        def F_dve3(e, n, j, q, types):
            if types[0] == 0:
                e_xcc.wait(e, n + 1)
                e_cs.wait(e, n + 1)
                e_Y.wait(e, n - 1)
                e_R.wait(e, n)
            X, R, c, s = xbc[j], rot[j % 2], cs[j % 2], sn[j % 2]
            for ty in types:
                bias_of = lambda i: bias[:, bass.ds(q, 1) if not isinstance(q, int) else slice(q, q + 1), i:i + 1].rearrange("p a c -> p (a c)")
                for o, i, f in ((R[:, 2 * ty, :], 2 * ty, c), (tmp[:, 2 * ty, :], 2 * ty + 1, s),
                                (R[:, 2 * ty + 1, :], 2 * ty, s), (tmp[:, 2 * ty + 1, :], 2 * ty + 1, c)):
                    ins = e.scalar_tensor_tensor(o, X[:, i, :], bias_of(i), f[:, :], ALU.add, ALU.mult)
                e_t.mark(ins)

        def F_pool(e, n, j, types):
            R = rot[j % 2]
            for ty in types:
                e_t.wait(e, 2 * n + ty + 1)
                e.tensor_tensor(R[:, 2 * ty, :], R[:, 2 * ty, :], tmp[:, 2 * ty, :], ALU.subtract)
                ins = e.tensor_tensor(R[:, 2 * ty + 1, :], R[:, 2 * ty + 1, :], tmp[:, 2 * ty + 1, :], ALU.add)
            if ty == 1:
                e_R.mark(ins)

        def XP_pool(e, n, j, q):
            e_Y.wait(e, n - 3)
            mask = constant("chunk_mask").rearrange("p (c k d) -> p c k d", c=2 * TT, k=2)
            for dst, src in ((x1p, x1), (x2p, x2)):
                v = src[:, bass.ds(2 * q, 2) if not isinstance(q, int) else slice(2 * q, 2 * q + 2), :, :]
                v = v.rearrange("p a t d -> p (a t) d").unsqueeze(2).to_broadcast([P, 2 * TT, 2, HP])
                ins = e.tensor_tensor(dst[j % 4][:, :].rearrange("p (c k d) -> p c k d", c=2 * TT, k=2), v, mask, ALU.mult)
            e_xp.mark(ins)

        def K1_pe(e, p, j, with_F, with_T):
            R = rot[j % 2]
            e_R.wait(e, p + 1)
            e_tu.hold(e, p + 1 + with_F + with_T)
            for a in range(2):
                if a and with_F:
                    e_xb.hold(e, p + 2)
                dst, h = W[3 if a == 0 else 0], slice(CL * a, CL * a + CL)
                for k in range(NC):
                    o = dst[CL * (k % 2):CL * (k % 2) + CL, CL * (k // 2):CL * (k // 2) + CL]
                    for eo in range(2):
                        ins = e.matmul(o, R[h, eo, CL * k:CL * k + CL], R[h, 2 + eo, CL * k:CL * k + CL],
                                       start=eo == 0, stop=eo == 1)
            e_G.mark(ins)
            for eo in range(2):
                if with_F:
                    (e_xcc, e_D)[eo].wait(e, p + 2)
                for t in range(TT):
                    ins = e.transpose(W[1 + eo][:, t * P:(t + 1) * P], R[:, eo, t * P:(t + 1) * P], ident[:, :])
                e_bte.mark(ins)

        def K_act(e, p, j):
            for eo in range(2):
                e_bte.wait(e, 2 * p + eo + 1)
                e_S.wait(e, p)
                e_bt.mark(e.activation(btr[:, eo, :], W[1 + eo][:, :], ACT.Copy))

        def K_dve1(e, p, j):
            e_G.wait(e, p + 1)
            e_D.wait(e, p + 1)
            e_Y.wait(e, p)
            half, dk = slice(0, SEQ // 2), dks[j % 2]
            for a in range(2):
                g, c = W[3 if a == 0 else 0][:, half], slice(a * SEQ // 2, (a + 1) * SEQ // 2)
                e.tensor_tensor(m1[:, c], g, dk[:, c], ALU.mult)
                ins = e.tensor_tensor(m2[:, c], g, constant("diag_mask")[:, c], ALU.mult)
            e_M.mark(ins)

        def K2_pe(e, p, j):
            e_bt.wait(e, 2 * (p + 1))
            e_xw.wait(e, p + 1)
            e_M.wait(e, p + 1)
            xw = xwp[j % 2][:, :].rearrange("p (a t w) -> p a t w", a=2, t=TT)
            S = W[3]
            for eo in range(2):
                for t in range(TT):
                    nk = 2 if t < TT - 1 else 1
                    o = S[:, eo * 128:(eo + 1) * 128].rearrange("p (a d k) -> p a k d", a=2, d=HP)[:, :, 2 * t + 1:2 * t + 1 + nk, :]
                    i = xw[:, :, t, :].rearrange("p a (k d) -> p a k d", k=2)[:, :, 0:nk, :]
                    e.matmul(o, btr[:, eo, t * P:(t + 1) * P], i, start=True, stop=True)
            r = slice(32 * j, 32 * j + 4)
            ends = rows[r, 2 * SEQ:ROWW].unsqueeze(1).to_broadcast([4, 32, NC])
            e_S.mark(e.matmul(S[:, 256:512].rearrange("p (c k) -> p c k", k=NC), row_sel[r, :], ends, start=True, stop=True))

        def K_dve2(e, p, j):
            e_S.wait(e, p + 1)
            e_Y.wait(e, p)
            v = lambda a: a.rearrange("p (c k) -> p c k", k=NC)[:, :, 1:NC]
            e_sm.mark(e.tensor_tensor(v(st_in[:, :]), v(W[3][:, 0:256]),
                                      constant("head_mask").rearrange("p (c k) -> p c k", k=NC - 1), ALU.mult))
            e_sm.wait(e, p + 1)
            e_H.mark(e.tensor_tensor_scan(st[:, :], W[3][:, 256:512], st_in[:, :], 0.0, ALU.mult, ALU.add))

        def Y_pe(e, p, j, yev):
            if j == 0:
                e_yev.wait(e, yev)
            R, y, hist = rot[j % 2], YB[:, :].rearrange("p (k w) -> p k w", k=NC), st[:, :].rearrange("p (o w k) -> p o w k", o=2, k=NC)
            c16 = slice(PW * j, PW * j + PW)
            c4 = lambda a: a.rearrange("p (c k d) -> p c k d", k=2, d=HP)
            for a in range(2):
                for t in range(TT):
                    o = y[0:CL, 2 * t:2 * t + 2, PW * j + HP * a:PW * j + HP * a + HP]
                    for n, (m, x) in enumerate(((m1, x1p), (m2, x2p))):
                        e.matmul(o, m[:, (a * TT + t) * CL:(a * TT + t + 1) * CL], c4(x[j][:, :])[:, a * TT + t],
                                 start=n == 0, stop=n == 1)
            e_H.wait(e, p + 1)
            for k in range(NC):
                for eo in range(2):
                    ins = e.matmul(y[CL:P, k, c16], R[:, 2 + eo, CL * k:CL * k + CL], hist[:, eo, :, k], start=eo == 0, stop=eo == 1)
            e_Y.mark(ins)

        def Y_dve(e, p, q4, n):
            e_Y.wait(e, p + 1)
            if isinstance(q4, int):
                dec, cols = decay_t[CL:P, :, q4:q4 + UN, :], slice(q4 * PW, (q4 + UN) * PW)
            else:
                dec, cols = decay_t[CL:P, :, bass.ds(q4, UN), :], bass.ds(q4 * PW, UN * PW)
            dec = dec.rearrange("p k q a -> p k (q a)").unsqueeze(3).to_broadcast([CL, NC, 2 * UN, HP])
            e_ym.mark(e.tensor_tensor(y4(ytmp), y4(YB[CL:P, :]), dec, ALU.mult))
            e_ym.wait(e, n + 1)
            for h in range(2):
                of = lambda a: a.rearrange("p (t h w) -> p t h w", t=TT, h=2)[:, :, h, :]
                ins = e.tensor_tensor(ysb[h * CL:(h + 1) * CL, :, cols], of(ytmp), of(YB[0:CL, :]), ALU.add)
            e_yev.mark(ins)

        e_ym = ev("e_ym")

        def turn(eng, e, b, it, first, last):
            N, Q = b * NP + it * UN, it * UN
            NB = NP // UN
            for j in range(UN):
                n, q, p = N + j, Q + j, N + j - 1
                jp = (j - 1) % UN
                T = not (last and j == UN - 1)
                A = not last or j == 0
                SS = not last or j <= 1
                RG = j % 2 == 1 and not (last and j == 3)
                K = not (first and j == 0)
                gm = b * (NP // 2) + it * 2 + j // 2
                if eng == "pe":
                    if SS:
                        ss_pe(e, n + 2, j)
                    if T:
                        a_rows[(j + 1) % 4].wait(e, b * NB + it + 1 + (j == 3))
                        T_pe(e, n + 1, j + 1)
                    F_pe(e, n, j, b * NB + it + 1)
                    if A:
                        A_pe(e, n + 3, j + 3, [0])
                    F_pe2(e, n, j, T)
                    if A:
                        A_pe(e, n + 3, j + 3, [1])
                    if K:
                        K1_pe(e, p, jp, True, T)
                    if A:
                        A_pe(e, n + 3, j + 3, [2])
                    if K:
                        K2_pe(e, p, jp)
                    if A:
                        A_pe(e, n + 3, j + 3, [3])
                    if K:
                        Y_pe(e, p, jp, b * NB + it)
                elif eng == "act":
                    if T:
                        T_act1(e, n + 1, j + 1)
                    if RG:
                        R_act(e, gm + 1)
                    if A:
                        A_act(e, n + 3, j + 3, [0])
                    if T:
                        T_act2(e, n + 1, j + 1)
                    if A:
                        A_act(e, n + 3, j + 3, [1])
                    if not last:
                        sb_act(e, n + 4, j, b * (NP // 2) + it * 2 + 3 + j // 2)
                    if K:
                        K_act(e, p, jp)
                    if T:
                        T_act3(e, n + 1, j + 1)
                    if not (last and j >= 2):
                        st_act(e, n + 2, j, b * (NP // 2) + it * 2 + 2 + j // 2)
                    if A:
                        A_act(e, n + 3, j + 3, [2, 3])
                elif eng == "pool":
                    if A:
                        A_pool(e, n + 3, [0])
                    if T:
                        XP_pool(e, n + 1, j + 1, q + 1)
                    if not last:
                        sb_pool(e, n + 4, j)
                    if not (last and j >= 2):
                        st_pool(e, n + 2, j)
                    F_pool(e, n, j, [0])
                    if A:
                        A_pool(e, n + 3, [1])
                    F_pool(e, n, j, [1])
                elif eng == "dve":
                    if T:
                        T_dve1(e, n + 1, j + 1)
                    F_dve1(e, n, j)
                    F_dve2(e, n, j)
                    if T:
                        T_dve2(e, n + 1, j + 1)
                    if j == 1 and not first:
                        Y_dve(e, n - 2, q - 1 - UN, b * NB + it - 1)
                    if K:
                        K_dve1(e, p, jp)
                    F_dve3(e, n, j, q, [0])
                    if RG:
                        R_dve(e, gm + 1)
                    if K:
                        K_dve2(e, p, jp)
                    F_dve3(e, n, j, q, [1])
                elif eng == "sp":
                    if not (last and j >= 2):
                        e_S.hold(e, n - 1)
                        s = (j + 2) % 4
                        src = row_dram[q + 2] if isinstance(q, int) else row_dram[bass.ds(q + 2, 1)].rearrange("a r w -> (a r) w")
                        a_rows[s].mark(e.dma_start(rows[32 * s:32 * s + 4, :].bitcast(F32), src))
                    if not (last and j >= 1):
                        e_tP.hold(e, n + 2)
                        src = w_th[q + 3] if isinstance(q, int) else w_th[bass.ds(q + 3, 1)].rearrange("a p w -> (a p) w")
                        a_th[(j + 1) % 2].mark(e.dma_start(th_raw[(j + 1) % 2][:, :], src))
                    if not last:
                        e_bP.hold(e, n + 3)
                        src = w_bc[q + 4] if isinstance(q, int) else w_bc[bass.ds(q + 4, 1)].rearrange("a p w -> (a p) w")
                        a_wb[j % 2].mark(e.dma_start(wb_raw[j % 2][:, :], src))
                    if RG:
                        R_sp(e, gm + 1, (j // 2 + 1) % 2, b * NB + it + 1)

        def pairs(eng, e, b):
            N, NB = b * NP, NP // UN
            if eng == "pe":
                a_rows[0].wait(e, b * NB + 1)
                T_pe(e, N, 0)
                for m in range(2):
                    A_pe(e, N + m, m)
                    ss_pe(e, N + m, m)
                A_pe(e, N + 2, 2)
            elif eng == "act":
                G = b * (NP // 2)
                st_act(e, N, 0, G + 1)
                sb_act(e, N, 0, G + 1)
                sb_act(e, N + 1, 1, G + 1)
                T_act1(e, N, 0)
                T_act2(e, N, 0)
                A_act(e, N, 0)
                sb_act(e, N + 2, 0, G + 2)
                A_act(e, N + 1, 1)
                R_act(e, G)
                T_act3(e, N, 0)
                sb_act(e, N + 3, 1, G + 2)
                st_act(e, N + 1, 1, G + 1)
                A_act(e, N + 2, 2)
            elif eng == "pool":
                st_pool(e, N, 0)
                sb_pool(e, N, 0)
                sb_pool(e, N + 1, 1)
                XP_pool(e, N, 0, 0)
                A_pool(e, N)
                sb_pool(e, N + 2, 0)
                A_pool(e, N + 1)
                sb_pool(e, N + 3, 1)
                st_pool(e, N + 1, 1)
                A_pool(e, N + 2)
            elif eng == "dve":
                T_dve1(e, N, 0)
                T_dve2(e, N, 0)
                R_dve(e, b * (NP // 2))
            elif eng == "sp":
                e_tP.hold(e, N + 1)
                a_th[0].mark(e.dma_start(th_raw[0][:, :], w_th[2]))
                for i in range(2):
                    e_bP.hold(e, N + 1 + i)
                    a_wb[i].mark(e.dma_start(wb_raw[i][:, :], w_bc[2 + i]))
                R_sp(e, b * (NP // 2), 0, b * NB + 1)
            turn(eng, e, b, 0, True, False)
            with e.Fori(1, NB - 1) as it:
                turn(eng, e, b, it, False, False)
            turn(eng, e, b, NB - 1, False, True)
            if eng == "sp":
                e_t.hold(e, 2 * (N + NP - 3))
                a_tw.mark(e.dma_start(wz_sb, w_z))
                a_tw.mark(e.dma_start(wo_sb, w_out))
            p, j = N + NP - 1, UN - 1
            if eng == "pe":
                K1_pe(e, p, j, False, False)
                K2_pe(e, p, j)
                Y_pe(e, p, j, 0)
            elif eng == "act":
                K_act(e, p, j)
            elif eng == "dve":
                K_dve1(e, p, j)
                K_dve2(e, p, j)
                Y_dve(e, p, NP - UN, b * NB + NB - 1)

        def tail_pe(e, b):
            a_tw.wait(e, 2 * (b + 1))
            for f in range(KI):
                for k in range(KD):
                    ins = e.matmul(bank[4 + f][:, :], wz_sb[:, k, f * P:(f + 1) * P], xn[:, k, 0:SEQ], start=k == 0, stop=k == KD - 1)
                e_z.mark(ins)
            e_yev.wait(e, (b + 1) * (NP // UN))
            for f in range(KI):
                for t in range(TT):
                    ins = e.transpose(bank[f][:, t * P:(t + 1) * P], ysb[:, t, f * P:(f + 1) * P], ident[:, :])
                e_yT.mark(ins)
            e_gt.wait(e, KI * (b + 1))
            for m in range(KD):
                for f in range(KI):
                    ins = e.matmul(bank[4 + m][:, :], wo_sb[:, f, m * P:(m + 1) * P], gated[:, f, :], start=f == 0, stop=f == KI - 1)
                e_o.mark(ins)

        def tail_act(e, b):
            e_Y.wait(e, (b + 1) * NP)
            for f in range(KI):
                e_z.wait(e, KI * b + f + 1)
                e_sz.mark(e.activation(silu_z[:, f, :], bank[4 + f][:, :], ACT.Silu))

        def tail_dve(e, b):
            for f in range(KI):
                e_sz.wait(e, KI * b + f + 1)
                e_yT.wait(e, KI * b + f + 1)
                e_gt.mark(e.tensor_tensor(gated[:, f, :], silu_z[:, f, :], bank[f][:, :], ALU.mult))
            for m in range(KD):
                e_o.wait(e, KD * b + m + 1)
                e.tensor_tensor(xT[:, m, :], xT[:, m, :], bank[4 + m][:, :], ALU.add)

        NCONST = 4
        block = ctx.enter_context(nc.Block())

        def give_ahead(e, n):
            for v in events[n::5]:
                v.give_ahead(e)

        @block.tensor
        def _(e):
            give_ahead(e, 0)
            a_const.wait(e, NCONST)
            e_init.wait(e, 3)
            with e.Fori(0, BATCH) as b:
                a_x.wait(e, b + 1)
                ln_pe(e, 3 * b)
                router_pe(e, 2 * b, 3 * b)
                e_xl.wait(e, KD * (3 * b + 1))
                ffn_pe(e, 2 * b)
                end_phase(e, PHASES * b)
                ln_pe(e, 3 * b + 1)
                e_xl.wait(e, KD * (3 * b + 2))
                prep_pe(e, b)
                e_p3.wait(e, 3 * b + 3)
                e_p4b.wait(e, b + 1)
                pairs("pe", e, b)
                tail_pe(e, b)
                end_phase(e, PHASES * b + 1)
                ln_pe(e, 3 * b + 2)
                router_pe(e, 2 * b + 1, 3 * b + 2)
                e_xl.wait(e, KD * (3 * b + 3))
                ffn_pe(e, 2 * b + 1)
                end_phase(e, PHASES * b + 2)

        @block.scalar
        def _(e):
            give_ahead(e, 1)
            a_const.wait(e, NCONST)
            e.activation(sel[:, :, :], sel_raw[:, :, :], ACT.Copy)
            e_init.mark(e.activation(row_sel[:, :], constant("row_sel"), ACT.Copy))
            e_init.wait(e, 3)
            with e.Fori(0, BATCH) as b:
                ln_act(e, 3 * b)
                router_act(e, 2 * b)
                ffn_act(e, 2 * b)
                end_phase(e, PHASES * b)
                ln_act(e, 3 * b + 1)
                prep_act(e, b)
                e_p4b.wait(e, b + 1)
                pairs("act", e, b)
                tail_act(e, b)
                end_phase(e, PHASES * b + 1)
                ln_act(e, 3 * b + 2)
                router_act(e, 2 * b + 1)
                ffn_act(e, 2 * b + 1)
                end_phase(e, PHASES * b + 2)

        @block.gpsimd
        def _(e):
            give_ahead(e, 2)
            e.memset(zero_w[:, :].bitcast(F32), 0.0)
            e.memset(mean_w[:, :], 1.0 / D)
            e.memset(xn[:, :, SEQ:], 0.0)
            e.memset(eps_nm[:, :], EPS_NORM)
            e.memset(magic[:, :], MAGIC)
            e.memset(half_pi[:, :], float(np.pi / 2))
            e_init.mark(e.memset(eps_ln[:, :], EPS_LN))
            with e.Fori(0, BATCH) as b:
                ffn_pool(e, 2 * b)
                end_phase(e, PHASES * b)
                e_p3.wait(e, 3 * b + 3)
                e_p4b.wait(e, b + 1)
                pairs("pool", e, b)
                end_phase(e, PHASES * b + 1)
                ffn_pool(e, 2 * b + 1)
                end_phase(e, PHASES * b + 2)

        @block.vector
        def _(e):
            give_ahead(e, 3)
            e_init.mark(e.memset(top[:, :, :], 0.0))
            with e.Fori(0, BATCH) as b:
                ln_dve(e, 3 * b)
                ffn_start_dve(e, 2 * b)
                router_dve(e, 2 * b)
                ffn_dve(e, 2 * b)
                end_phase(e, PHASES * b)
                ln_dve(e, 3 * b + 1)
                a_aw.wait(e, 6 * (b + 1))
                prep_dve(e, b)
                pairs("dve", e, b)
                tail_dve(e, b)
                end_phase(e, PHASES * b + 1)
                ln_dve(e, 3 * b + 2)
                ffn_start_dve(e, 2 * b + 1)
                router_dve(e, 2 * b + 1)
                ffn_dve(e, 2 * b + 1)
                end_phase(e, PHASES * b + 2)

        @block.sync
        def _(e):
            give_ahead(e, 4)
            a_const.mark(e.dma_start(sel_raw[:, :, :], sel_ffn_in))
            a_const.mark(e.dma_start(ident[:, :], ident_in))
            a_const.mark(e.dma_start(wr_sb[:, :, :], w_router))
            a_const.mark(e.dma_start(cst[:, :], cst_in))
            e_init.wait(e, 3)
            with e.Fori(0, BATCH) as b:
                a_out.wait(e, b)
                a_x.mark(e.dma_start(xT[:, :, :], x_in[bass.ds(b, 1), :, :, :].rearrange("a p k t -> (a p) k t")))
                ffn_load_sp(e, 2 * b)
                router_sp(e, 2 * b)
                ffn_sp(e, 2 * b)
                end_phase(e, PHASES * b)
                attn_load_sp(e, b)
                prep_sp(e, b)
                pairs("sp", e, b)
                end_phase(e, PHASES * b + 1)
                ffn_load_sp(e, 2 * b + 1)
                router_sp(e, 2 * b + 1)
                ffn_sp(e, 2 * b + 1)
                end_phase(e, PHASES * b + 2)
                a_out.mark(e.dma_start(out[bass.ds(b, 1), :, :, :].rearrange("a p k t -> (a p) k t"), xT[:, :, :]))
            a_out.wait(e, BATCH)


def feature_major(w):
    return np.ascontiguousarray(w.reshape(-1, P, w.shape[1]).transpose(1, 0, 2))


def arrays_of(a):
    x = a["L0_attn_x"].transpose(0, 2, 1).reshape(BATCH, KD, P, SEQ).transpose(0, 2, 1, 3)
    groups = []
    for n in range(NG):
        s = slice(n * GE, (n + 1) * GE)
        g, u = (a[w][s].transpose(1, 0, 2).reshape(KD, P, GT * P).transpose(1, 0, 2).reshape(P, -1)
                for w in ("L0_ffn_Wg", "L0_ffn_Wu"))
        d = a["L0_ffn_Wd"][s].reshape(GT, P, D).transpose(1, 0, 2).reshape(P, -1)
        groups.append(np.concatenate([g, u, d], axis=1))
    def tiles(w, eo):
        w = w.reshape(NP, 2, -1, eo, D).transpose(0, 3, 4, 1, 2).reshape(NP, eo, KD, P, P)
        return w.transpose(0, 3, 1, 2, 4)
    bc = np.concatenate([tiles(a["L0_attn_WB"], 2), tiles(a["L0_attn_WC"], 2)], axis=2).reshape(NP, P, BCW)
    th = tiles(a["L0_attn_Wth"], 1).reshape(NP, P, THW)
    per_row = lambda v: v.reshape(NP, 2, NS // 2, 2).transpose(1, 2, 0, 3).reshape(P, NP, 2)
    bias = np.concatenate([per_row(a["L0_attn_B_bias"]), per_row(a["L0_attn_C_bias"])], axis=2)
    nw = np.concatenate([np.tile(a[w].reshape(NS // 2, 2), (2, 1)) for w in ("L0_attn_Bn_w", "L0_attn_Cn_w")], axis=1)
    by_parity = lambda v: v.reshape(NP, 2, -1).transpose(1, 0, 2).reshape(NH, -1)
    sel = np.zeros((2 * GE, GT, P), np.float32)
    for i in range(GT):
        for p in range(P):
            n = (i * P + p) // NI
            sel[2 * n:2 * n + 2, i, p] = 1.0
    p = np.arange(P)
    t = np.arange(SEQ) % CL
    shift = (t[None] == p[:, None] % CL + 1).astype(np.float32)
    diag = (t[None] == p[:, None] % CL).astype(np.float32)
    last = (p % CL == CL - 1).astype(np.float32)[:, None]
    head = (p[:, None, None, None, None] // CL == np.arange(2)[None, None, :, None, None]) * np.ones((P, 2, 2, HP, NC - 1))
    chunk = (p[:, None, None, None] // CL == np.arange(2)[None, None, :, None]) * np.ones((P, 2 * TT, 2, HP))
    row_sel = ((p[:, None] % 32) // 2 == p[None] // CL) * np.ones((P, P))
    one_hot = np.zeros((P, 4, 8))
    for c in range(4):
        one_hot[p, c, 2 * c + p // CL] = 1.0
    cst = np.concatenate([v.reshape(P, -1) for v in (shift, diag, last, head, chunk, row_sel, one_hot)], axis=1)
    arrays = {
        "x_in": x,
        "w_ffn": np.stack(groups),
        "w_router": feature_major(a["L0_ffn_Wr"].T),
        "w_bc": bc,
        "w_th": th,
        "w_x": feature_major(a["L0_attn_Wx"].T),
        "w_z": feature_major(a["L0_attn_Wz"].T),
        "w_dtl": feature_major(np.concatenate([a["L0_attn_Wdt"], a["L0_attn_Wlam"]]).T),
        "w_dth": feature_major(by_parity(a["L0_attn_Wdt"]).T),
        "a_log": by_parity(a["L0_attn_A_log"]),
        "w_out": feature_major(a["L0_attn_Wout"].T),
        "bias_in": bias,
        "norm_w_in": nw,
        "sel_ffn_in": sel,
        "ident_in": np.eye(P, dtype=np.float32),
        "cst_in": cst.astype(np.float32),
    }
    return {k: np.ascontiguousarray(v) for k, v in arrays.items()}


def kernel(**inputs):
    import concourse.bacc as bacc
    from concourse.bass_utils import run_bass_kernel_spmd

    arrays = arrays_of({k: np.asarray(v) for k, v in inputs.items()})
    nc = bacc.Bacc("TRN2", target_bir_lowering=False, num_devices=1)
    args = [nc.dram_tensor(n, v.shape, mybir.dt.from_np(v.dtype), kind="ExternalInput").ap() for n, v in arrays.items()]
    out = nc.dram_tensor("out_x", (BATCH, P, KD, SEQ), F32, kind="ExternalOutput").ap()
    build(nc, *args, out)
    r = run_bass_kernel_spmd(nc, [arrays], core_ids=[0])
    got = r.results[0]["out_x"]
    return np.ascontiguousarray(got.transpose(0, 3, 2, 1).reshape(BATCH, SEQ, D))
```

```python
from contextlib import ExitStack

import numpy as np
import concourse.bass as bass
from concourse import mybir

F32 = mybir.dt.float32
F32R = mybir.dt.float32r
ALU = mybir.AluOpType
ACT = mybir.ActivationFunctionType
AX_X = mybir.AxisListType.X

P = 128
BATCH, SEQ, D = 4, 512, 256
KD = D // P
NE, NI, TOPK = 64, 96, 8
GE = 4
GT = GE * NI // P
NG = NE // GE
GW = 3 * GT * D
PIECE = GW // GT
NT = NG * GT
TT = SEQ // P
LAG = 2
NH, HP, NS = 64, 8, 128
NP = NH // 2
CL = 64
NC = SEQ // CL
DIN = NH * HP
KI = DIN // P
UN = 4
PW = 2 * HP
ROWW = 2 * SEQ + NC
BCW, THW = 4 * KD * P, KD * P
EPS_LN, EPS_NORM = 1e-5, 1e-6
MAGIC = 12582912.0
TWO_PI = 6.283185


class Event:
    unit = 1

    def __init__(self, all_events, ctx, nc, name, ahead=0):
        self.sem, self.ahead = ctx.enter_context(nc.semaphore(name)), 1 + ahead
        all_events.append(self)

    def give_ahead(self, eng):
        eng.sem_inc(self.sem, self.ahead)

    def wait(self, eng, count):
        if isinstance(count, int) and count + self.ahead <= 1:
            return
        eng.wait_ge(self.sem, count * self.unit + self.ahead)

    def hold(self, eng, count):
        self.wait(eng, count)
        eng.nop(nofuse=True)

    def mark(self, ins):
        ins.then_inc(self.sem, self.unit)


class Arrival(Event):
    unit = 16


def split_matmul(e, dst, pairs, start, stop):
    n, c, ins = len(pairs) * 3, 0, None
    for (ah, al), (mh, ml) in pairs:
        for a, m in ((ah, mh), (al, mh), (ah, ml)):
            ins = e.matmul(dst, a, m, start=start and c == 0, stop=stop and c == n - 1,
                           skip_group_check=not (start and stop))
            c += 1
    return ins


def build(nc, x_in, w_ffn, w_router, w_bc, w_th, w_x, w_z, w_dtl, w_dth, a_log, w_out, bias_in, norm_w_in,
          sel_ffn_in, ident_in, cst_in, out):
    with ExitStack() as ctx:
        events = []

        def ev(name, ahead=0):
            return Event(events, ctx, nc, name, ahead)

        def arr(name):
            return Arrival(events, ctx, nc, name)

        def sb_in(c):
            return lambda name, shape, dt=F32: c.enter_context(nc.sbuf_tensor(name, shape, dt))

        bank = [ctx.enter_context(nc.psum_tensor(f"bank{i}", [P, SEQ], F32)) for i in range(8)]

        sb = sb_in(ctx)
        xT = sb("xT", [P, KD, SEQ])
        xn = sb("xn", [P, KD, SEQ + 2])
        xh, xl = sb("xh", [P, KD, SEQ], F32R), sb("xl", [P, KD, SEQ], F32R)
        xc, sq = sb("xc", [P, KD, SEQ]), sb("sq", [P, KD, SEQ])
        std, rstd = sb("std", [P, TT]), sb("rstd", [P, TT])
        eps_ln, eps_nm, magic, half_pi = (sb(n, [P, 1]) for n in ("eps_ln", "eps_nm", "magic", "half_pi"))
        mean_w = sb("mean_w", [P, P])
        zero_w = sb("zero_w", [P, P], F32R)
        ident = sb("ident", [P, P])
        wr_sb = sb("wr_sb", [P, KD, NE])
        CST = {}
        at_col = 0
        for n, w in (("shift_mask", SEQ), ("diag_mask", SEQ), ("last_row", 1), ("head_mask", 32 * (NC - 1)),
                     ("chunk_mask", P), ("row_sel", P), ("one_hot", P + 6)):
            CST[n] = (at_col, w)
            at_col += w
        cst = sb("cst", [P, at_col])
        constant = lambda n: cst[:, CST[n][0]:CST[n][0] + CST[n][1]]
        row_sel = sb("row_sel", [P, P], F32R)
        one_hot = sb("one_hot", [P, P + 6], F32R)
        sel = sb("sel", [2 * GE, GT, P], F32R)

        with ExitStack() as ffn_ctx:
            sb = sb_in(ffn_ctx)
            sel_raw = sb("sel_raw", [2 * GE, GT, P])
            lmax, wsum, wrec = sb("lmax", [P, TT]), sb("wsum", [P, TT]), sb("wrec", [P, TT])
            lg, ex, rest, wsel, comb = (sb(n, [P, TT, NE]) for n in ("lg", "ex", "rest", "wsel", "comb"))
            top = sb("top", [P, TT, TOPK])
            comb_h, comb_l = sb("comb_h", [NE, SEQ], F32R), sb("comb_l", [NE, SEQ], F32R)
            comb_rows = [sb(f"comb_rows{i}", [2 * GE, SEQ], F32R) for i in range(2)]
            w_raw = [sb(f"w_raw{i}", [P, GW]) for i in range(2)]
            w_hi = [sb(f"w_hi{i}", [P, GW], F32R) for i in range(2)]
            w_lo = [sb(f"w_lo{i}", [P, GW], F32R) for i in range(2)]
            sg, h1, hf = ([sb(f"{n}{i}", [P, SEQ]) for i in range(2)] for n in ("sg", "h1_", "hf"))
            h_hi = [sb(f"h_hi{i}", [P, SEQ], F32R) for i in range(3)]
            h_lo = [sb(f"h_lo{i}", [P, SEQ], F32R) for i in range(3)]
            x_first = sb("x_first", [P, KD, SEQ])
            x_last = sb("x_last", [P, KD, SEQ])
        comb_dram = nc.dram_tensor("comb_dram", [NE, 2, SEQ], F32R, kind="Internal").ap().bitcast(F32)

        attn_ctx = ctx
        sb = sb_in(attn_ctx)
        xbc = [sb(f"xbc{i}", [P, 4, SEQ]) for i in range(4)]
        rot = [sb(f"rot{i}", [P, 4, SEQ]) for i in range(2)]
        tmp = sb("tmp", [P, 4, SEQ])
        sn, cs = ([sb(f"{n}{i}", [P, SEQ]) for i in range(2)] for n in ("sn", "cs"))
        ths, turns, nfr = (sb(n, [P, SEQ]) for n in ("ths", "turns", "nfr"))
        sqt = sb("sqt", [P, 2, SEQ])
        sqs = sb("sqs", [P, 2, SEQ])
        sq_hi, sq_lo = sb("sq_hi", [P, 2, SEQ], F32R), sb("sq_lo", [P, 2, SEQ], F32R)
        btr = sb("btr", [P, 2, SEQ])
        x1, x2 = sb("x1", [P, NH, TT, HP]), sb("x2", [P, NH, TT, HP])
        x1p = [sb(f"x1p{i}", [P, P]) for i in range(4)]
        x2p = [sb(f"x2p{i}", [P, P]) for i in range(4)]
        xwp = [sb(f"xwp{i}", [P, P]) for i in range(2)]
        st_in = sb("st_in", [P, 32 * NC])
        st = sb("st", [P, 32 * NC])
        ysb = sb("ysb", [P, TT, DIN])
        decay_t = sb("decay_t", [P, NC, NP, 2])
        rows = sb("rows", [P, ROWW], F32R)
        rrow = sb("rrow", [P, 4, SEQ], F32R)
        wb_raw, th_raw = ([sb(f"{n}{i}", [P, w]) for i in range(2)] for n, w in (("wb_raw", BCW), ("th_raw", THW)))
        wb_hi, wb_lo = ([sb(f"{n}{i}", [P, BCW], F32R) for i in range(2)] for n in ("wb_hi", "wb_lo"))
        th_hi, th_lo = ([sb(f"{n}{i}", [P, THW], F32R) for i in range(2)] for n in ("th_hi", "th_lo"))
        wx_sb = xbc[3][:, 0:KD, :]
        wz_sb = xbc[0][:, 0:KD, :]
        wo_sb = xbc[0][:, KD:, :].rearrange("p a b -> p (a b)").rearrange("p (f m) -> p f m", f=KI)
        wdtl_sb, wdth_sb = sb("wdtl_sb", [P, KD, 2 * NH]), sb("wdth_sb", [P, KD, NH])
        neg_a = sb("neg_a", [NH, 1])
        bias = sb("bias", [P, NP, 4])
        norm_w = sb("norm_w", [P, 4])
        stdr = sb("stdr", [8, SEQ])
        rc_in, rc, rc_hi, rc_lo = sb("rc_in", [P, 32]), sb("rc", [P, 32]), sb("rc_hi", [P, 32], F32R), sb("rc_lo", [P, 32], F32R)
        dks = [xc[:, i, :] for i in range(2)]
        m1, m2 = sq[:, 0, :], sq[:, 1, :]
        one, cum = sb("one", [P, 1]), sb("cum", [P, SEQ])
        ones = one[:, :].to_broadcast([P, SEQ])
        ytmp = cum[0:CL, :]
        afr, rnd = ths, turns
        dth = rot[0][0:NH, 0, :]
        alpha = rot[0][0:NH, 1, :]
        alpha0 = rot[0][0:NH, 2, :]
        dect = rot[0][0:NH, 3, :]
        hrow = rot[1][0:NH, 0:3, :].rearrange("p a b -> p (a b)")[:, 0:ROWW]
        dtk = tmp[:, 0, :].rearrange("p (s t n) -> p s t n", s=2, t=TT)
        lamk = tmp[:, 1, :].rearrange("p (s t n) -> p s t n", s=2, t=TT)
        gam = tmp[:, 2, 0:TT * NH].rearrange("p (t n) -> p t n", t=TT)
        oml = tmp[:, 2, TT * NH:].rearrange("p (t n) -> p t n", t=TT)
        dlt = tmp[:, 3, 0:TT * NH].rearrange("p (t n) -> p t n", t=TT)
        coef = tmp[:, 3, TT * NH:].rearrange("p (t n) -> p t n", t=TT)
        hrow_hi = rows[0:NH, :]
        hrow_lo = rrow[0:NH, :, :].rearrange("p a b -> p (a b)")[:, 0:ROWW]
        silu_z = rot[0]
        gated = rot[1]
        row_dram = nc.dram_tensor("row_dram", [NP, 4, ROWW], F32R, kind="Internal").ap().bitcast(F32)
        rr_dram = [nc.dram_tensor(f"rr_dram{i}", [2, 8, SEQ], F32R, kind="Internal").ap().bitcast(F32) for i in range(2)]

        a_const, a_x, a_out = arr("a_const"), arr("a_x"), arr("a_out")
        a_wraw = [arr(f"a_wraw{i}") for i in range(2)]
        a_combw, a_comb = arr("a_combw"), [arr(f"a_comb{i}") for i in range(2)]
        e_init, e_phase = ev("e_init"), ev("e_phase")
        e_mean, e_xc, e_sq, e_var, e_std, e_rstd, e_xn, e_xh, e_xl = (
            ev(n) for n in "e_mean e_xc e_sq e_var e_std e_rstd e_xn e_xh e_xl".split())
        e_lg, e_sub, e_ex, e_chain, e_comb, e_ct, e_ch, e_cl = (
            ev(n) for n in "e_lg e_sub e_ex e_chain e_comb e_ct e_ch e_cl".split())
        e_hz = ev("e_hz")
        e_g, e_u, e_cb, e_down = ev("e_g"), ev("e_u"), ev("e_cb", 2 * GT), ev("e_down")
        e_silu, e_h1, e_h = ev("e_silu", 2), ev("e_h1", 2), ev("e_h", 2)
        e_hh, e_hl = ev("e_hh", LAG), ev("e_hl", LAG)
        e_wA, e_wP = ev("e_wA"), ev("e_wP")

        PHASES = 3

        def end_phase(e, n):
            e_phase.mark(e.drain())
            e_phase.hold(e, 5 * (n + 1))

        def ln_pe(e, r, x=xT):
            for k in range(KD):
                ins = e.matmul(bank[2][:, :], mean_w[:, :], x[:, k, :], start=k == 0, stop=k == KD - 1)
            e_mean.mark(ins)
            e_sq.wait(e, r + 1)
            for t in range(TT):
                for k in range(KD):
                    ins = e.matmul(bank[3][:, t:t + 1], sq[:, k, t * P:(t + 1) * P], mean_w[:, 0:1], start=k == 0, stop=k == KD - 1)
            e_var.mark(ins)
            e_rstd.wait(e, r + 1)
            for t in range(TT):
                ins = e.matmul(bank[2][:, t * P:(t + 1) * P], rstd[:, t:t + 1].to_broadcast([P, P]), ident[:, :], start=True, stop=True)
            e_rb.mark(ins)

        e_rb = ev("e_rb")

        def ln_dve(e, r, between, x=xT):
            e_mean.wait(e, r + 1)
            for k in range(KD):
                ins = e.tensor_tensor(xc[:, k, :], x[:, k, :], bank[2][:, :], ALU.subtract)
            e_xc.mark(ins)
            between()
            e_std.wait(e, r + 1)
            e_rstd.mark(e.reciprocal(rstd[:, :], std[:, :]))
            e_rb.wait(e, r + 1)
            for k in range(KD):
                e_xn.mark(e.tensor_tensor(xn[:, k, 0:SEQ], xc[:, k, :], bank[2][:, :], ALU.mult))
            for k in range(KD):
                e_xh.wait(e, KD * r + k + 1)
                e_xl.mark(e.tensor_tensor(xl[:, k, :], xn[:, k, 0:SEQ], xh[:, k, :].bitcast(F32), ALU.subtract))

        def ln_act(e, r, between):
            e_xc.wait(e, r + 1)
            e_sq.mark(e.activation(sq[:, :, :], xc[:, :, :], ACT.Square))
            e_var.wait(e, r + 1)
            e_std.mark(e.activation(std[:, :], bank[3][:, 0:TT], ACT.Sqrt, bias=eps_ln[:, 0:1]))
            between()
            for k in range(KD):
                e_xn.wait(e, KD * r + k + 1)
                e_xh.mark(e.activation(xh[:, k, :], xn[:, k, 0:SEQ], ACT.Copy))

        lgb, ctb = bank[6], bank[7]

        def router_pe(e, f, r):
            e_xn.wait(e, KD * (r + 1))
            for t in range(TT):
                for k in range(KD):
                    ins = e.matmul(lgb[:, t * NE:(t + 1) * NE], xn[:, k, t * P:(t + 1) * P], wr_sb[:, k, :],
                                   start=k == 0, stop=k == KD - 1)
            e_lg.mark(ins)

        def comb_pe(e, f):
            e_comb.hold(e, f + 1)
            for t in range(TT):
                ins = e.transpose(ctb[0:NE, t * P:(t + 1) * P], comb[:, t, :], ident[:, :])
            e_ct.mark(ins)

        CHAIN = 9

        def router_dve(e, f):
            n = [0]

            def step(ins):
                e_chain.mark(ins)
                n[0] += 1
                e_chain.hold(e, f * CHAIN + n[0])

            logits = lgb[:, 0:TT * NE].rearrange("p (t n) -> p t n", t=TT)
            wide = lambda a: a[:, :].unsqueeze(2).to_broadcast([P, TT, NE])
            e_lg.wait(e, f + 1)
            step(e.tensor_reduce(lmax[:, :], logits, AX_X, ALU.max))
            e_sub.mark(e.tensor_tensor(lg[:, :, :], logits, wide(lmax), ALU.subtract))
            e_ex.hold(e, f + 1)
            for t in range(TT):
                ins = e.max(top[:, t, :], ex[:, t, :])
            step(ins)
            for t in range(TT):
                step(e.match_replace(rest[:, t, :], top[:, t, :], ex[:, t, :], -1.0))
            step(e.scalar_tensor_tensor(wsel[:, :, :], rest[:, :, :], 0.0, ex[:, :, :], ALU.is_lt, ALU.mult))
            step(e.tensor_reduce(wsum[:, :], wsel[:, :, :], AX_X, ALU.add))
            step(e.reciprocal(wrec[:, :], wsum[:, :]))
            assert n[0] == CHAIN
            e_comb.mark(e.tensor_tensor(comb[:, :, :], wsel[:, :, :], wide(wrec), ALU.mult))

        def comb_dve(e, f):
            e_ch.wait(e, f + 1)
            e_cl.mark(e.tensor_tensor(comb_l[:, :], ctb[0:NE, :], comb_h[:, :].bitcast(F32), ALU.subtract))

        def router_act(e, f):
            e_sub.wait(e, f + 1)
            e_ex.mark(e.activation(ex[:, :, :], lg[:, :, :], ACT.Exp))

        def comb_act(e, f):
            e_ct.wait(e, f + 1)
            e_ch.mark(e.activation(comb_h[:, :], ctb[0:NE, :], ACT.Copy))

        def router_sp(e, f):
            e_ch.hold(e, f + 1)
            a_combw.mark(e.dma_start(comb_dram[:, 0, :], comb_h[:, :].bitcast(F32)))
            e_cl.hold(e, f + 1)
            a_combw.mark(e.dma_start(comb_dram[:, 1, :], comb_l[:, :].bitcast(F32)))
            a_combw.hold(e, 2 * (f + 1))

        DOWNS = NT + LAG
        SPLITS = NG * GT

        wg = lambda w, k, i: w[:, k * GT * P + i * P:k * GT * P + (i + 1) * P]
        wu = lambda w, k, i: wg(w, KD + k, i)
        wd = lambda w, i, m: w[:, 2 * KD * GT * P + i * D + m * P:2 * KD * GT * P + i * D + (m + 1) * P]
        piece = lambda w, i: w[:, i * PIECE:(i + 1) * PIECE]

        def each_group(e, f, body):
            for g in range(2):
                body(g, f * NG + g, 0, True, False)
            with e.Fori(1, NG // 2 - 1) as it:
                for g in range(2):
                    body(g, f * NG + it * 2 + g, it, False, False)
            for g in range(2):
                body(g, f * NG + NG - 2 + g, NG // 2 - 1, False, True)

        def ffn_pe(e, f):
            e_hz.wait(e, f + 1)
            for m in range(KD):
                e.matmul(bank[m][:, :], zero_w[:, :], xh[:, 0, :], start=True, stop=False, skip_group_check=True)

            def down(i):
                for m in range(KD):
                    ins = split_matmul(e, bank[m][:, :],
                                       [((wd(w_hi[i // GT], i % GT, m), wd(w_lo[i // GT], i % GT, m)),
                                         (h_hi[i % 3][:, :], h_lo[i % 3][:, :]))], False, False)
                e_down.mark(ins)

            def group(g, G, it, first, last):
                def gate_up(i):
                    T = G * GT + i
                    s = (g * GT + i) % 2
                    e_silu.wait(e, T + 1 - 2)
                    e_g.mark(split_matmul(e, bank[2 + s][:, :],
                                          [((wg(w_hi[g], k, i), wg(w_lo[g], k, i)), (xh[:, k, :], xl[:, k, :]))
                                           for k in range(KD)], True, True))
                    e_h1.wait(e, T + 1 - 2)
                    e_u.mark(split_matmul(e, bank[4 + s][:, :],
                                          [((wu(w_hi[g], k, i), wu(w_lo[g], k, i)), (xh[:, k, :], xl[:, k, :]))
                                           for k in range(KD)], True, True))

                for i in range(GT):
                    T = G * GT + i
                    s = (g * GT + i) % 2
                    if i == 0:
                        e_wP.wait(e, GT * G + 2)
                    if i == LAG:
                        e_wP.wait(e, GT * G + 3)
                    if first and g == 0:
                        if i == 0:
                            gate_up(0)
                            gate_up(1)
                            comb_pe(e, f)
                            for n in range(LAG):
                                down(2 * GT - LAG + n)
                        if i == 2:
                            gate_up(2)
                    else:
                        gate_up(i)
                    if i == 0:
                        a_comb[g].wait(e, f * (NG // 2) + it + 1)
                    e_h.wait(e, T + 1 - 2)
                    e_cb.mark(e.matmul(bank[6 + s][:, :], sel[:, i, :], comb_rows[g][:, :], start=True, stop=True))
                    if not (first and g == 0 and i < LAG):
                        e_hl.wait(e, T + 1 - LAG)
                        down((g * GT + i - LAG) % (2 * GT))

            each_group(e, f, group)
            for j in range(LAG):
                e_hl.wait(e, (f + 1) * NT - LAG + j + 1)
                down(2 * GT - LAG + j)

        def ffn_start_act(e, f):
            a_wraw[0].wait(e, f * (NG // 2) + 1)
            for i in range(GT):
                e_wA.mark(e.activation(piece(w_hi[0], i), piece(w_raw[0], i), ACT.Copy))

        def ffn_act(e, f):
            def silu(T, s):
                e_g.wait(e, T + 1)
                e_h1.wait(e, T + 1 - 2)
                e_silu.mark(e.activation(sg[s][:, :], bank[2 + s][:, :], ACT.Silu))

            def group(g, G, it, first, last):
                for i in range(GT):
                    T = G * GT + i
                    s = (g * GT + i) % 2
                    tau = (it * 2 + g) * GT + i
                    if first and g == 0 and i < 2:
                        if i == 0:
                            silu(T, 0)
                            silu(T + 1, 1)
                            comb_act(e, f)
                    else:
                        silu(T, s)
                    e_h.wait(e, T + 1)
                    e_down.wait(e, f * DOWNS + tau)
                    e_hh.mark(e.activation(h_hi[(g * GT + i) % 3][:, :], hf[s][:, :], ACT.Copy))
                    if last and g:
                        continue
                    nx = 1 - g
                    a_wraw[nx].wait(e, f * (NG // 2) + it + 1 + g)
                    if i < 2:
                        e_u.wait(e, GT * G)
                    else:
                        e_down.wait(e, f * DOWNS + (it * 2 + g) * GT + LAG)
                    e_wA.mark(e.activation(piece(w_hi[nx], i), piece(w_raw[nx], i), ACT.Copy))

            each_group(e, f, group)

        def ffn_pool(e, f):
            def lo(s, i):
                e_wP.mark(e.tensor_tensor(piece(w_lo[s], i), piece(w_raw[s], i), piece(w_hi[s], i).bitcast(F32), ALU.subtract))

            for i in range(GT):
                e_wA.wait(e, f * SPLITS + i + 1)
                lo(0, i)

            def group(g, G, it, first, last):
                if not (last and g):
                    for i in range(GT):
                        e_wA.wait(e, GT * (G + 1) + i + 1)
                        lo(1 - g, i)

            each_group(e, f, group)

        def ffn_start_dve(e, f):
            for m in range(KD):
                for i in range(GT - LAG, GT):
                    e.memset(wd(w_hi[1], i, m).bitcast(F32), 0.0)
                    e.memset(wd(w_lo[1], i, m).bitcast(F32), 0.0)
            for sl in range(3 - LAG, 3):
                e.memset(h_hi[sl][:, :].bitcast(F32), 0.0)
                ins = e.memset(h_lo[sl][:, :].bitcast(F32), 0.0)
            e_hz.mark(ins)

        def ffn_dve(e, f, x_from, x_to):
            def group(g, G, it, first, last):
                for i in range(GT):
                    T = G * GT + i
                    s = (g * GT + i) % 2
                    e_silu.wait(e, T + 1)
                    e_u.wait(e, T + 1)
                    e_h1.mark(e.tensor_tensor(h1[s][:, :], sg[s][:, :], bank[4 + s][:, :], ALU.mult))
                    if first and g == 0 and i == 0:
                        comb_dve(e, f)
                    e_cb.wait(e, T + 1)
                    e_h1.wait(e, T + 1)
                    e_h.mark(e.tensor_tensor(hf[s][:, :], h1[s][:, :], bank[6 + s][:, :], ALU.mult))
                    e_hh.wait(e, T + 1)
                    e_hl.mark(e.tensor_tensor(h_lo[(g * GT + i) % 3][:, :], hf[s][:, :],
                                              h_hi[(g * GT + i) % 3][:, :].bitcast(F32), ALU.subtract))

            each_group(e, f, group)
            e_down.wait(e, (f + 1) * DOWNS)
            for m in range(KD):
                e.scalar_tensor_tensor(x_to[:, m, :], bank[m][:, :], 0.5, x_from[:, m, :], ALU.mult, ALU.add)

        def ffn_load_sp(e, f):
            for g in range(2):
                a_wraw[g].mark(e.dma_start(w_raw[g][:, :], w_ffn[g]))

        def ffn_sp(e, f):
            def group(g, G, it, first, last):
                e_cb.wait(e, GT * (G - 1))
                n = it * 2 + g
                src = comb_dram[n * GE:(n + 1) * GE] if last else comb_dram[bass.ds(n * GE, GE), :, :]
                a_comb[g].mark(e.dma_start(comb_rows[g][:, :].bitcast(F32), src.rearrange("n h t -> (n h) t")))
                if not last:
                    e_wP.wait(e, GT * (G + 1))
                    a_wraw[g].mark(e.dma_start(w_raw[g][:, :], w_ffn[bass.ds(n + 2, 1), :, :].rearrange("a p c -> (a p) c")))

            each_group(e, f, group)

        a_r1, a_r2, a_roww = arr("a_r1"), arr("a_r2"), arr("a_roww")
        a_rows, a_rr = [arr(f"a_rows{i}") for i in range(4)], [arr(f"a_rr{i}") for i in range(2)]
        a_wb, a_th = [arr(f"a_wb{i}") for i in range(2)], [arr(f"a_th{i}") for i in range(2)]
        a_aw, a_tw = arr("a_aw"), arr("a_tw")
        e_bA, e_bP, e_tA, e_tP = ev("e_bA"), ev("e_bP"), ev("e_tA"), ev("e_tP")
        e_th, e_dtb, e_ths, e_tu, e_cum = ev("e_th", 1), ev("e_dtb"), ev("e_ths"), ev("e_tu"), ev("e_cum")
        e_rnd, e_nfr, e_afr, e_cs = ev("e_rnd"), ev("e_nfr"), ev("e_afr"), ev("e_cs")
        e_rB, e_rC, e_aB, e_xb, e_xcc = ev("e_rB"), ev("e_rC", 2), ev("e_aB"), ev("e_xb"), ev("e_xcc")
        e_t, e_R, e_D, e_xw, e_xp = ev("e_t", 6), ev("e_R"), ev("e_D"), ev("e_xw"), ev("e_xp")
        e_G, e_M, e_bte, e_bt = ev("e_G"), ev("e_M", 1), ev("e_bte"), ev("e_bt", 4)
        e_S, e_sm, e_H, e_Y, e_yev = ev("e_S", 1), ev("e_sm"), ev("e_H", 2), ev("e_Y", 3), ev("e_yev")
        e_pj, e_X, e_sqs, e_ssm, e_sr = ev("e_pj", 4), ev("e_X", 2), ev("e_sqs"), ev("e_ssm", 2), ev("e_sr")
        e_rl, e_p1, e_p2, e_p3, e_p4, e_p5, e_pc = (ev(n) for n in "e_rl e_p1 e_p2 e_p3 e_p4 e_p5 e_pc".split())
        e_z, e_sz, e_yT, e_gt, e_o = (ev(n) for n in "e_z e_sz e_yT e_gt e_o".split())
        W = [bank[4], bank[5], bank[6], bank[7]]
        XBANK = [bank[0], bank[1]]
        SSB, YB = bank[2], bank[3]
        pair_w = lambda w, i, k: w[:, (i * KD + k) * P:(i * KD + k + 1) * P]
        xpair = [(xh[:, k, :], xl[:, k, :]) for k in range(KD)]
        y4 = lambda a: a.rearrange("p (k h d) -> p k h d", k=NC, h=2 * UN)

        xbanks = [bank[3], W[3], W[0], W[1]]

        def prep_pe(e, b):
            def inner(t):
                for k in range(KD):
                    ins = e.matmul(xbanks[t][:, :], xn[:, k, t * P:(t + 1) * P], wx_sb[:, k, :], start=k == 0, stop=k == KD - 1)
                e_p2.mark(ins)

            a_aw.wait(e, 6 * (b + 1))
            for k in range(KD):
                ins = e.matmul(W[0][0:NH, :], wdth_sb[:, k, :], xn[:, k, 0:SEQ], start=k == 0, stop=k == KD - 1)
            for s in range(2):
                for t in range(TT):
                    for k in range(KD):
                        ins = e.matmul(W[1 + s][:, t * P:(t + 1) * P], xn[:, k, t * P + s:(t + 1) * P + s], wdtl_sb[:, k, :],
                                       start=k == 0, stop=k == KD - 1)
            e_p1.mark(ins)
            e_xl.wait(e, KD * (3 * b + 2))
            A_pe(e, b * NP, 0)
            inner(0)
            inner(1)
            A_pe(e, b * NP + 1, 1)
            e_pd.wait(e, b * PREP_STEPS + 3)
            inner(2)
            inner(3)
            ss_pe(e, b * NP, 0)
            ss_pe(e, b * NP + 1, 1)
            e_p4.hold(e, b + 1)
            for k in range(NC):
                ins = e.matmul(W[2][CL:P, k * CL:(k + 1) * CL], dect[:, k * CL:(k + 1) * CL], ident[0:NH, 0:NH],
                               start=True, stop=True)
            e_p5.mark(ins)
            A_pe(e, b * NP + 2, 2)

        def prep_act(e, b):
            e_p1.wait(e, b + 1)
            parts = ((sp_e[0:NH, 0, :], W[0][0:NH, :]), (tok(sp_e, 1), steps_of(0)), (tok(sp_e, 2), steps_of(1)))
            for s in range(2):
                ins = e.activation(lamk[:, s], tail_of(s), ACT.Sigmoid)
            e_p3.mark(ins)
            for o, i in parts:
                ins = e.activation(o, i, ACT.Abs)
            e_pc.mark(ins)
            A_act(e, b * NP, 0, [0])
            e_pc.wait(e, 6 * b + 1)
            e.activation(hm(sp_e), hm(sp_e), ACT.Exp, scale=-1.0)
            e_pc.mark(e.activation(tm(sp_e), tm(sp_e), ACT.Exp, scale=-1.0))
            e_pc.mark(e.activation(neg_a[:, :], neg_a[:, :], ACT.Exp))
            A_act(e, b * NP, 0, [1])
            e_pc.wait(e, 6 * b + 3)
            e_pc.mark(e.activation(neg_a[:, :], neg_a[:, :], ACT.Copy, scale=-1.0))
            e_pu.wait(e, b + 1)
            e.activation(hm(sp_l), hm(sp_u), ACT.Ln)
            e_pc.mark(e.activation(tm(sp_l), tm(sp_u), ACT.Ln))
            A_act(e, b * NP, 0, [2, 3])
            sb_act(e, b * NP + 2, 0, b * (NP // 2) + 2)
            e_pc.wait(e, 6 * b + 5)
            e_p6.wait(e, b + 1)
            e_pc.mark(e.activation(alpha, dth, ACT.Exp, scale=neg_a[:, 0:1]))
            A_act(e, b * NP + 1, 1, [0, 1])
            sq_act(e, b * NP)
            e_p4.wait(e, b + 1)
            e_p3.mark(e.activation(hrow_hi, hrow, ACT.Copy))
            A_act(e, b * NP + 1, 1, [2, 3])
            sq_act(e, b * NP + 1)
            e_p5.wait(e, b + 1)
            src = W[2][CL:P, :].rearrange("p (k a q) -> p k q a", k=NC, a=2)
            e_p3.mark(e.activation(decay_t[CL:P, :, :, :], src, ACT.Copy))

        PREP_STEPS = 10
        e_pd, e_pu, e_p6 = ev("e_pd"), ev("e_pu"), ev("e_p6")
        sp_e, sp_u, sp_l = rot[1][:, 0:2, :], rot[1][:, 2:4, :], btr
        hm, tm = (lambda a: a[0:NH, 0, :]), (lambda a: a[:, 1, :])
        tok = lambda a, s: a[:, 1, (s - 1) * TT * NH:s * TT * NH].rearrange("p (t n) -> p t n", t=TT)
        steps_of = lambda s: W[1 + s][:, :].rearrange("p (t n) -> p t n", t=TT)[:, :, 0:NH]
        tail_of = lambda s: W[1 + s][:, :].rearrange("p (t n) -> p t n", t=TT)[:, :, NH:]

        def prep_dve(e, b):
            n = [0]
            def step(ins):
                e_pd.mark(ins)
                n[0] += 1
                e_pd.wait(e, b * PREP_STEPS + n[0])

            starts = lambda a: a.rearrange("p (k c) -> p k c", k=NC)[:, :, 0:1]
            e.memset(st_in[:, :], 0.0)
            e.memset(one[:, :], 1.0)
            e_pc.wait(e, 6 * b + 2)
            for part in (hm, tm):
                ins = e.tensor_scalar(part(sp_u), part(sp_e), 1.0, None, ALU.add)
            e_pu.mark(ins)
            e_pu.wait(e, b + 1)
            for part in (hm, tm):
                ins = e.scalar_tensor_tensor(part(sp_e), part(sp_u), 1.0, part(sp_e), ALU.subtract, ALU.subtract)
            step(ins)
            e_pc.wait(e, 6 * b + 5)
            for part in (hm, tm):
                ins = e.tensor_tensor(part(sp_l), part(sp_l), part(sp_e), ALU.subtract)
            step(ins)
            e_p6.mark(e.scalar_tensor_tensor(dth, W[0][0:NH, :], 0.0, sp_l[0:NH, 0, :], ALU.max, ALU.add))
            for s in range(2):
                ins = e.scalar_tensor_tensor(dtk[:, s], steps_of(s), 0.0, tok(sp_l, s + 1), ALU.max, ALU.add)
            step(ins)
            e_pc.wait(e, 6 * b + 6)
            step(e.tensor_copy(alpha0, alpha))
            step(e.memset(starts(alpha0), 0.0))
            step(e.tensor_tensor(alpha, alpha, alpha0, ALU.subtract))
            step(e.tensor_tensor_scan(dect, alpha0, alpha, 0.0, ALU.mult, ALU.add))
            e.tensor_copy(hrow[:, 0:SEQ], dth)
            e.tensor_copy(hrow[:, SEQ:2 * SEQ], alpha0)
            e.memset(hrow[:, 2 * SEQ:2 * SEQ + 1], 0.0)
            ends = dect.rearrange("p (k c) -> p k c", k=NC)[:, 0:NC - 1, CL - 1]
            e_p4.mark(e.tensor_copy(hrow[:, 2 * SEQ + 1:ROWW], ends))
            e_p3.wait(e, 3 * b + 2)
            e_p4b.mark(e.tensor_tensor(hrow_lo, hrow, hrow_hi.bitcast(F32), ALU.subtract))
            e.tensor_tensor(gam, lamk[:, 0], dtk[:, 0], ALU.mult)
            step(e.tensor_scalar(oml, lamk[:, 1], -1.0, 1.0, ALU.mult, ALU.add))
            step(e.tensor_tensor(dlt, oml, dtk[:, 1], ALU.mult))
            step(e.tensor_tensor(coef, gam, dlt, ALU.add))
            assert n[0] == PREP_STEPS
            wide = lambda a, t: a[:, t, :].unsqueeze(2).to_broadcast([P, NH, HP])
            for t in range(TT):
                e_p2.wait(e, TT * b + t + 1)
                src = xbanks[t][:, :].rearrange("p (n d) -> p n d", n=NH)
                e.tensor_tensor(x1[:, :, t, :], src, wide(coef, t), ALU.mult)
                ins = e.tensor_tensor(x2[:, :, t, :], src, wide(gam, t), ALU.mult)
            e_x12.mark(ins)

        e_x12 = ev("e_x12")
        e_p4b = ev("e_p4b")

        def attn_load_sp(e, b):
            for s in range(2):
                a_th[s].mark(e.dma_start(th_raw[s][:, :], w_th[s]))
                a_wb[s].mark(e.dma_start(wb_raw[s][:, :], w_bc[s]))
            for dst, src in ((wx_sb, w_x), (wdtl_sb, w_dtl), (wdth_sb, w_dth),
                             (bias, bias_in), (norm_w, norm_w_in), (neg_a, a_log)):
                a_aw.mark(e.dma_start(dst[:], src))

        def early_sp(e, b):
            e_tP.hold(e, b * NP + 1)
            a_th[0].mark(e.dma_start(th_raw[0][:, :], w_th[2]))
            for i in range(2):
                e_bP.hold(e, b * NP + 1 + i)
                a_wb[i].mark(e.dma_start(wb_raw[i][:, :], w_bc[2 + i]))

        def attn_start_act(e, b):
            st_act(e, b * NP, 0, b * (NP // 2) + 1)
            sb_act(e, b * NP, 0, b * (NP // 2) + 1)
            sb_act(e, b * NP + 1, 1, b * (NP // 2) + 1)

        def prep_sp(e, b):
            for hl, src, evt in ((0, hrow_hi, (e_p3, 3 * b + 2)), (1, hrow_lo, (e_p4b, b + 1))):
                evt[0].hold(e, evt[1])
                src = src[:, :].bitcast(F32)
                for a in range(2):
                    r = slice(a * NP, (a + 1) * NP)
                    a_roww.mark(e.dma_start(row_dram[:, 2 * a + hl, 0:SEQ], src[r, 0:SEQ]))
                    a_roww.mark(e.dma_start(row_dram[:, 2 * a + hl, 2 * SEQ:ROWW], src[r, 2 * SEQ:ROWW]))
                    for kp in range(2):
                        dst = row_dram[:, 2 * kp + hl, SEQ + a * (SEQ // 2):SEQ + (a + 1) * (SEQ // 2)]
                        s4 = src[r, SEQ:2 * SEQ].rearrange("p (t k c) -> p t k c", t=TT, k=2)
                        a_roww.mark(e.dma_start(dst.rearrange("q (t c) -> q t c", t=TT), s4[:, :, kp, :]))
            a_roww.hold(e, 16 * (b + 1))
            for j in range(2):
                a_rows[j].mark(e.dma_start(rows[32 * j:32 * j + 4, :].bitcast(F32), row_dram[j]))

        def T_pe(e, m, j):
            e_tP.wait(e, m + 1)
            e_bt.wait(e, 2 * (m - 2))
            e_th.mark(split_matmul(e, W[2][:, :], [((pair_w(th_hi[j % 2], 0, k), pair_w(th_lo[j % 2], 0, k)), xpair[k])
                                                   for k in range(KD)], True, True))
            e_H.wait(e, m - 2)
            r = slice(32 * (j % 4), 32 * (j % 4) + 4)
            e_dtb.mark(e.matmul(W[3][:, :], row_sel[r, :], rows[r, 0:SEQ], start=True, stop=True))

        def T_dve1(e, m, j):
            e_ths.wait(e, m + 1)
            e_dtb.wait(e, m + 1)
            e_nfr.wait(e, m)
            e_tu.mark(e.tensor_tensor(turns[:, :], ths[:, :], W[3][:, :], ALU.mult))
            e_tu.wait(e, m + 1)
            e_cum.mark(e.tensor_tensor_scan(cum[:, :], ones, turns[:, :], 0.0, ALU.mult, ALU.add))

        def T_dve2(e, m, j):
            e_rnd.wait(e, m + 1)
            e_cs.wait(e, m)
            e_cum.wait(e, m + 1)
            e_nfr.mark(e.scalar_tensor_tensor(nfr[:, :], rnd[:, :], MAGIC, cum[:, :], ALU.subtract, ALU.subtract))

        def T_act1(e, m, j):
            e_th.wait(e, m + 1)
            e_tu.wait(e, m)
            e_cs.wait(e, m)
            e_ths.mark(e.activation(ths[:, :], W[2][:, :], ACT.Copy, scale=float(1 / (2 * np.pi))))

        def T_act2(e, m, j):
            e_cum.wait(e, m + 1)
            e_nfr.wait(e, m)
            e_rnd.mark(e.activation(rnd[:, :], cum[:, :], ACT.Identity, bias=magic[:, 0:1]))

        def T_act3(e, m, j):
            e_nfr.wait(e, m + 1)
            e_t.wait(e, 2 * (m - 1))
            e_afr.mark(e.activation(afr[:, :], nfr[:, :], ACT.Abs))
            e.activation(sn[j % 2][:, :], nfr[:, :], ACT.Sin, scale=-TWO_PI)
            e_afr.wait(e, m + 1)
            e_cs.mark(e.activation(cs[j % 2][:, :], afr[:, :], ACT.Sin, scale=-TWO_PI, bias=half_pi[:, 0:1]))

        def A_pe(e, m, j, parts=range(4)):
            if parts[0] == 0:
                e_bP.wait(e, m + 1)
            for i in parts:
                e_X.wait(e, 4 * m + i - 1)
                e_pj.mark(split_matmul(e, XBANK[i % 2][:, :],
                                       [((pair_w(wb_hi[j % 2], i, k), pair_w(wb_lo[j % 2], i, k)), xpair[k])
                                        for k in range(KD)], True, True))

        def ss_pe(e, m, j):
            if j % 2 == 0:
                e_sr.wait(e, m // 2 if isinstance(m, int) else m >> 1)
            for ty in range(2):
                e_sql.wait(e, 2 * m + ty + 1)
                c = (j % 2) * 2 + ty
                for part in (sq_hi, sq_lo):
                    ins = e.matmul(SSB[:, :], one_hot[:, 6 - 2 * c:6 - 2 * c + P], part[:, ty, :],
                                   start=c == 0 and part is sq_hi, stop=c == 3 and part is sq_lo, skip_group_check=True)
                e_ssm.mark(ins)

        def A_act(e, m, j, parts=range(4)):
            if parts[0] == 0:
                e_t.wait(e, 2 * (m - 3))
            for i in parts:
                e_pj.wait(e, 4 * m + i + 1)
                e.activation(xbc[j % 4][:, i, :], XBANK[i % 2][:, :], ACT.Copy)
                if i % 2 == 0:
                    e_sqs.wait(e, 2 * m + i // 2)
                e_X.mark(e.activation(sqt[:, i % 2, :], XBANK[i % 2][:, :], ACT.Square))

        def A_pool(e, m, types=range(2)):
            for ty in types:
                e_X.wait(e, 4 * m + 2 * ty + 2)
                e_sql.wait(e, 2 * (m - 1) + ty + 1)
                e_sqs.mark(e.tensor_tensor(sqs[:, ty, :], sqt[:, 0, :], sqt[:, 1, :], ALU.add))

        def sq_act(e, m, types=range(2)):
            for ty in types:
                e_sqs.wait(e, 2 * m + ty + 1)
                e_ssm.wait(e, 2 * (m - 1) + ty + 1)
                e_sqh.mark(e.activation(sq_hi[:, ty, :], sqs[:, ty, :], ACT.Copy))

        def sq_pool(e, m, types=range(2)):
            for ty in types:
                e_sqh.wait(e, 2 * m + ty + 1)
                e_sql.mark(e.tensor_tensor(sq_lo[:, ty, :], sqs[:, ty, :], sq_hi[:, ty, :].bitcast(F32), ALU.subtract))

        e_sqh, e_sql = ev("e_sqh"), ev("e_sql", 2)

        def split_act(e, s, m, evA, free, arrival, raw, hi, n):
            arrival[s].wait(e, n)
            free()
            evA.mark(e.activation(hi[s][:, :], raw[s][:, :], ACT.Copy))

        def sb_act(e, m, j, cnt):
            a_wb[j % 2].wait(e, cnt)
            e_pj.wait(e, 4 * (m - 1))
            e_bA.mark(e.activation(wb_hi[j % 2][:, :], wb_raw[j % 2][:, :], ACT.Copy))

        def sb_pool(e, m, j):
            e_bA.wait(e, m + 1)
            e_bP.mark(e.tensor_tensor(wb_lo[j % 2][:, :], wb_raw[j % 2][:, :], wb_hi[j % 2][:, :].bitcast(F32), ALU.subtract))

        def st_act(e, m, j, cnt):
            a_th[j % 2].wait(e, cnt)
            e_th.wait(e, m - 1)
            e_tA.mark(e.activation(th_hi[j % 2][:, :], th_raw[j % 2][:, :], ACT.Copy))

        def st_pool(e, m, j):
            e_tA.wait(e, m + 1)
            e_tP.mark(e.tensor_tensor(th_lo[j % 2][:, :], th_raw[j % 2][:, :], th_hi[j % 2][:, :].bitcast(F32), ALU.subtract))

        def R_act(e, gm):
            e_ssm.wait(e, 4 * (gm + 1))
            a_r1.wait(e, gm)
            e_sr.mark(e.activation(stdr[:, :], SSB[0:8, :], ACT.Sqrt, scale=1.0 / NS, bias=eps_nm[0:8, 0:1]))

        def R_dve(e, gm):
            a_r1.wait(e, gm + 1)
            a_r2.wait(e, 2 * gm)
            e_rc.mark(e.reciprocal(rc[:, :], rc_in[:, :]))
            e_rc.wait(e, 2 * gm + 1)
            e_rc.mark(e.tensor_copy(rc_hi[:, :], rc[:, :]))
            e_rc.wait(e, 2 * gm + 2)
            e_rl.mark(e.tensor_tensor(rc_lo[:, :], rc[:, :], rc_hi[:, :].bitcast(F32), ALU.subtract))

        e_rc = ev("e_rc")

        def R_sp(e, gm, par, cnt):
            e_sr.hold(e, gm + 1)
            e_rl.hold(e, gm)
            a_r1.mark(e.dma_start(rc_in[:, :], stdr[:, :].rearrange("r (c w) -> r c w", w=32)))
            e_rl.hold(e, gm + 1)
            for hl, src in ((0, rc_hi), (1, rc_lo)):
                dst = rr_dram[par][hl].rearrange("r (c w) -> (r c) w", w=32)
                a_r2.mark(e.dma_start(dst, src[:, :].bitcast(F32)))
            a_r2.hold(e, 2 * (gm + 1))
            e_rC.hold(e, 2 * (gm - 1))
            for a in range(2):
                src = rr_dram[par].rearrange("h (g a) t -> a h g t", a=2)[a]
                a_rr[par].mark(e.dma_start(rrow[32 * par + 2 * a:32 * par + 2 * a + 2, :, :].bitcast(F32), src))

        def F_pe(e, n, j, cnt):
            par = (j // 2) % 2
            if j % 2 == 0:
                a_rr[par].wait(e, 2 * cnt)
            e_M.wait(e, n - 1)
            r = slice(32 * par, 32 * par + 4)
            for ty, evt in ((0, e_rB), (1, e_rC)):
                evt.mark(e.matmul(W[ty][:, :], row_sel[r, :], rrow[r, (j % 2) * 2 + ty, :], start=True, stop=True))

        def F_pe2(e, n, j, with_T):
            e_ths.wait(e, n + 2 if with_T else n + 1)
            r = slice(32 * j, 32 * j + 4)
            e_aB.mark(e.matmul(W[2][:, :], row_sel[r, :], rows[r, SEQ:2 * SEQ], start=True, stop=True))

        def F_dve1(e, n, j):
            e_X.wait(e, 4 * (n + 1))
            for ty, src, dst in ((0, e_rB, e_xb), (1, e_rC, e_xcc)):
                src.wait(e, n + 1)
                for i in (2 * ty, 2 * ty + 1):
                    ins = e.scalar_tensor_tensor(xbc[j][:, i, :], xbc[j][:, i, :], norm_w[:, i:i + 1], W[ty][:, :], ALU.mult, ALU.mult)
                dst.mark(ins)

        def F_dve2(e, n, j):
            p2, dk = j % 2, dks[j % 2]
            e_aB.wait(e, n + 1)
            e_M.wait(e, n - 1)
            e_D.mark(e.tensor_tensor_scan(dk, constant("shift_mask"), W[2][:, :], 0.0, ALU.add, ALU.mult))
            e_D.wait(e, n + 1)
            e_xp.wait(e, n + 1)
            e_S.wait(e, n - 1)
            dend = dk.rearrange("p (c w) -> p c w", w=CL)[:, :, CL - 1:CL].to_broadcast([P, 2 * TT, PW])
            e_xw.mark(e.scalar_tensor_tensor(xwp[p2][:, :].rearrange("p (c w) -> p c w", w=PW), dend, constant("last_row"),
                                             x1p[j][:, :].rearrange("p (c w) -> p c w", w=PW), ALU.add, ALU.mult))

        def F_dve3(e, n, j, q, types):
            if types[0] == 0:
                e_xcc.wait(e, n + 1)
                e_cs.wait(e, n + 1)
                e_Y.wait(e, n - 1)
                e_R.wait(e, n)
            X, R, c, s = xbc[j], rot[j % 2], cs[j % 2], sn[j % 2]
            for ty in types:
                bias_of = lambda i: bias[:, bass.ds(q, 1) if not isinstance(q, int) else slice(q, q + 1), i:i + 1].rearrange("p a c -> p (a c)")
                for o, i, f in ((R[:, 2 * ty, :], 2 * ty, c), (tmp[:, 2 * ty, :], 2 * ty + 1, s),
                                (R[:, 2 * ty + 1, :], 2 * ty, s), (tmp[:, 2 * ty + 1, :], 2 * ty + 1, c)):
                    ins = e.scalar_tensor_tensor(o, X[:, i, :], bias_of(i), f[:, :], ALU.add, ALU.mult)
                e_t.mark(ins)

        def F_pool(e, n, j, types):
            R = rot[j % 2]
            for ty in types:
                e_t.wait(e, 2 * n + ty + 1)
                e.tensor_tensor(R[:, 2 * ty, :], R[:, 2 * ty, :], tmp[:, 2 * ty, :], ALU.subtract)
                ins = e.tensor_tensor(R[:, 2 * ty + 1, :], R[:, 2 * ty + 1, :], tmp[:, 2 * ty + 1, :], ALU.add)
            if ty == 1:
                e_R.mark(ins)

        def XP_pool(e, n, j, q):
            e_Y.wait(e, n - 3)
            mask = constant("chunk_mask").rearrange("p (c k d) -> p c k d", c=2 * TT, k=2)
            for dst, src in ((x1p, x1), (x2p, x2)):
                v = src[:, bass.ds(2 * q, 2) if not isinstance(q, int) else slice(2 * q, 2 * q + 2), :, :]
                v = v.rearrange("p a t d -> p (a t) d").unsqueeze(2).to_broadcast([P, 2 * TT, 2, HP])
                ins = e.tensor_tensor(dst[j % 4][:, :].rearrange("p (c k d) -> p c k d", c=2 * TT, k=2), v, mask, ALU.mult)
            e_xp.mark(ins)

        def K1_pe(e, p, j, with_F, with_T):
            R = rot[j % 2]
            e_R.wait(e, p + 1)
            e_tu.hold(e, p + 1 + with_F + with_T)
            for a in range(2):
                if a and with_F:
                    e_xb.hold(e, p + 2)
                dst, h = W[3 if a == 0 else 0], slice(CL * a, CL * a + CL)
                for k in range(NC):
                    o = dst[CL * (k % 2):CL * (k % 2) + CL, CL * (k // 2):CL * (k // 2) + CL]
                    for eo in range(2):
                        ins = e.matmul(o, R[h, eo, CL * k:CL * k + CL], R[h, 2 + eo, CL * k:CL * k + CL],
                                       start=eo == 0, stop=eo == 1)
            e_G.mark(ins)
            for eo in range(2):
                if with_F:
                    (e_xcc, e_D)[eo].wait(e, p + 2)
                for t in range(TT):
                    ins = e.transpose(W[1 + eo][:, t * P:(t + 1) * P], R[:, eo, t * P:(t + 1) * P], ident[:, :])
                e_bte.mark(ins)

        def K_act(e, p, j):
            for eo in range(2):
                e_bte.wait(e, 2 * p + eo + 1)
                e_S.wait(e, p)
                e_bt.mark(e.activation(btr[:, eo, :], W[1 + eo][:, :], ACT.Copy))

        def K_dve1(e, p, j):
            e_G.wait(e, p + 1)
            e_D.wait(e, p + 1)
            e_Y.wait(e, p)
            half, dk = slice(0, SEQ // 2), dks[j % 2]
            for a in range(2):
                g, c = W[3 if a == 0 else 0][:, half], slice(a * SEQ // 2, (a + 1) * SEQ // 2)
                e.tensor_tensor(m1[:, c], g, dk[:, c], ALU.mult)
                ins = e.tensor_tensor(m2[:, c], g, constant("diag_mask")[:, c], ALU.mult)
            e_M.mark(ins)

        def K2_pe(e, p, j):
            e_bt.wait(e, 2 * (p + 1))
            e_xw.wait(e, p + 1)
            e_M.wait(e, p + 1)
            xw = xwp[j % 2][:, :].rearrange("p (a t w) -> p a t w", a=2, t=TT)
            S = W[3]
            for eo in range(2):
                for t in range(TT):
                    nk = 2 if t < TT - 1 else 1
                    o = S[:, eo * 128:(eo + 1) * 128].rearrange("p (a d k) -> p a k d", a=2, d=HP)[:, :, 2 * t + 1:2 * t + 1 + nk, :]
                    i = xw[:, :, t, :].rearrange("p a (k d) -> p a k d", k=2)[:, :, 0:nk, :]
                    e.matmul(o, btr[:, eo, t * P:(t + 1) * P], i, start=True, stop=True)
            r = slice(32 * j, 32 * j + 4)
            ends = rows[r, 2 * SEQ:ROWW].unsqueeze(1).to_broadcast([4, 32, NC])
            e_S.mark(e.matmul(S[:, 256:512].rearrange("p (c k) -> p c k", k=NC), row_sel[r, :], ends, start=True, stop=True))

        def K_dve2(e, p, j):
            e_S.wait(e, p + 1)
            e_Y.wait(e, p)
            v = lambda a: a.rearrange("p (c k) -> p c k", k=NC)[:, :, 1:NC]
            e_sm.mark(e.tensor_tensor(v(st_in[:, :]), v(W[3][:, 0:256]),
                                      constant("head_mask").rearrange("p (c k) -> p c k", k=NC - 1), ALU.mult))
            e_sm.wait(e, p + 1)
            e_H.mark(e.tensor_tensor_scan(st[:, :], W[3][:, 256:512], st_in[:, :], 0.0, ALU.mult, ALU.add))

        def Y_pe(e, p, j, yev):
            if j == 0:
                e_yev.wait(e, yev)
            R, y, hist = rot[j % 2], YB[:, :].rearrange("p (k w) -> p k w", k=NC), st[:, :].rearrange("p (o w k) -> p o w k", o=2, k=NC)
            c16 = slice(PW * j, PW * j + PW)
            c4 = lambda a: a.rearrange("p (c k d) -> p c k d", k=2, d=HP)
            for a in range(2):
                for t in range(TT):
                    o = y[0:CL, 2 * t:2 * t + 2, PW * j + HP * a:PW * j + HP * a + HP]
                    for n, (m, x) in enumerate(((m1, x1p), (m2, x2p))):
                        e.matmul(o, m[:, (a * TT + t) * CL:(a * TT + t + 1) * CL], c4(x[j][:, :])[:, a * TT + t],
                                 start=n == 0, stop=n == 1)
            e_H.wait(e, p + 1)
            for k in range(NC):
                for eo in range(2):
                    ins = e.matmul(y[CL:P, k, c16], R[:, 2 + eo, CL * k:CL * k + CL], hist[:, eo, :, k], start=eo == 0, stop=eo == 1)
            e_Y.mark(ins)

        def Y_dve(e, p, q4, n):
            e_Y.wait(e, p + 1)
            if isinstance(q4, int):
                dec, cols = decay_t[CL:P, :, q4:q4 + UN, :], slice(q4 * PW, (q4 + UN) * PW)
            else:
                dec, cols = decay_t[CL:P, :, bass.ds(q4, UN), :], bass.ds(q4 * PW, UN * PW)
            dec = dec.rearrange("p k q a -> p k (q a)").unsqueeze(3).to_broadcast([CL, NC, 2 * UN, HP])
            e_ym.mark(e.tensor_tensor(y4(ytmp), y4(YB[CL:P, :]), dec, ALU.mult))
            e_ym.wait(e, n + 1)
            for h in range(2):
                of = lambda a: a.rearrange("p (t h w) -> p t h w", t=TT, h=2)[:, :, h, :]
                ins = e.tensor_tensor(ysb[h * CL:(h + 1) * CL, :, cols], of(ytmp), of(YB[0:CL, :]), ALU.add)
            e_yev.mark(ins)

        e_ym = ev("e_ym")

        def turn(eng, e, b, it, first, last):
            N, Q = b * NP + it * UN, it * UN
            NB = NP // UN
            for j in range(UN):
                n, q, p = N + j, Q + j, N + j - 1
                jp = (j - 1) % UN
                T = not (last and j == UN - 1)
                A = not last or j == 0
                SS = not last or j <= 1
                RG = j % 2 == 1 and not (last and j == 3)
                K = not (first and j == 0)
                gm = b * (NP // 2) + it * 2 + j // 2
                if eng == "pe":
                    if first and j == 1:
                        e_D.wait(e, n)
                    if T:
                        a_rows[(j + 1) % 4].wait(e, b * NB + it + 1 + (j == 3))
                        T_pe(e, n + 1, j + 1)
                    if A:
                        A_pe(e, n + 3, j + 3, [0])
                    F_pe(e, n, j, b * NB + it + 1)
                    F_pe2(e, n, j, T)
                    if A:
                        A_pe(e, n + 3, j + 3, [1])
                    if SS:
                        ss_pe(e, n + 2, j)
                    if K:
                        K1_pe(e, p, jp, True, T)
                    if A:
                        A_pe(e, n + 3, j + 3, [2])
                    if K:
                        K2_pe(e, p, jp)
                    if A:
                        A_pe(e, n + 3, j + 3, [3])
                    if K:
                        Y_pe(e, p, jp, b * NB + it)
                elif eng == "act":
                    if T:
                        T_act1(e, n + 1, j + 1)
                    if SS:
                        sq_act(e, n + 2, [1])
                    if not (last and j >= 2):
                        st_act(e, n + 2, j, b * (NP // 2) + it * 2 + 2 + j // 2)
                    if A:
                        A_act(e, n + 3, j + 3, [0])
                    if not last:
                        sb_act(e, n + 4, j, b * (NP // 2) + it * 2 + 3 + j // 2)
                    if T:
                        T_act2(e, n + 1, j + 1)
                    if RG:
                        R_act(e, gm + 1)
                    if A:
                        A_act(e, n + 3, j + 3, [1])
                    if K:
                        K_act(e, p, jp)
                    if A:
                        sq_act(e, n + 3, [0])
                    if T:
                        T_act3(e, n + 1, j + 1)
                    if A:
                        A_act(e, n + 3, j + 3, [2, 3])
                elif eng == "pool":
                    if SS:
                        sq_pool(e, n + 2, [1])
                    if not (last and j >= 2):
                        st_pool(e, n + 2, j)
                    if not last:
                        sb_pool(e, n + 4, j)
                    if A:
                        A_pool(e, n + 3, [0])
                    if T:
                        XP_pool(e, n + 1, j + 1, q + 1)
                    if A:
                        sq_pool(e, n + 3, [0])
                    if first and j == 0:
                        A_pool(e, n + 3, [1])
                    F_pool(e, n, j, [0])
                    if A and not (first and j == 0):
                        A_pool(e, n + 3, [1])
                    F_pool(e, n, j, [1])
                elif eng == "dve":
                    if j == 1 and not first:
                        Y_dve(e, n - 2, q - 1 - UN, b * NB + it - 1)
                    if T:
                        T_dve1(e, n + 1, j + 1)
                    F_dve1(e, n, j)
                    F_dve2(e, n, j)
                    if T:
                        T_dve2(e, n + 1, j + 1)
                    if K:
                        K_dve1(e, p, jp)
                    F_dve3(e, n, j, q, [0])
                    if RG:
                        R_dve(e, gm + 1)
                    if K:
                        K_dve2(e, p, jp)
                    F_dve3(e, n, j, q, [1])
                elif eng == "sp":
                    if not (last and j >= 2):
                        e_S.hold(e, n - 1)
                        s = (j + 2) % 4
                        src = row_dram[q + 2] if isinstance(q, int) else row_dram[bass.ds(q + 2, 1)].rearrange("a r w -> (a r) w")
                        a_rows[s].mark(e.dma_start(rows[32 * s:32 * s + 4, :].bitcast(F32), src))
                    if not (last and j >= 1):
                        e_tP.hold(e, n + 2)
                        src = w_th[q + 3] if isinstance(q, int) else w_th[bass.ds(q + 3, 1)].rearrange("a p w -> (a p) w")
                        a_th[(j + 1) % 2].mark(e.dma_start(th_raw[(j + 1) % 2][:, :], src))
                    if not last:
                        e_bP.hold(e, n + 3)
                        src = w_bc[q + 4] if isinstance(q, int) else w_bc[bass.ds(q + 4, 1)].rearrange("a p w -> (a p) w")
                        a_wb[j % 2].mark(e.dma_start(wb_raw[j % 2][:, :], src))
                    if RG:
                        R_sp(e, gm + 1, (j // 2 + 1) % 2, b * NB + it + 1)

        def pairs(eng, e, b):
            N, NB = b * NP, NP // UN
            G = b * (NP // 2)
            if eng == "pe":
                e_p3.wait(e, 3 * b + 3)
                e_x12.wait(e, b + 1)
                a_rows[0].wait(e, b * NB + 1)
                T_pe(e, N, 0)
                e_tu.wait(e, N + 1)
            elif eng == "act":
                R_act(e, G)
                st_act(e, N + 1, 1, G + 1)
                A_act(e, N + 2, 2)
                sb_act(e, N + 3, 1, G + 2)
                T_act1(e, N, 0)
                T_act2(e, N, 0)
                T_act3(e, N, 0)
                sq_act(e, N + 2, [0])
            elif eng == "pool":
                st_pool(e, N, 0)
                sb_pool(e, N, 0)
                sb_pool(e, N + 1, 1)
                A_pool(e, N)
                sb_pool(e, N + 2, 0)
                sq_pool(e, N)
                A_pool(e, N + 1)
                sq_pool(e, N + 1)
                e_x12.wait(e, b + 1)
                XP_pool(e, N, 0, 0)
                st_pool(e, N + 1, 1)
                A_pool(e, N + 2)
                sb_pool(e, N + 3, 1)
                sq_pool(e, N + 2, [0])
            elif eng == "dve":
                R_dve(e, G)
                T_dve1(e, N, 0)
                T_dve2(e, N, 0)
            elif eng == "sp":
                R_sp(e, G, 0, b * NB + 1)
            turn(eng, e, b, 0, True, False)
            with e.Fori(1, NB - 1) as it:
                turn(eng, e, b, it, False, False)
            turn(eng, e, b, NB - 1, False, True)
            if eng == "sp":
                e_t.hold(e, 2 * (N + NP - 3))
                a_tw.mark(e.dma_start(wz_sb, w_z))
                a_tw.mark(e.dma_start(wo_sb, w_out))
            p, j = N + NP - 1, UN - 1
            if eng == "pe":
                K1_pe(e, p, j, False, False)
                K2_pe(e, p, j)
                Y_pe(e, p, j, 0)
            elif eng == "act":
                K_act(e, p, j)
            elif eng == "dve":
                K_dve1(e, p, j)
                K_dve2(e, p, j)
                Y_dve(e, p, NP - UN, b * NB + NB - 1)

        def tail_pe(e, b):
            a_tw.wait(e, 2 * (b + 1))
            for f in range(KI):
                for k in range(KD):
                    ins = e.matmul(bank[4 + f][:, :], wz_sb[:, k, f * P:(f + 1) * P], xn[:, k, 0:SEQ], start=k == 0, stop=k == KD - 1)
                e_z.mark(ins)
            e_yev.wait(e, (b + 1) * (NP // UN))
            for f in range(KI):
                for t in range(TT):
                    ins = e.transpose(bank[f][:, t * P:(t + 1) * P], ysb[:, t, f * P:(f + 1) * P], ident[:, :])
                e_yT.mark(ins)
            e_gt.wait(e, KI * (b + 1))
            for m in range(KD):
                for f in range(KI):
                    ins = e.matmul(bank[4 + m][:, :], wo_sb[:, f, m * P:(m + 1) * P], gated[:, f, :], start=f == 0, stop=f == KI - 1)
                e_o.mark(ins)

        def tail_act(e, b):
            e_Y.wait(e, (b + 1) * NP)
            for f in range(KI):
                e_z.wait(e, KI * b + f + 1)
                e_sz.mark(e.activation(silu_z[:, f, :], bank[4 + f][:, :], ACT.Silu))

        def tail_dve(e, b):
            for f in range(KI):
                e_sz.wait(e, KI * b + f + 1)
                e_yT.wait(e, KI * b + f + 1)
                e_gt.mark(e.tensor_tensor(gated[:, f, :], silu_z[:, f, :], bank[f][:, :], ALU.mult))
            for m in range(KD):
                e_o.wait(e, KD * b + m + 1)
                e.tensor_tensor(xT[:, m, :], xT[:, m, :], bank[4 + m][:, :], ALU.add)

        NCONST = 4
        block = ctx.enter_context(nc.Block())

        def give_ahead(e, n):
            for v in events[n::5]:
                v.give_ahead(e)

        @block.tensor
        def _(e):
            give_ahead(e, 0)
            a_const.wait(e, NCONST)
            e_init.wait(e, 3)
            with e.Fori(0, BATCH) as b:
                a_x.wait(e, b + 1)
                ln_pe(e, 3 * b, x_first)
                router_pe(e, 2 * b, 3 * b)
                e_xl.wait(e, KD * (3 * b + 1))
                ffn_pe(e, 2 * b)
                end_phase(e, PHASES * b)
                ln_pe(e, 3 * b + 1)
                e_xn.wait(e, KD * (3 * b + 2))
                prep_pe(e, b)
                pairs("pe", e, b)
                tail_pe(e, b)
                end_phase(e, PHASES * b + 1)
                ln_pe(e, 3 * b + 2)
                router_pe(e, 2 * b + 1, 3 * b + 2)
                e_xl.wait(e, KD * (3 * b + 3))
                ffn_pe(e, 2 * b + 1)
                end_phase(e, PHASES * b + 2)

        @block.scalar
        def _(e):
            give_ahead(e, 1)
            a_const.wait(e, NCONST)
            e.activation(sel[:, :, :], sel_raw[:, :, :], ACT.Copy)
            e.activation(one_hot[:, :], constant("one_hot"), ACT.Copy)
            e_init.mark(e.activation(row_sel[:, :], constant("row_sel"), ACT.Copy))
            e_init.wait(e, 3)
            with e.Fori(0, BATCH) as b:
                ln_act(e, 3 * b, lambda: ffn_start_act(e, 2 * b))
                router_act(e, 2 * b)
                ffn_act(e, 2 * b)
                end_phase(e, PHASES * b)
                ln_act(e, 3 * b + 1, lambda: attn_start_act(e, b))
                prep_act(e, b)
                pairs("act", e, b)
                tail_act(e, b)
                end_phase(e, PHASES * b + 1)
                ln_act(e, 3 * b + 2, lambda: ffn_start_act(e, 2 * b + 1))
                router_act(e, 2 * b + 1)
                ffn_act(e, 2 * b + 1)
                end_phase(e, PHASES * b + 2)

        @block.gpsimd
        def _(e):
            give_ahead(e, 2)
            e.memset(zero_w[:, :].bitcast(F32), 0.0)
            e.memset(mean_w[:, :], 1.0 / D)
            e.memset(xn[:, :, SEQ:], 0.0)
            e.memset(eps_nm[:, :], EPS_NORM)
            e.memset(magic[:, :], MAGIC)
            e.memset(half_pi[:, :], float(np.pi / 2))
            e_init.mark(e.memset(eps_ln[:, :], EPS_LN))
            with e.Fori(0, BATCH) as b:
                ffn_pool(e, 2 * b)
                end_phase(e, PHASES * b)
                pairs("pool", e, b)
                end_phase(e, PHASES * b + 1)
                ffn_pool(e, 2 * b + 1)
                end_phase(e, PHASES * b + 2)

        @block.vector
        def _(e):
            give_ahead(e, 3)
            e_init.mark(e.memset(top[:, :, :], 0.0))
            with e.Fori(0, BATCH) as b:
                ln_dve(e, 3 * b, lambda: ffn_start_dve(e, 2 * b), x_first)
                router_dve(e, 2 * b)
                ffn_dve(e, 2 * b, x_first, xT)
                end_phase(e, PHASES * b)
                ln_dve(e, 3 * b + 1, lambda: None)
                a_aw.wait(e, 6 * (b + 1))
                prep_dve(e, b)
                pairs("dve", e, b)
                tail_dve(e, b)
                end_phase(e, PHASES * b + 1)
                ln_dve(e, 3 * b + 2, lambda: ffn_start_dve(e, 2 * b + 1))
                router_dve(e, 2 * b + 1)
                ffn_dve(e, 2 * b + 1, xT, x_last)
                end_phase(e, PHASES * b + 2)

        @block.sync
        def _(e):
            give_ahead(e, 4)
            a_x.mark(e.dma_start(x_first[:, :, :], x_in[0]))
            a_const.mark(e.dma_start(sel_raw[:, :, :], sel_ffn_in))
            a_const.mark(e.dma_start(ident[:, :], ident_in))
            a_const.mark(e.dma_start(wr_sb[:, :, :], w_router))
            a_const.mark(e.dma_start(cst[:, :], cst_in))
            e_init.wait(e, 3)
            with e.Fori(0, BATCH) as b:
                ffn_load_sp(e, 2 * b)
                router_sp(e, 2 * b)
                ffn_sp(e, 2 * b)
                a_out.hold(e, b)
                end_phase(e, PHASES * b)
                attn_load_sp(e, b)
                early_sp(e, b)
                prep_sp(e, b)
                pairs("sp", e, b)
                end_phase(e, PHASES * b + 1)
                ffn_load_sp(e, 2 * b + 1)
                a_x.mark(e.dma_start(x_first[:, :, :], x_in[bass.ds((b + 1) % BATCH, 1), :, :, :].rearrange("a p k t -> (a p) k t")))
                router_sp(e, 2 * b + 1)
                ffn_sp(e, 2 * b + 1)
                end_phase(e, PHASES * b + 2)
                a_out.mark(e.dma_start(out[bass.ds(b, 1), :, :, :].rearrange("a p k t -> (a p) k t"), x_last[:, :, :]))
            a_x.hold(e, BATCH + 1)
            a_out.wait(e, BATCH)


def feature_major(w):
    return np.ascontiguousarray(w.reshape(-1, P, w.shape[1]).transpose(1, 0, 2))


def arrays_of(a):
    x = a["L0_attn_x"].transpose(0, 2, 1).reshape(BATCH, KD, P, SEQ).transpose(0, 2, 1, 3)
    groups = []
    for n in range(NG):
        s = slice(n * GE, (n + 1) * GE)
        g, u = (a[w][s].transpose(1, 0, 2).reshape(KD, P, GT * P).transpose(1, 0, 2).reshape(P, -1)
                for w in ("L0_ffn_Wg", "L0_ffn_Wu"))
        d = a["L0_ffn_Wd"][s].reshape(GT, P, D).transpose(1, 0, 2).reshape(P, -1)
        groups.append(np.concatenate([g, u, d], axis=1))
    def tiles(w, eo):
        w = w.reshape(NP, 2, -1, eo, D).transpose(0, 3, 4, 1, 2).reshape(NP, eo, KD, P, P)
        return w.transpose(0, 3, 1, 2, 4)
    bc = np.concatenate([tiles(a["L0_attn_WB"], 2), tiles(a["L0_attn_WC"], 2)], axis=2).reshape(NP, P, BCW)
    th = tiles(a["L0_attn_Wth"], 1).reshape(NP, P, THW)
    per_row = lambda v: v.reshape(NP, 2, NS // 2, 2).transpose(1, 2, 0, 3).reshape(P, NP, 2)
    bias = np.concatenate([per_row(a["L0_attn_B_bias"]), per_row(a["L0_attn_C_bias"])], axis=2)
    nw = np.concatenate([np.tile(a[w].reshape(NS // 2, 2), (2, 1)) for w in ("L0_attn_Bn_w", "L0_attn_Cn_w")], axis=1)
    by_parity = lambda v: v.reshape(NP, 2, -1).transpose(1, 0, 2).reshape(NH, -1)
    sel = np.zeros((2 * GE, GT, P), np.float32)
    for i in range(GT):
        for p in range(P):
            n = (i * P + p) // NI
            sel[2 * n:2 * n + 2, i, p] = 1.0
    p = np.arange(P)
    t = np.arange(SEQ) % CL
    shift = (t[None] == p[:, None] % CL + 1).astype(np.float32)
    diag = (t[None] == p[:, None] % CL).astype(np.float32)
    last = (p % CL == CL - 1).astype(np.float32)[:, None]
    head = (p[:, None, None, None, None] // CL == np.arange(2)[None, None, :, None, None]) * np.ones((P, 2, 2, HP, NC - 1))
    chunk = (p[:, None, None, None] // CL == np.arange(2)[None, None, :, None]) * np.ones((P, 2 * TT, 2, HP))
    row_sel = ((p[:, None] % 32) // 2 == p[None] // CL) * np.ones((P, P))
    one_hot = np.zeros((P, P + 6))
    one_hot[p, 6 + p // CL] = 1.0
    cst = np.concatenate([v.reshape(P, -1) for v in (shift, diag, last, head, chunk, row_sel, one_hot)], axis=1)
    arrays = {
        "x_in": x,
        "w_ffn": np.stack(groups),
        "w_router": feature_major(a["L0_ffn_Wr"].T),
        "w_bc": bc,
        "w_th": th,
        "w_x": feature_major(a["L0_attn_Wx"].T),
        "w_z": feature_major(a["L0_attn_Wz"].T),
        "w_dtl": feature_major(np.concatenate([a["L0_attn_Wdt"], a["L0_attn_Wlam"]]).T),
        "w_dth": feature_major(by_parity(a["L0_attn_Wdt"]).T),
        "a_log": by_parity(a["L0_attn_A_log"]),
        "w_out": feature_major(a["L0_attn_Wout"].T),
        "bias_in": bias,
        "norm_w_in": nw,
        "sel_ffn_in": sel,
        "ident_in": np.eye(P, dtype=np.float32),
        "cst_in": cst.astype(np.float32),
    }
    return {k: np.ascontiguousarray(v) for k, v in arrays.items()}


def kernel(**inputs):
    import concourse.bacc as bacc
    from concourse.bass_utils import run_bass_kernel_spmd

    arrays = arrays_of({k: np.asarray(v) for k, v in inputs.items()})
    nc = bacc.Bacc("TRN2", target_bir_lowering=False, num_devices=1)
    args = [nc.dram_tensor(n, v.shape, mybir.dt.from_np(v.dtype), kind="ExternalInput").ap() for n, v in arrays.items()]
    out = nc.dram_tensor("out_x", (BATCH, P, KD, SEQ), F32, kind="ExternalOutput").ap()
    build(nc, *args, out)
    r = run_bass_kernel_spmd(nc, [arrays], core_ids=[0])
    got = r.results[0]["out_x"]
    return np.ascontiguousarray(got.transpose(0, 3, 2, 1).reshape(BATCH, SEQ, D))
```

```python
from contextlib import ExitStack

import numpy as np
import concourse.bass as bass
from concourse import mybir

F32 = mybir.dt.float32
F32R = mybir.dt.float32r
ALU = mybir.AluOpType
ACT = mybir.ActivationFunctionType
AX_X = mybir.AxisListType.X

P = 128
BATCH, SEQ, D = 4, 512, 256
SG = 2
KD = D // P
NE, NI, TOPK = 64, 96, 8
GE = 4
GT = GE * NI // P
NG = NE // GE
GW = 3 * GT * D
PIECE = GW // GT
NT = NG * GT
TT = SEQ // P
RT = SG * TT
NU = NT * SG
LAG = SG
NH, HP, NS = 64, 8, 128
NP = NH // 2
CL = 64
NC = SEQ // CL
DIN = NH * HP
KI = DIN // P
UN = 4
PW = 2 * HP
ROWW = 2 * SEQ + NC
BCW, THW = 4 * KD * P, KD * P
EPS_LN, EPS_NORM = 1e-5, 1e-6
MAGIC = 12582912.0
TWO_PI = 6.283185


class Event:
    unit = 1

    def __init__(self, all_events, ctx, nc, name, ahead=0):
        self.sem, self.ahead = ctx.enter_context(nc.semaphore(name)), 1 + ahead
        all_events.append(self)

    def give_ahead(self, eng):
        eng.sem_inc(self.sem, self.ahead)

    def wait(self, eng, count):
        if isinstance(count, int) and count + self.ahead <= 1:
            return
        eng.wait_ge(self.sem, count * self.unit + self.ahead)

    def hold(self, eng, count):
        self.wait(eng, count)
        eng.nop(nofuse=True)

    def mark(self, ins):
        ins.then_inc(self.sem, self.unit)


class Arrival(Event):
    unit = 16


def split_matmul(e, dst, pairs, start, stop):
    n, c, ins = len(pairs) * 3, 0, None
    for (ah, al), (mh, ml) in pairs:
        for a, m in ((ah, mh), (al, mh), (ah, ml)):
            ins = e.matmul(dst, a, m, start=start and c == 0, stop=stop and c == n - 1,
                           skip_group_check=not (start and stop))
            c += 1
    return ins


def build(nc, x_in, w_ffn, w_router, w_bc, w_th, w_x, w_z, w_dtl, w_dth, a_log, w_out, bias_in, norm_w_in,
          sel_ffn_in, ident_in, cst_in, out):
    with ExitStack() as ctx:
        events = []

        def ev(name, ahead=0):
            return Event(events, ctx, nc, name, ahead)

        def arr(name):
            return Arrival(events, ctx, nc, name)

        def sb_in(c):
            return lambda name, shape, dt=F32: c.enter_context(nc.sbuf_tensor(name, shape, dt))

        bank = [ctx.enter_context(nc.psum_tensor(f"bank{i}", [P, SEQ], F32)) for i in range(8)]

        sb = sb_in(ctx)
        xs = sb("xs", [P, SG, KD, SEQ])
        xn = sb("xn", [P, KD, SEQ + 2])
        xh, xl = sb("xh", [P, KD, SEQ], F32R), sb("xl", [P, KD, SEQ], F32R)
        xc, sq = sb("xc", [P, KD, SEQ]), sb("sq", [P, KD, SEQ])
        std, rstd = sb("std", [P, TT]), sb("rstd", [P, TT])
        eps_ln, eps_nm, magic, half_pi = (sb(n, [P, 1]) for n in ("eps_ln", "eps_nm", "magic", "half_pi"))
        mean_w = sb("mean_w", [P, P])
        zero_w = sb("zero_w", [P, P], F32R)
        ident = sb("ident", [P, P])
        wr_sb = sb("wr_sb", [P, KD, NE])
        CST = {}
        at_col = 0
        for n, w in (("shift_mask", SEQ), ("diag_mask", SEQ), ("last_row", 1), ("head_mask", 32 * (NC - 1)),
                     ("chunk_mask", P), ("row_sel", P), ("one_hot", P + 6)):
            CST[n] = (at_col, w)
            at_col += w
        cst = sb("cst", [P, at_col])
        constant = lambda n: cst[:, CST[n][0]:CST[n][0] + CST[n][1]]
        row_sel = sb("row_sel", [P, P], F32R)
        one_hot = sb("one_hot", [P, P + 6], F32R)
        sel = sb("sel", [2 * GE, GT, P], F32R)

        with ExitStack() as ffn_ctx:
            sb = sb_in(ffn_ctx)
            sel_raw = sb("sel_raw", [2 * GE, GT, P])
            lmax, wsum, wrec = sb("lmax", [P, RT]), sb("wsum", [P, RT]), sb("wrec", [P, RT])
            lg, ex, rest, wsel, comb = (sb(n, [P, RT, NE]) for n in ("lg", "ex", "rest", "wsel", "comb"))
            top = sb("top", [P, RT, TOPK])
            comb_h, comb_l = sb("comb_h", [NE, SG, SEQ], F32R), sb("comb_l", [NE, SG, SEQ], F32R)
            comb_rows = [sb(f"comb_rows{i}", [2 * GE, SG, SEQ], F32R) for i in range(2)]
            w_raw = [sb(f"w_raw{i}", [P, GW]) for i in range(2)]
            w_hi = [sb(f"w_hi{i}", [P, GW], F32R) for i in range(2)]
            w_lo = [sb(f"w_lo{i}", [P, GW], F32R) for i in range(2)]
            sg, h1, hf = ([sb(f"{n}{i}", [P, SEQ]) for i in range(2)] for n in ("sg", "h1_", "hf"))
            h_hi = [sb(f"h_hi{i}", [P, SEQ], F32R) for i in range(3)]
            h_lo = [sb(f"h_lo{i}", [P, SEQ], F32R) for i in range(3)]
            xhs = [xh, sb("xh1", [P, KD, SEQ], F32R)]
            xls = [xl, sb("xl1", [P, KD, SEQ], F32R)]
            xn1, xc1, sq1 = (sb(n, [P, KD, SEQ]) for n in ("xn1", "xc1", "sq1"))
            std1, rstd1 = sb("std1", [P, TT]), sb("rstd1", [P, TT])
        comb_dram = nc.dram_tensor("comb_dram", [NE, 2, SG, SEQ], F32R, kind="Internal").ap().bitcast(F32)

        attn_ctx = ctx
        sb = sb_in(attn_ctx)
        xbc = [sb(f"xbc{i}", [P, 4, SEQ]) for i in range(4)]
        rot = [sb(f"rot{i}", [P, 4, SEQ]) for i in range(2)]
        tmp = sb("tmp", [P, 4, SEQ])
        sn, cs = ([sb(f"{n}{i}", [P, SEQ]) for i in range(2)] for n in ("sn", "cs"))
        ths, turns, nfr = (sb(n, [P, SEQ]) for n in ("ths", "turns", "nfr"))
        sqt = sb("sqt", [P, 2, SEQ])
        sqs = sb("sqs", [P, 2, SEQ])
        sq_hi, sq_lo = sb("sq_hi", [P, 2, SEQ], F32R), sb("sq_lo", [P, 2, SEQ], F32R)
        btr = sb("btr", [P, 2, SEQ])
        x1, x2 = sb("x1", [P, NH, TT, HP]), sb("x2", [P, NH, TT, HP])
        x1p = [sb(f"x1p{i}", [P, P]) for i in range(4)]
        x2p = [sb(f"x2p{i}", [P, P]) for i in range(4)]
        xwp = [sb(f"xwp{i}", [P, P]) for i in range(2)]
        st_in = sb("st_in", [P, 32 * NC])
        st = sb("st", [P, 32 * NC])
        ysb = sb("ysb", [P, TT, DIN])
        decay_t = sb("decay_t", [P, NC, NP, 2])
        rows = sb("rows", [P, ROWW], F32R)
        rrow = sb("rrow", [P, 4, SEQ], F32R)
        wb_raw, th_raw = ([sb(f"{n}{i}", [P, w]) for i in range(2)] for n, w in (("wb_raw", BCW), ("th_raw", THW)))
        wb_hi, wb_lo = ([sb(f"{n}{i}", [P, BCW], F32R) for i in range(2)] for n in ("wb_hi", "wb_lo"))
        th_hi, th_lo = ([sb(f"{n}{i}", [P, THW], F32R) for i in range(2)] for n in ("th_hi", "th_lo"))
        wx_sb = xbc[3][:, 0:KD, :]
        wz_sb = xbc[0][:, 0:KD, :]
        wo_sb = xbc[0][:, KD:, :].rearrange("p a b -> p (a b)").rearrange("p (f m) -> p f m", f=KI)
        wdtl_sb = xbc[2][:, 0, 0:KD * 2 * NH].rearrange("p (k n) -> p k n", k=KD)
        wdth_sb = xbc[2][:, 1, 0:KD * NH].rearrange("p (k n) -> p k n", k=KD)
        neg_a = sb("neg_a", [NH, 1])
        bias = sb("bias", [P, NP, 4])
        norm_w = sb("norm_w", [P, 4])
        stdr = decay_t[0:8, :, :, :].rearrange("p k q a -> p (k q a)")
        rc_in, rc, rc_hi, rc_lo = sb("rc_in", [P, 32]), sb("rc", [P, 32]), sb("rc_hi", [P, 32], F32R), sb("rc_lo", [P, 32], F32R)
        dks = [xc[:, i, :] for i in range(2)]
        m1, m2 = sq[:, 0, :], sq[:, 1, :]
        one, cum = sb("one", [P, 1]), sb("cum", [P, SEQ])
        ones = one[:, :].to_broadcast([P, SEQ])
        ytmp = cum[0:CL, :]
        afr, rnd = ths, turns
        dth = rot[0][0:NH, 0, :]
        alpha = rot[0][0:NH, 1, :]
        alpha0 = rot[0][0:NH, 2, :]
        dect = rot[0][0:NH, 3, :]
        hrow = rot[1][0:NH, 0:3, :].rearrange("p a b -> p (a b)")[:, 0:ROWW]
        dtk = tmp[:, 0, :].rearrange("p (s t n) -> p s t n", s=2, t=TT)
        lamk = tmp[:, 1, :].rearrange("p (s t n) -> p s t n", s=2, t=TT)
        gam = tmp[:, 2, 0:TT * NH].rearrange("p (t n) -> p t n", t=TT)
        oml = tmp[:, 2, TT * NH:].rearrange("p (t n) -> p t n", t=TT)
        dlt = tmp[:, 3, 0:TT * NH].rearrange("p (t n) -> p t n", t=TT)
        coef = tmp[:, 3, TT * NH:].rearrange("p (t n) -> p t n", t=TT)
        hrow_hi = rows[0:NH, :]
        hrow_lo = rrow[0:NH, :, :].rearrange("p a b -> p (a b)")[:, 0:ROWW]
        silu_z = [sqt[:, 0, :], sqt[:, 1, :], sqs[:, 0, :], sqs[:, 1, :]]
        gated = rot[1]
        row_dram = nc.dram_tensor("row_dram", [NP, 4, ROWW], F32R, kind="Internal").ap().bitcast(F32)
        rr_dram = [nc.dram_tensor(f"rr_dram{i}", [2, 8, SEQ], F32R, kind="Internal").ap().bitcast(F32) for i in range(2)]

        a_const, a_x, a_out = arr("a_const"), arr("a_x"), arr("a_out")
        a_wraw = [arr(f"a_wraw{i}") for i in range(2)]
        a_combw, a_comb = arr("a_combw"), [arr(f"a_comb{i}") for i in range(2)]
        e_init, e_phase = ev("e_init"), ev("e_phase")
        e_mean, e_xc, e_sq, e_var, e_std, e_rstd, e_xn, e_xh, e_xl = (
            ev(n) for n in "e_mean e_xc e_sq e_var e_std e_rstd e_xn e_xh e_xl".split())
        e_lg, e_sub, e_ex, e_chain, e_comb, e_ct, e_ch, e_cl = (
            ev(n) for n in "e_lg e_sub e_ex e_chain e_comb e_ct e_ch e_cl".split())
        e_hz = ev("e_hz")
        e_g, e_u, e_cb, e_down = ev("e_g"), ev("e_u"), ev("e_cb", 2 * GT), ev("e_down")
        e_silu, e_h1, e_h = ev("e_silu", 2), ev("e_h1", 2), ev("e_h", 2)
        e_hh, e_hl = ev("e_hh", LAG), ev("e_hl", LAG)
        e_wA, e_wP = ev("e_wA"), ev("e_wP")

        PHASES = 2 + SG
        e_xo = ev("e_xo")

        def end_phase(e, n):
            e_phase.mark(e.drain())
            e_phase.hold(e, 5 * (n + 1))

        def stream(s):
            if isinstance(s, int):
                return lambda k: xs[:, s, k, :]
            return lambda k: xs[:, bass.ds(s, 1), k, :].rearrange("p a t -> p (a t)")

        e_rb = ev("e_rb")
        LN_TILES = [(xc, sq, xn, xh, xl, std, rstd, bank[2], bank[3]),
                    (xc1, sq1, xn1, xhs[1], xls[1], std1, rstd1, bank[4], bank[5])]

        def layernorm(eng, e, r, streams, between):
            runs = [(r + i, x) + LN_TILES[i] for i, x in enumerate(streams)]
            if eng == "pe":
                for r, x, xc, sq, xn, h, l, std, rstd, mb, vb in runs:
                    for k in range(KD):
                        ins = e.matmul(mb[:, :], mean_w[:, :], x(k), start=k == 0, stop=k == KD - 1)
                    e_mean.mark(ins)
                for r, x, xc, sq, xn, h, l, std, rstd, mb, vb in runs:
                    e_sq.wait(e, r + 1)
                    for t in range(TT):
                        for k in range(KD):
                            ins = e.matmul(vb[:, t:t + 1], sq[:, k, t * P:(t + 1) * P], mean_w[:, 0:1], start=k == 0, stop=k == KD - 1)
                    e_var.mark(ins)
                for r, x, xc, sq, xn, h, l, std, rstd, mb, vb in runs:
                    e_rstd.wait(e, r + 1)
                    for t in range(TT):
                        ins = e.matmul(mb[:, t * P:(t + 1) * P], rstd[:, t:t + 1].to_broadcast([P, P]), ident[:, :], start=True, stop=True)
                    e_rb.mark(ins)
            elif eng == "dve":
                for r, x, xc, sq, xn, h, l, std, rstd, mb, vb in runs:
                    e_mean.wait(e, r + 1)
                    for k in range(KD):
                        ins = e.tensor_tensor(xc[:, k, :], x(k), mb[:, :], ALU.subtract)
                    e_xc.mark(ins)
                between()
                for r, x, xc, sq, xn, h, l, std, rstd, mb, vb in runs:
                    e_std.wait(e, r + 1)
                    e_rstd.mark(e.reciprocal(rstd[:, :], std[:, :]))
                for r, x, xc, sq, xn, h, l, std, rstd, mb, vb in runs:
                    e_rb.wait(e, r + 1)
                    for k in range(KD):
                        e_xn.mark(e.tensor_tensor(xn[:, k, 0:SEQ], xc[:, k, :], mb[:, :], ALU.mult))
                for r, x, xc, sq, xn, h, l, std, rstd, mb, vb in runs:
                    for k in range(KD):
                        e_xh.wait(e, KD * r + k + 1)
                        e_xl.mark(e.tensor_tensor(l[:, k, :], xn[:, k, 0:SEQ], h[:, k, :].bitcast(F32), ALU.subtract))
            else:
                for r, x, xc, sq, xn, h, l, std, rstd, mb, vb in runs:
                    e_xc.wait(e, r + 1)
                    e_sq.mark(e.activation(sq[:, :, :], xc[:, :, :], ACT.Square))
                for r, x, xc, sq, xn, h, l, std, rstd, mb, vb in runs:
                    e_var.wait(e, r + 1)
                    e_std.mark(e.activation(std[:, :], vb[:, 0:TT], ACT.Sqrt, bias=eps_ln[:, 0:1]))
                between()
                for r, x, xc, sq, xn, h, l, std, rstd, mb, vb in runs:
                    for k in range(KD):
                        e_xn.wait(e, KD * r + k + 1)
                        e_xh.mark(e.activation(h[:, k, :], xn[:, k, 0:SEQ], ACT.Copy))

        lgb, ctb = bank[0], [bank[1], bank[2]]

        def router_pe(e, s, r):
            e_xn.wait(e, KD * (r + 1))
            x = (xn, xn1)[s]
            for t in range(TT):
                for k in range(KD):
                    ins = e.matmul(lgb[:, (s * TT + t) * NE:(s * TT + t + 1) * NE], x[:, k, t * P:(t + 1) * P], wr_sb[:, k, :],
                                   start=k == 0, stop=k == KD - 1)
            e_lg.mark(ins)

        def comb_pe(e, f):
            e_comb.hold(e, f + 1)
            for s in range(SG):
                for t in range(TT):
                    ins = e.transpose(ctb[s][0:NE, t * P:(t + 1) * P], comb[:, s * TT + t, :], ident[:, :])
            e_ct.mark(ins)

        CHAIN = 6

        def router_dve(e, f):
            n = [0]

            def step(ins):
                e_chain.mark(ins)
                n[0] += 1
                e_chain.hold(e, f * CHAIN + n[0])

            logits = lgb[:, 0:RT * NE].rearrange("p (t n) -> p t n", t=RT)
            wide = lambda a: a[:, :].unsqueeze(2).to_broadcast([P, RT, NE])
            e_lg.wait(e, SG * (f + 1))
            step(e.tensor_reduce(lmax[:, :], logits, AX_X, ALU.max))
            e_sub.mark(e.tensor_tensor(lg[:, :, :], logits, wide(lmax), ALU.subtract))
            e_ex.hold(e, f + 1)
            for t in range(RT):
                ins = e.max(top[:, t, :], ex[:, t, :])
            step(ins)
            for t in range(RT):
                ins = e.match_replace(rest[:, t, :], top[:, t, :], ex[:, t, :], -1.0)
            step(ins)
            step(e.scalar_tensor_tensor(wsel[:, :, :], rest[:, :, :], 0.0, ex[:, :, :], ALU.is_lt, ALU.mult))
            step(e.tensor_reduce(wsum[:, :], wsel[:, :, :], AX_X, ALU.add))
            step(e.reciprocal(wrec[:, :], wsum[:, :]))
            assert n[0] == CHAIN
            e_comb.mark(e.tensor_tensor(comb[:, :, :], wsel[:, :, :], wide(wrec), ALU.mult))

        def comb_dve(e, f):
            e_ch.wait(e, f + 1)
            for s in range(SG):
                ins = e.tensor_tensor(comb_l[:, s, :], ctb[s][0:NE, :], comb_h[:, s, :].bitcast(F32), ALU.subtract)
            e_cl.mark(ins)

        def router_act(e, f):
            e_sub.wait(e, f + 1)
            e_ex.mark(e.activation(ex[:, :, :], lg[:, :, :], ACT.Exp))

        def comb_act(e, f):
            e_ct.wait(e, f + 1)
            for s in range(SG):
                ins = e.activation(comb_h[:, s, :], ctb[s][0:NE, :], ACT.Copy)
            e_ch.mark(ins)

        def router_sp(e, f):
            e_ch.hold(e, f + 1)
            a_combw.mark(e.dma_start(comb_dram[:, 0], comb_h[:, :, :].bitcast(F32)))
            e_cl.hold(e, f + 1)
            a_combw.mark(e.dma_start(comb_dram[:, 1], comb_l[:, :, :].bitcast(F32)))
            a_combw.hold(e, 2 * (f + 1))

        DOWNS = NU + LAG
        SPLITS = NG * GT

        wg = lambda w, k, i: w[:, k * GT * P + i * P:k * GT * P + (i + 1) * P]
        wu = lambda w, k, i: wg(w, KD + k, i)
        wd = lambda w, i, m: w[:, 2 * KD * GT * P + i * D + m * P:2 * KD * GT * P + i * D + (m + 1) * P]
        piece = lambda w, i: w[:, i * PIECE:(i + 1) * PIECE]

        def each_group(e, f, body):
            for g in range(2):
                body(g, f * NG + g, 0, True, False)
            with e.Fori(1, NG // 2 - 1) as it:
                for g in range(2):
                    body(g, f * NG + it * 2 + g, it, False, False)
            for g in range(2):
                body(g, f * NG + NG - 2 + g, NG // 2 - 1, False, True)

        acc = lambda s, m: bank[KD * s + m]
        gate_bank, up_bank = bank[4:6], bank[6:8]
        hslot = lambda i, s: (SG * i + s) % 3

        def ffn_pe(e, f):
            def down(i, s):
                for m in range(KD):
                    ins = split_matmul(e, acc(s, m)[:, :],
                                       [((wd(w_hi[i // GT], i % GT, m), wd(w_lo[i // GT], i % GT, m)),
                                         (h_hi[hslot(i, s)][:, :], h_lo[hslot(i, s)][:, :]))], False, False)
                e_down.mark(ins)

            def group(g, G, it, first, last):
                def gate_up(i, s):
                    u = (G * GT + i) * SG + s
                    x = [(xhs[s][:, k, :], xls[s][:, k, :]) for k in range(KD)]
                    e_h.wait(e, u + 1 - 2)
                    e_g.mark(split_matmul(e, gate_bank[s][:, :],
                                          [((wg(w_hi[g], k, i), wg(w_lo[g], k, i)), x[k]) for k in range(KD)], True, True))
                    e_h1.wait(e, u + 1 - 2)
                    e_u.mark(split_matmul(e, up_bank[s][:, :],
                                          [((wu(w_hi[g], k, i), wu(w_lo[g], k, i)), x[k]) for k in range(KD)], True, True))

                for i in range(GT):
                    if i == 0:
                        e_wP.wait(e, GT * G + 2)
                    if i == 1:
                        e_wP.wait(e, GT * G + 3)
                    start = first and g == 0 and i == 0
                    if start:
                        for s in range(SG):
                            gate_up(0, s)
                        comb_pe(e, f)
                        e_cl.wait(e, f + 1)
                        e_hz.wait(e, f + 1)
                        for n in range(SG * KD):
                            e.matmul(bank[n][:, :], zero_w[:, :], xh[:, 0, :], start=True, stop=False, skip_group_check=True)
                        for s in range(SG):
                            down(2 * GT - 1, s)
                    for s in range(SG):
                        u = (G * GT + i) * SG + s
                        if not start:
                            gate_up(i, s)
                        if i == 0 and s == 0:
                            a_comb[g].wait(e, f * (NG // 2) + it + 1)
                        e_silu.wait(e, u + 1)
                        e_cb.mark(e.matmul(gate_bank[s][:, :], sel[:, i, :], comb_rows[g][:, s, :], start=True, stop=True))
                        if not start:
                            e_hl.wait(e, u + 1 - LAG)
                            down((g * GT + i - 1) % (2 * GT), s)

            each_group(e, f, group)
            for s in range(SG):
                e_hl.wait(e, (f + 1) * NU - SG + s + 1)
                down(2 * GT - 1, s)

        def ffn_start_act(e, f):
            a_wraw[0].wait(e, f * (NG // 2) + 1)
            for i in range(GT):
                e_wA.mark(e.activation(piece(w_hi[0], i), piece(w_raw[0], i), ACT.Copy))

        def ffn_act(e, f):
            def silu(u, s):
                e_g.wait(e, u + 1)
                e_h1.wait(e, u + 1 - 2)
                e_silu.mark(e.activation(sg[s][:, :], gate_bank[s][:, :], ACT.Silu))

            def group(g, G, it, first, last):
                for i in range(GT):
                    for s in range(SG):
                        u = (G * GT + i) * SG + s
                        if first and g == 0 and i == 0:
                            if s == 0:
                                silu(u, 0)
                                silu(u + 1, 1)
                                comb_act(e, f)
                        else:
                            silu(u, s)
                        e_h.wait(e, u + 1)
                        e_down.wait(e, f * DOWNS + ((it * 2 + g) * GT + i) * SG + s)
                        e_hh.mark(e.activation(h_hi[hslot(i, s)][:, :], hf[s][:, :], ACT.Copy))
                        if s or (last and g):
                            continue
                        nx = 1 - g
                        a_wraw[nx].wait(e, f * (NG // 2) + it + 1 + g)
                        if i < 2:
                            e_u.wait(e, SG * GT * G)
                        else:
                            e_down.wait(e, f * DOWNS + (it * 2 + g) * GT * SG + LAG)
                        e_wA.mark(e.activation(piece(w_hi[nx], i), piece(w_raw[nx], i), ACT.Copy))

            each_group(e, f, group)

        def ffn_pool(e, f):
            def lo(s, i):
                e_wP.mark(e.tensor_tensor(piece(w_lo[s], i), piece(w_raw[s], i), piece(w_hi[s], i).bitcast(F32), ALU.subtract))

            for i in range(GT):
                e_wA.wait(e, f * SPLITS + i + 1)
                lo(0, i)

            def group(g, G, it, first, last):
                if not (last and g):
                    for i in range(GT):
                        e_wA.wait(e, GT * (G + 1) + i + 1)
                        lo(1 - g, i)

            each_group(e, f, group)

        def ffn_start_dve(e, f):
            for m in range(KD):
                e.memset(wd(w_hi[1], GT - 1, m).bitcast(F32), 0.0)
                e.memset(wd(w_lo[1], GT - 1, m).bitcast(F32), 0.0)
            for sl in range(3 - LAG, 3):
                e.memset(h_hi[sl][:, :].bitcast(F32), 0.0)
                ins = e.memset(h_lo[sl][:, :].bitcast(F32), 0.0)
            e_hz.mark(ins)

        def ffn_dve(e, f):
            def group(g, G, it, first, last):
                for i in range(GT):
                    for s in range(SG):
                        u = (G * GT + i) * SG + s
                        e_silu.wait(e, u + 1)
                        e_u.wait(e, u + 1)
                        e_h1.mark(e.tensor_tensor(h1[s][:, :], sg[s][:, :], up_bank[s][:, :], ALU.mult))
                        if first and g == 0 and i == 0 and s == 0:
                            comb_dve(e, f)
                        e_cb.wait(e, u + 1)
                        e_h1.wait(e, u + 1)
                        e_h.mark(e.tensor_tensor(hf[s][:, :], h1[s][:, :], gate_bank[s][:, :], ALU.mult))
                        e_hh.wait(e, u + 1)
                        e_hl.mark(e.tensor_tensor(h_lo[hslot(i, s)][:, :], hf[s][:, :],
                                                  h_hi[hslot(i, s)][:, :].bitcast(F32), ALU.subtract))

            each_group(e, f, group)
            e_down.wait(e, (f + 1) * DOWNS)
            for s in range(SG):
                for m in range(KD):
                    ins = e.scalar_tensor_tensor(xs[:, s, m, :], acc(s, m)[:, :], 0.5, xs[:, s, m, :], ALU.mult, ALU.add)
                e_xo.mark(ins)

        def ffn_load_sp(e, f):
            for g in range(2):
                a_wraw[g].mark(e.dma_start(w_raw[g][:, :], w_ffn[g]))

        def ffn_sp(e, f):
            def group(g, G, it, first, last):
                e_cb.wait(e, SG * GT * (G - 1))
                n = it * 2 + g
                src = comb_dram[n * GE:(n + 1) * GE] if isinstance(n, int) else comb_dram[bass.ds(n * GE, GE), :, :, :]
                a_comb[g].mark(e.dma_start(comb_rows[g][:, :, :].bitcast(F32), src.rearrange("n h s t -> (n h) s t")))
                if not last:
                    e_wP.wait(e, GT * (G + 1))
                    a_wraw[g].mark(e.dma_start(w_raw[g][:, :], w_ffn[bass.ds(n + 2, 1), :, :].rearrange("a p c -> (a p) c")))

            each_group(e, f, group)

        def ffn_start(eng, e, f, r):
            between = {"act": lambda: ffn_start_act(e, f), "dve": lambda: ffn_start_dve(e, f)}.get(eng)
            layernorm(eng, e, r, [stream(s) for s in range(SG)], between)
            if eng == "pe":
                for s in range(SG):
                    router_pe(e, s, r + s)
                e_xl.wait(e, KD * (r + SG))

        a_r1, a_r2, a_roww = arr("a_r1"), arr("a_r2"), arr("a_roww")
        a_rows, a_rr = [arr(f"a_rows{i}") for i in range(4)], [arr(f"a_rr{i}") for i in range(2)]
        a_wb, a_th = [arr(f"a_wb{i}") for i in range(2)], [arr(f"a_th{i}") for i in range(2)]
        a_aw, a_tw = arr("a_aw"), arr("a_tw")
        e_bA, e_bP, e_tA, e_tP = ev("e_bA"), ev("e_bP"), ev("e_tA"), ev("e_tP")
        e_th, e_dtb, e_ths, e_tu, e_cum = ev("e_th", 1), ev("e_dtb"), ev("e_ths"), ev("e_tu"), ev("e_cum")
        e_rnd, e_nfr, e_afr, e_cs = ev("e_rnd"), ev("e_nfr"), ev("e_afr"), ev("e_cs")
        e_rB, e_rC, e_aB, e_xb, e_xcc = ev("e_rB"), ev("e_rC", 2), ev("e_aB"), ev("e_xb"), ev("e_xcc")
        e_t, e_R, e_D, e_xw, e_xp = ev("e_t", 6), ev("e_R"), ev("e_D"), ev("e_xw"), ev("e_xp")
        e_G, e_M, e_bte, e_bt = ev("e_G"), ev("e_M", 1), ev("e_bte"), ev("e_bt", 4)
        e_S, e_sm, e_H, e_Y, e_yev = ev("e_S", 1), ev("e_sm"), ev("e_H", 2), ev("e_Y", 3), ev("e_yev")
        e_pj, e_X, e_sqs, e_ssm, e_sr = ev("e_pj", 4), ev("e_X", 2), ev("e_sqs"), ev("e_ssm", 2), ev("e_sr")
        e_rl, e_p1, e_p2, e_p3, e_p4, e_p5, e_pc = (ev(n) for n in "e_rl e_p1 e_p2 e_p3 e_p4 e_p5 e_pc".split())
        e_z, e_sz, e_yT, e_gt, e_o = (ev(n) for n in "e_z e_sz e_yT e_gt e_o".split())
        W = [bank[4], bank[5], bank[6], bank[7]]
        XBANK = [bank[0], bank[1]]
        SSB, YB = bank[2], bank[3]
        pair_w = lambda w, i, k: w[:, (i * KD + k) * P:(i * KD + k + 1) * P]
        xpair = [(xh[:, k, :], xl[:, k, :]) for k in range(KD)]
        y4 = lambda a: a.rearrange("p (k h d) -> p k h d", k=NC, h=2 * UN)

        xbanks = [bank[3], W[3], W[0], W[1]]

        def prep_pe(e, b, r):
            def inner(t):
                for k in range(KD):
                    ins = e.matmul(xbanks[t][:, :], xn[:, k, t * P:(t + 1) * P], wx_sb[:, k, :], start=k == 0, stop=k == KD - 1)
                e_p2.mark(ins)

            a_aw.wait(e, 6 * (b + 1))
            for k in range(KD):
                ins = e.matmul(W[0][0:NH, :], wdth_sb[:, k, :], xn[:, k, 0:SEQ], start=k == 0, stop=k == KD - 1)
            for s in range(2):
                for t in range(TT):
                    for k in range(KD):
                        ins = e.matmul(W[1 + s][:, t * P:(t + 1) * P], xn[:, k, t * P + s:(t + 1) * P + s], wdtl_sb[:, k, :],
                                       start=k == 0, stop=k == KD - 1)
            e_p1.mark(ins)
            e_xl.wait(e, KD * (r + 1))
            A_pe(e, b * NP, 0)
            inner(0)
            inner(1)
            A_pe(e, b * NP + 1, 1)
            e_pd.wait(e, b * PREP_STEPS + 3)
            inner(2)
            inner(3)
            ss_pe(e, b * NP, 0)
            ss_pe(e, b * NP + 1, 1)
            e_p4.hold(e, b + 1)
            for k in range(NC):
                ins = e.matmul(W[2][CL:P, k * CL:(k + 1) * CL], dect[:, k * CL:(k + 1) * CL], ident[0:NH, 0:NH],
                               start=True, stop=True)
            e_p5.mark(ins)
            A_pe(e, b * NP + 2, 2)

        def prep_act(e, b):
            e_p1.wait(e, b + 1)
            parts = ((sp_e[0:NH, 0, :], W[0][0:NH, :]), (tok(sp_e, 1), steps_of(0)), (tok(sp_e, 2), steps_of(1)))
            for s in range(2):
                ins = e.activation(lamk[:, s], tail_of(s), ACT.Sigmoid)
            e_p3.mark(ins)
            for o, i in parts:
                ins = e.activation(o, i, ACT.Abs)
            e_pc.mark(ins)
            A_act(e, b * NP, 0, [0])
            e_pc.wait(e, 6 * b + 1)
            e.activation(hm(sp_e), hm(sp_e), ACT.Exp, scale=-1.0)
            e_pc.mark(e.activation(tm(sp_e), tm(sp_e), ACT.Exp, scale=-1.0))
            e_pc.mark(e.activation(neg_a[:, :], neg_a[:, :], ACT.Exp))
            A_act(e, b * NP, 0, [1])
            e_pc.wait(e, 6 * b + 3)
            e_pc.mark(e.activation(neg_a[:, :], neg_a[:, :], ACT.Copy, scale=-1.0))
            e_pu.wait(e, b + 1)
            e.activation(hm(sp_l), hm(sp_u), ACT.Ln)
            e_pc.mark(e.activation(tm(sp_l), tm(sp_u), ACT.Ln))
            A_act(e, b * NP, 0, [2, 3])
            sb_act(e, b * NP + 2, 0, b * (NP // 2) + 2)
            e_pc.wait(e, 6 * b + 5)
            e_p6.wait(e, b + 1)
            e_pc.mark(e.activation(alpha, dth, ACT.Exp, scale=neg_a[:, 0:1]))
            A_act(e, b * NP + 1, 1, [0, 1])
            sq_act(e, b * NP)
            e_p4.wait(e, b + 1)
            e_p3.mark(e.activation(hrow_hi, hrow, ACT.Copy))
            A_act(e, b * NP + 1, 1, [2, 3])
            sq_act(e, b * NP + 1)
            e_p5.wait(e, b + 1)
            src = W[2][CL:P, :].rearrange("p (k a q) -> p k q a", k=NC, a=2)
            e_p3.mark(e.activation(decay_t[CL:P, :, :, :], src, ACT.Copy))

        PREP_STEPS = 10
        e_pd, e_pu, e_p6 = ev("e_pd"), ev("e_pu"), ev("e_p6")
        sp_e, sp_u, sp_l = rot[1][:, 0:2, :], rot[1][:, 2:4, :], btr
        hm, tm = (lambda a: a[0:NH, 0, :]), (lambda a: a[:, 1, :])
        tok = lambda a, s: a[:, 1, (s - 1) * TT * NH:s * TT * NH].rearrange("p (t n) -> p t n", t=TT)
        steps_of = lambda s: W[1 + s][:, :].rearrange("p (t n) -> p t n", t=TT)[:, :, 0:NH]
        tail_of = lambda s: W[1 + s][:, :].rearrange("p (t n) -> p t n", t=TT)[:, :, NH:]

        def prep_dve(e, b):
            n = [0]
            def step(ins):
                e_pd.mark(ins)
                n[0] += 1
                e_pd.wait(e, b * PREP_STEPS + n[0])

            starts = lambda a: a.rearrange("p (k c) -> p k c", k=NC)[:, :, 0:1]
            e.memset(st_in[:, :], 0.0)
            e.memset(one[:, :], 1.0)
            e_pc.wait(e, 6 * b + 2)
            for part in (hm, tm):
                ins = e.tensor_scalar(part(sp_u), part(sp_e), 1.0, None, ALU.add)
            e_pu.mark(ins)
            e_pu.wait(e, b + 1)
            for part in (hm, tm):
                ins = e.scalar_tensor_tensor(part(sp_e), part(sp_u), 1.0, part(sp_e), ALU.subtract, ALU.subtract)
            step(ins)
            e_pc.wait(e, 6 * b + 5)
            for part in (hm, tm):
                ins = e.tensor_tensor(part(sp_l), part(sp_l), part(sp_e), ALU.subtract)
            step(ins)
            e_p6.mark(e.scalar_tensor_tensor(dth, W[0][0:NH, :], 0.0, sp_l[0:NH, 0, :], ALU.max, ALU.add))
            for s in range(2):
                ins = e.scalar_tensor_tensor(dtk[:, s], steps_of(s), 0.0, tok(sp_l, s + 1), ALU.max, ALU.add)
            step(ins)
            e_pc.wait(e, 6 * b + 6)
            step(e.tensor_copy(alpha0, alpha))
            step(e.memset(starts(alpha0), 0.0))
            step(e.tensor_tensor(alpha, alpha, alpha0, ALU.subtract))
            step(e.tensor_tensor_scan(dect, alpha0, alpha, 0.0, ALU.mult, ALU.add))
            e.tensor_copy(hrow[:, 0:SEQ], dth)
            e.tensor_copy(hrow[:, SEQ:2 * SEQ], alpha0)
            e.memset(hrow[:, 2 * SEQ:2 * SEQ + 1], 0.0)
            ends = dect.rearrange("p (k c) -> p k c", k=NC)[:, 0:NC - 1, CL - 1]
            e_p4.mark(e.tensor_copy(hrow[:, 2 * SEQ + 1:ROWW], ends))
            e_p3.wait(e, 3 * b + 2)
            e_p4b.mark(e.tensor_tensor(hrow_lo, hrow, hrow_hi.bitcast(F32), ALU.subtract))
            e.tensor_tensor(gam, lamk[:, 0], dtk[:, 0], ALU.mult)
            step(e.tensor_scalar(oml, lamk[:, 1], -1.0, 1.0, ALU.mult, ALU.add))
            step(e.tensor_tensor(dlt, oml, dtk[:, 1], ALU.mult))
            step(e.tensor_tensor(coef, gam, dlt, ALU.add))
            assert n[0] == PREP_STEPS
            wide = lambda a, t: a[:, t, :].unsqueeze(2).to_broadcast([P, NH, HP])
            for t in range(TT):
                e_p2.wait(e, TT * b + t + 1)
                src = xbanks[t][:, :].rearrange("p (n d) -> p n d", n=NH)
                e.tensor_tensor(x1[:, :, t, :], src, wide(coef, t), ALU.mult)
                ins = e.tensor_tensor(x2[:, :, t, :], src, wide(gam, t), ALU.mult)
            e_x12.mark(ins)

        e_x12 = ev("e_x12")
        e_p4b = ev("e_p4b")

        def attn_load_sp(e, b):
            for s in range(2):
                a_th[s].mark(e.dma_start(th_raw[s][:, :], w_th[s]))
                a_wb[s].mark(e.dma_start(wb_raw[s][:, :], w_bc[s]))
            for dst, src in ((wx_sb, w_x), (wdtl_sb, w_dtl), (wdth_sb, w_dth),
                             (bias, bias_in), (norm_w, norm_w_in), (neg_a, a_log)):
                a_aw.mark(e.dma_start(dst[:], src))

        def early_sp(e, b):
            e_tP.hold(e, b * NP + 1)
            a_th[0].mark(e.dma_start(th_raw[0][:, :], w_th[2]))
            for i in range(2):
                e_bP.hold(e, b * NP + 1 + i)
                a_wb[i].mark(e.dma_start(wb_raw[i][:, :], w_bc[2 + i]))

        def attn_start_act(e, b):
            st_act(e, b * NP, 0, b * (NP // 2) + 1)
            sb_act(e, b * NP, 0, b * (NP // 2) + 1)
            sb_act(e, b * NP + 1, 1, b * (NP // 2) + 1)

        def prep_sp(e, b):
            for hl, src, evt in ((0, hrow_hi, (e_p3, 3 * b + 2)), (1, hrow_lo, (e_p4b, b + 1))):
                evt[0].hold(e, evt[1])
                src = src[:, :].bitcast(F32)
                for a in range(2):
                    r = slice(a * NP, (a + 1) * NP)
                    a_roww.mark(e.dma_start(row_dram[:, 2 * a + hl, 0:SEQ], src[r, 0:SEQ]))
                    a_roww.mark(e.dma_start(row_dram[:, 2 * a + hl, 2 * SEQ:ROWW], src[r, 2 * SEQ:ROWW]))
                    for kp in range(2):
                        dst = row_dram[:, 2 * kp + hl, SEQ + a * (SEQ // 2):SEQ + (a + 1) * (SEQ // 2)]
                        s4 = src[r, SEQ:2 * SEQ].rearrange("p (t k c) -> p t k c", t=TT, k=2)
                        a_roww.mark(e.dma_start(dst.rearrange("q (t c) -> q t c", t=TT), s4[:, :, kp, :]))
            a_roww.hold(e, 16 * (b + 1))
            for j in range(2):
                a_rows[j].mark(e.dma_start(rows[32 * j:32 * j + 4, :].bitcast(F32), row_dram[j]))

        def T_pe(e, m, j):
            e_tP.wait(e, m + 1)
            e_bt.wait(e, 2 * (m - 2))
            e_th.mark(split_matmul(e, W[2][:, :], [((pair_w(th_hi[j % 2], 0, k), pair_w(th_lo[j % 2], 0, k)), xpair[k])
                                                   for k in range(KD)], True, True))
            e_H.wait(e, m - 2)
            r = slice(32 * (j % 4), 32 * (j % 4) + 4)
            e_dtb.mark(e.matmul(W[3][:, :], row_sel[r, :], rows[r, 0:SEQ], start=True, stop=True))

        def T_dve1(e, m, j):
            e_ths.wait(e, m + 1)
            e_dtb.wait(e, m + 1)
            e_nfr.wait(e, m)
            e_tu.mark(e.tensor_tensor(turns[:, :], ths[:, :], W[3][:, :], ALU.mult))
            e_tu.wait(e, m + 1)
            e_cum.mark(e.tensor_tensor_scan(cum[:, :], ones, turns[:, :], 0.0, ALU.mult, ALU.add))

        def T_dve2(e, m, j):
            e_rnd.wait(e, m + 1)
            e_cs.wait(e, m)
            e_cum.wait(e, m + 1)
            e_nfr.mark(e.scalar_tensor_tensor(nfr[:, :], rnd[:, :], MAGIC, cum[:, :], ALU.subtract, ALU.subtract))

        def T_act1(e, m, j):
            e_th.wait(e, m + 1)
            e_tu.wait(e, m)
            e_cs.wait(e, m)
            e_ths.mark(e.activation(ths[:, :], W[2][:, :], ACT.Copy, scale=float(1 / (2 * np.pi))))

        def T_act2(e, m, j):
            e_cum.wait(e, m + 1)
            e_nfr.wait(e, m)
            e_rnd.mark(e.activation(rnd[:, :], cum[:, :], ACT.Identity, bias=magic[:, 0:1]))

        def T_act3(e, m, j):
            e_nfr.wait(e, m + 1)
            e_t.wait(e, 2 * (m - 1))
            e_afr.mark(e.activation(afr[:, :], nfr[:, :], ACT.Abs))
            e.activation(sn[j % 2][:, :], nfr[:, :], ACT.Sin, scale=-TWO_PI)
            e_afr.wait(e, m + 1)
            e_cs.mark(e.activation(cs[j % 2][:, :], afr[:, :], ACT.Sin, scale=-TWO_PI, bias=half_pi[:, 0:1]))

        def A_pe(e, m, j, parts=range(4)):
            if parts[0] == 0:
                e_bP.wait(e, m + 1)
            for i in parts:
                e_X.wait(e, 4 * m + i - 1)
                e_pj.mark(split_matmul(e, XBANK[i % 2][:, :],
                                       [((pair_w(wb_hi[j % 2], i, k), pair_w(wb_lo[j % 2], i, k)), xpair[k])
                                        for k in range(KD)], True, True))

        def ss_pe(e, m, j):
            if j % 2 == 0:
                e_sr.wait(e, m // 2 if isinstance(m, int) else m >> 1)
            for ty in range(2):
                e_sql.wait(e, 2 * m + ty + 1)
                c = (j % 2) * 2 + ty
                for part in (sq_hi, sq_lo):
                    ins = e.matmul(SSB[:, :], one_hot[:, 6 - 2 * c:6 - 2 * c + P], part[:, ty, :],
                                   start=c == 0 and part is sq_hi, stop=c == 3 and part is sq_lo, skip_group_check=True)
                e_ssm.mark(ins)

        def A_act(e, m, j, parts=range(4)):
            if parts[0] == 0:
                e_t.wait(e, 2 * (m - 3))
            for i in parts:
                e_pj.wait(e, 4 * m + i + 1)
                e.activation(xbc[j % 4][:, i, :], XBANK[i % 2][:, :], ACT.Copy)
                if i % 2 == 0:
                    e_sqs.wait(e, 2 * m + i // 2)
                e_X.mark(e.activation(sqt[:, i % 2, :], XBANK[i % 2][:, :], ACT.Square))

        def A_pool(e, m, types=range(2)):
            for ty in types:
                e_X.wait(e, 4 * m + 2 * ty + 2)
                e_sql.wait(e, 2 * (m - 1) + ty + 1)
                e_sqs.mark(e.tensor_tensor(sqs[:, ty, :], sqt[:, 0, :], sqt[:, 1, :], ALU.add))

        def sq_act(e, m, types=range(2)):
            for ty in types:
                e_sqs.wait(e, 2 * m + ty + 1)
                e_ssm.wait(e, 2 * (m - 1) + ty + 1)
                e_sqh.mark(e.activation(sq_hi[:, ty, :], sqs[:, ty, :], ACT.Copy))

        def sq_pool(e, m, types=range(2)):
            for ty in types:
                e_sqh.wait(e, 2 * m + ty + 1)
                e_sql.mark(e.tensor_tensor(sq_lo[:, ty, :], sqs[:, ty, :], sq_hi[:, ty, :].bitcast(F32), ALU.subtract))

        e_sqh, e_sql = ev("e_sqh"), ev("e_sql", 2)

        def sb_act(e, m, j, cnt):
            a_wb[j % 2].wait(e, cnt)
            e_pj.wait(e, 4 * (m - 1))
            e_bA.mark(e.activation(wb_hi[j % 2][:, :], wb_raw[j % 2][:, :], ACT.Copy))

        def sb_pool(e, m, j):
            e_bA.wait(e, m + 1)
            e_bP.mark(e.tensor_tensor(wb_lo[j % 2][:, :], wb_raw[j % 2][:, :], wb_hi[j % 2][:, :].bitcast(F32), ALU.subtract))

        def st_act(e, m, j, cnt):
            a_th[j % 2].wait(e, cnt)
            e_th.wait(e, m - 1)
            e_tA.mark(e.activation(th_hi[j % 2][:, :], th_raw[j % 2][:, :], ACT.Copy))

        def st_pool(e, m, j):
            e_tA.wait(e, m + 1)
            e_tP.mark(e.tensor_tensor(th_lo[j % 2][:, :], th_raw[j % 2][:, :], th_hi[j % 2][:, :].bitcast(F32), ALU.subtract))

        def R_act(e, gm):
            e_ssm.wait(e, 4 * (gm + 1))
            a_r1.wait(e, gm)
            e_sr.mark(e.activation(stdr, SSB[0:8, :], ACT.Sqrt, scale=1.0 / NS, bias=eps_nm[0:8, 0:1]))

        def R_dve(e, gm):
            a_r1.wait(e, gm + 1)
            a_r2.wait(e, 2 * gm)
            e_rc.mark(e.reciprocal(rc[:, :], rc_in[:, :]))
            e_rc.wait(e, 2 * gm + 1)
            e_rc.mark(e.tensor_copy(rc_hi[:, :], rc[:, :]))
            e_rc.wait(e, 2 * gm + 2)
            e_rl.mark(e.tensor_tensor(rc_lo[:, :], rc[:, :], rc_hi[:, :].bitcast(F32), ALU.subtract))

        e_rc = ev("e_rc")

        def R_sp(e, gm, par, cnt):
            e_sr.hold(e, gm + 1)
            e_rl.hold(e, gm)
            a_r1.mark(e.dma_start(rc_in[:, :], stdr.rearrange("r (c w) -> r c w", w=32)))
            e_rl.hold(e, gm + 1)
            for hl, src in ((0, rc_hi), (1, rc_lo)):
                dst = rr_dram[par][hl].rearrange("r (c w) -> (r c) w", w=32)
                a_r2.mark(e.dma_start(dst, src[:, :].bitcast(F32)))
            a_r2.hold(e, 2 * (gm + 1))
            e_rC.hold(e, 2 * (gm - 1))
            for a in range(2):
                src = rr_dram[par].rearrange("h (g a) t -> a h g t", a=2)[a]
                a_rr[par].mark(e.dma_start(rrow[32 * par + 2 * a:32 * par + 2 * a + 2, :, :].bitcast(F32), src))

        def F_pe(e, n, j, cnt):
            par = (j // 2) % 2
            if j % 2 == 0:
                a_rr[par].wait(e, 2 * cnt)
            e_M.wait(e, n - 1)
            r = slice(32 * par, 32 * par + 4)
            for ty, evt in ((0, e_rB), (1, e_rC)):
                evt.mark(e.matmul(W[ty][:, :], row_sel[r, :], rrow[r, (j % 2) * 2 + ty, :], start=True, stop=True))

        def F_pe2(e, n, j, with_T):
            e_ths.wait(e, n + 2 if with_T else n + 1)
            r = slice(32 * j, 32 * j + 4)
            e_aB.mark(e.matmul(W[2][:, :], row_sel[r, :], rows[r, SEQ:2 * SEQ], start=True, stop=True))

        def F_dve1(e, n, j):
            e_X.wait(e, 4 * (n + 1))
            for ty, src, dst in ((0, e_rB, e_xb), (1, e_rC, e_xcc)):
                src.wait(e, n + 1)
                for i in (2 * ty, 2 * ty + 1):
                    ins = e.scalar_tensor_tensor(xbc[j][:, i, :], xbc[j][:, i, :], norm_w[:, i:i + 1], W[ty][:, :], ALU.mult, ALU.mult)
                dst.mark(ins)

        def F_dve2(e, n, j):
            p2, dk = j % 2, dks[j % 2]
            e_aB.wait(e, n + 1)
            e_M.wait(e, n - 1)
            e_D.mark(e.tensor_tensor_scan(dk, constant("shift_mask"), W[2][:, :], 0.0, ALU.add, ALU.mult))
            e_D.wait(e, n + 1)
            e_xp.wait(e, n + 1)
            e_S.wait(e, n - 1)
            dend = dk.rearrange("p (c w) -> p c w", w=CL)[:, :, CL - 1:CL].to_broadcast([P, 2 * TT, PW])
            e_xw.mark(e.scalar_tensor_tensor(xwp[p2][:, :].rearrange("p (c w) -> p c w", w=PW), dend, constant("last_row"),
                                             x1p[j][:, :].rearrange("p (c w) -> p c w", w=PW), ALU.add, ALU.mult))

        def F_dve3(e, n, j, q, types):
            if types[0] == 0:
                e_xcc.wait(e, n + 1)
                e_cs.wait(e, n + 1)
                e_Y.wait(e, n - 1)
                e_R.wait(e, n)
            X, R, c, s = xbc[j], rot[j % 2], cs[j % 2], sn[j % 2]
            for ty in types:
                bias_of = lambda i: bias[:, bass.ds(q, 1) if not isinstance(q, int) else slice(q, q + 1), i:i + 1].rearrange("p a c -> p (a c)")
                for o, i, f in ((R[:, 2 * ty, :], 2 * ty, c), (tmp[:, 2 * ty, :], 2 * ty + 1, s),
                                (R[:, 2 * ty + 1, :], 2 * ty, s), (tmp[:, 2 * ty + 1, :], 2 * ty + 1, c)):
                    ins = e.scalar_tensor_tensor(o, X[:, i, :], bias_of(i), f[:, :], ALU.add, ALU.mult)
                e_t.mark(ins)

        def F_pool(e, n, j, types):
            R = rot[j % 2]
            for ty in types:
                e_t.wait(e, 2 * n + ty + 1)
                e.tensor_tensor(R[:, 2 * ty, :], R[:, 2 * ty, :], tmp[:, 2 * ty, :], ALU.subtract)
                ins = e.tensor_tensor(R[:, 2 * ty + 1, :], R[:, 2 * ty + 1, :], tmp[:, 2 * ty + 1, :], ALU.add)
            if ty == 1:
                e_R.mark(ins)

        def XP_pool(e, n, j, q):
            e_Y.wait(e, n - 3)
            mask = constant("chunk_mask").rearrange("p (c k d) -> p c k d", c=2 * TT, k=2)
            for dst, src in ((x1p, x1), (x2p, x2)):
                v = src[:, bass.ds(2 * q, 2) if not isinstance(q, int) else slice(2 * q, 2 * q + 2), :, :]
                v = v.rearrange("p a t d -> p (a t) d").unsqueeze(2).to_broadcast([P, 2 * TT, 2, HP])
                ins = e.tensor_tensor(dst[j % 4][:, :].rearrange("p (c k d) -> p c k d", c=2 * TT, k=2), v, mask, ALU.mult)
            e_xp.mark(ins)

        def K1_pe(e, p, j, with_F, with_T):
            R = rot[j % 2]
            e_R.wait(e, p + 1)
            e_tu.hold(e, p + 1 + with_F + with_T)
            for a in range(2):
                if a and with_F:
                    e_xb.hold(e, p + 2)
                dst, h = W[3 if a == 0 else 0], slice(CL * a, CL * a + CL)
                for k in range(NC):
                    o = dst[CL * (k % 2):CL * (k % 2) + CL, CL * (k // 2):CL * (k // 2) + CL]
                    for eo in range(2):
                        ins = e.matmul(o, R[h, eo, CL * k:CL * k + CL], R[h, 2 + eo, CL * k:CL * k + CL],
                                       start=eo == 0, stop=eo == 1)
            e_G.mark(ins)
            for eo in range(2):
                if with_F:
                    (e_xcc, e_D)[eo].wait(e, p + 2)
                for t in range(TT):
                    ins = e.transpose(W[1 + eo][:, t * P:(t + 1) * P], R[:, eo, t * P:(t + 1) * P], ident[:, :])
                e_bte.mark(ins)

        def K_act(e, p, j):
            for eo in range(2):
                e_bte.wait(e, 2 * p + eo + 1)
                e_S.wait(e, p)
                e_bt.mark(e.activation(btr[:, eo, :], W[1 + eo][:, :], ACT.Copy))

        def K_dve1(e, p, j):
            e_G.wait(e, p + 1)
            e_D.wait(e, p + 1)
            e_Y.wait(e, p)
            half, dk = slice(0, SEQ // 2), dks[j % 2]
            for a in range(2):
                g, c = W[3 if a == 0 else 0][:, half], slice(a * SEQ // 2, (a + 1) * SEQ // 2)
                e.tensor_tensor(m1[:, c], g, dk[:, c], ALU.mult)
                ins = e.tensor_tensor(m2[:, c], g, constant("diag_mask")[:, c], ALU.mult)
            e_M.mark(ins)

        def K2_pe(e, p, j):
            e_bt.wait(e, 2 * (p + 1))
            e_xw.wait(e, p + 1)
            e_M.wait(e, p + 1)
            xw = xwp[j % 2][:, :].rearrange("p (a t w) -> p a t w", a=2, t=TT)
            S = W[3]
            for eo in range(2):
                for t in range(TT):
                    nk = 2 if t < TT - 1 else 1
                    o = S[:, eo * 128:(eo + 1) * 128].rearrange("p (a d k) -> p a k d", a=2, d=HP)[:, :, 2 * t + 1:2 * t + 1 + nk, :]
                    i = xw[:, :, t, :].rearrange("p a (k d) -> p a k d", k=2)[:, :, 0:nk, :]
                    e.matmul(o, btr[:, eo, t * P:(t + 1) * P], i, start=True, stop=True)
            r = slice(32 * j, 32 * j + 4)
            ends = rows[r, 2 * SEQ:ROWW].unsqueeze(1).to_broadcast([4, 32, NC])
            e_S.mark(e.matmul(S[:, 256:512].rearrange("p (c k) -> p c k", k=NC), row_sel[r, :], ends, start=True, stop=True))

        def K_dve2(e, p, j):
            e_S.wait(e, p + 1)
            e_Y.wait(e, p)
            v = lambda a: a.rearrange("p (c k) -> p c k", k=NC)[:, :, 1:NC]
            e_sm.mark(e.tensor_tensor(v(st_in[:, :]), v(W[3][:, 0:256]),
                                      constant("head_mask").rearrange("p (c k) -> p c k", k=NC - 1), ALU.mult))
            e_sm.wait(e, p + 1)
            e_H.mark(e.tensor_tensor_scan(st[:, :], W[3][:, 256:512], st_in[:, :], 0.0, ALU.mult, ALU.add))

        def Y_pe(e, p, j, yev):
            if j == 0:
                e_yev.wait(e, yev)
            R, y, hist = rot[j % 2], YB[:, :].rearrange("p (k w) -> p k w", k=NC), st[:, :].rearrange("p (o w k) -> p o w k", o=2, k=NC)
            c16 = slice(PW * j, PW * j + PW)
            c4 = lambda a: a.rearrange("p (c k d) -> p c k d", k=2, d=HP)
            for a in range(2):
                for t in range(TT):
                    o = y[0:CL, 2 * t:2 * t + 2, PW * j + HP * a:PW * j + HP * a + HP]
                    for n, (m, x) in enumerate(((m1, x1p), (m2, x2p))):
                        e.matmul(o, m[:, (a * TT + t) * CL:(a * TT + t + 1) * CL], c4(x[j][:, :])[:, a * TT + t],
                                 start=n == 0, stop=n == 1)
            e_H.wait(e, p + 1)
            for k in range(NC):
                for eo in range(2):
                    ins = e.matmul(y[CL:P, k, c16], R[:, 2 + eo, CL * k:CL * k + CL], hist[:, eo, :, k], start=eo == 0, stop=eo == 1)
            e_Y.mark(ins)

        def Y_dve(e, p, q4, n):
            e_Y.wait(e, p + 1)
            if isinstance(q4, int):
                dec, cols = decay_t[CL:P, :, q4:q4 + UN, :], slice(q4 * PW, (q4 + UN) * PW)
            else:
                dec, cols = decay_t[CL:P, :, bass.ds(q4, UN), :], bass.ds(q4 * PW, UN * PW)
            dec = dec.rearrange("p k q a -> p k (q a)").unsqueeze(3).to_broadcast([CL, NC, 2 * UN, HP])
            e_ym.mark(e.tensor_tensor(y4(ytmp), y4(YB[CL:P, :]), dec, ALU.mult))
            e_ym.wait(e, n + 1)
            for h in range(2):
                of = lambda a: a.rearrange("p (t h w) -> p t h w", t=TT, h=2)[:, :, h, :]
                ins = e.tensor_tensor(ysb[h * CL:(h + 1) * CL, :, cols], of(ytmp), of(YB[0:CL, :]), ALU.add)
            e_yev.mark(ins)

        e_ym = ev("e_ym")

        def turn(eng, e, b, it, first, last):
            N, Q = b * NP + it * UN, it * UN
            NB = NP // UN
            for j in range(UN):
                n, q, p = N + j, Q + j, N + j - 1
                jp = (j - 1) % UN
                T = not (last and j == UN - 1)
                A = not last or j == 0
                SS = not last or j <= 1
                RG = j % 2 == 1 and not (last and j == 3)
                K = not (first and j == 0)
                gm = b * (NP // 2) + it * 2 + j // 2
                if eng == "pe":
                    if first and j == 1:
                        e_D.wait(e, n)
                    if T:
                        a_rows[(j + 1) % 4].wait(e, b * NB + it + 1 + (j == 3))
                        T_pe(e, n + 1, j + 1)
                    if A:
                        A_pe(e, n + 3, j + 3, [0])
                    F_pe(e, n, j, b * NB + it + 1)
                    F_pe2(e, n, j, T)
                    if A:
                        A_pe(e, n + 3, j + 3, [1])
                    if SS:
                        ss_pe(e, n + 2, j)
                    if last and j >= 2:
                        z_pe(e, b, j - 2)
                    if K:
                        K1_pe(e, p, jp, True, T)
                    if A:
                        A_pe(e, n + 3, j + 3, [2])
                    if K:
                        K2_pe(e, p, jp)
                    if A:
                        A_pe(e, n + 3, j + 3, [3])
                    if K:
                        Y_pe(e, p, jp, b * NB + it)
                elif eng == "act":
                    if T:
                        T_act1(e, n + 1, j + 1)
                    if SS and not (first and j == 1):
                        sq_act(e, n + 2, [1])
                    if not (last and j >= 2):
                        st_act(e, n + 2, j, b * (NP // 2) + it * 2 + 2 + j // 2)
                    if A:
                        A_act(e, n + 3, j + 3, [0])
                    if not last:
                        sb_act(e, n + 4, j, b * (NP // 2) + it * 2 + 3 + j // 2)
                    if T:
                        T_act2(e, n + 1, j + 1)
                    if RG:
                        R_act(e, gm + 1)
                    if A:
                        A_act(e, n + 3, j + 3, [1])
                    if K:
                        K_act(e, p, jp)
                    if A:
                        sq_act(e, n + 3, [0])
                    if T:
                        T_act3(e, n + 1, j + 1)
                    if last and j >= 2:
                        z_act(e, b, j - 2)
                    if A:
                        A_act(e, n + 3, j + 3, [2, 3])
                    if first and j == 0:
                        sq_act(e, n + 3, [1])
                elif eng == "pool":
                    if SS and not (first and j == 1):
                        sq_pool(e, n + 2, [1])
                    if not (last and j >= 2):
                        st_pool(e, n + 2, j)
                    if not last:
                        sb_pool(e, n + 4, j)
                    if A:
                        A_pool(e, n + 3, [0])
                    if T:
                        XP_pool(e, n + 1, j + 1, q + 1)
                    if A:
                        sq_pool(e, n + 3, [0])
                    if first and j == 0:
                        A_pool(e, n + 3, [1])
                        sq_pool(e, n + 3, [1])
                    F_pool(e, n, j, [0])
                    if A and not (first and j == 0):
                        A_pool(e, n + 3, [1])
                    F_pool(e, n, j, [1])
                elif eng == "dve":
                    if j == 1 and not first:
                        Y_dve(e, n - 2, q - 1 - UN, b * NB + it - 1)
                    if T:
                        T_dve1(e, n + 1, j + 1)
                    F_dve1(e, n, j)
                    F_dve2(e, n, j)
                    if T:
                        T_dve2(e, n + 1, j + 1)
                    early = last and j >= 1
                    if early:
                        F_dve3(e, n, j, q, [0])
                    if K:
                        K_dve1(e, p, jp)
                    if not early:
                        F_dve3(e, n, j, q, [0])
                    if RG:
                        R_dve(e, gm + 1)
                    if K:
                        if last and j >= 2:
                            F_dve3(e, n, j, q, [1])
                        K_dve2(e, p, jp)
                    if not (last and j >= 2):
                        F_dve3(e, n, j, q, [1])
                elif eng == "sp":
                    if not (last and j >= 2):
                        e_S.hold(e, n - 1)
                        s = (j + 2) % 4
                        src = row_dram[q + 2] if isinstance(q, int) else row_dram[bass.ds(q + 2, 1)].rearrange("a r w -> (a r) w")
                        a_rows[s].mark(e.dma_start(rows[32 * s:32 * s + 4, :].bitcast(F32), src))
                    if not (last and j >= 1):
                        e_tP.hold(e, n + 2)
                        src = w_th[q + 3] if isinstance(q, int) else w_th[bass.ds(q + 3, 1)].rearrange("a p w -> (a p) w")
                        a_th[(j + 1) % 2].mark(e.dma_start(th_raw[(j + 1) % 2][:, :], src))
                    if not last:
                        e_bP.hold(e, n + 3)
                        src = w_bc[q + 4] if isinstance(q, int) else w_bc[bass.ds(q + 4, 1)].rearrange("a p w -> (a p) w")
                        a_wb[j % 2].mark(e.dma_start(wb_raw[j % 2][:, :], src))
                    if RG:
                        R_sp(e, gm + 1, (j // 2 + 1) % 2, b * NB + it + 1)

        def pairs(eng, e, b):
            N, NB = b * NP, NP // UN
            G = b * (NP // 2)
            if eng == "pe":
                e_p3.wait(e, 3 * b + 3)
                e_x12.wait(e, b + 1)
                a_rows[0].wait(e, b * NB + 1)
                T_pe(e, N, 0)
                e_tu.wait(e, N + 1)
            elif eng == "act":
                R_act(e, G)
                st_act(e, N + 1, 1, G + 1)
                A_act(e, N + 2, 2)
                sb_act(e, N + 3, 1, G + 2)
                T_act1(e, N, 0)
                T_act2(e, N, 0)
                T_act3(e, N, 0)
                sq_act(e, N + 2, [0])
            elif eng == "pool":
                st_pool(e, N, 0)
                sb_pool(e, N, 0)
                sb_pool(e, N + 1, 1)
                A_pool(e, N)
                sb_pool(e, N + 2, 0)
                sq_pool(e, N)
                A_pool(e, N + 1)
                sq_pool(e, N + 1)
                e_x12.wait(e, b + 1)
                XP_pool(e, N, 0, 0)
                st_pool(e, N + 1, 1)
                A_pool(e, N + 2)
                sb_pool(e, N + 3, 1)
                sq_pool(e, N + 2, [0])
            elif eng == "dve":
                R_dve(e, G)
                T_dve1(e, N, 0)
                T_dve2(e, N, 0)
            elif eng == "sp":
                R_sp(e, G, 0, b * NB + 1)
            turn(eng, e, b, 0, True, False)
            with e.Fori(1, NB - 1) as it:
                turn(eng, e, b, it, False, False)
            turn(eng, e, b, NB - 1, False, True)
            if eng == "sp":
                e_t.hold(e, 2 * (N + NP - 3))
                a_tw.mark(e.dma_start(wz_sb, w_z))
                a_tw.mark(e.dma_start(wo_sb, w_out))
            p, j = N + NP - 1, UN - 1
            if eng == "pe":
                z_pe(e, b, 2)
                K1_pe(e, p, j, False, False)
                K2_pe(e, p, j)
                z_pe(e, b, 3)
                Y_pe(e, p, j, 0)
            elif eng == "act":
                K_act(e, p, j)
                z_act(e, b, 2)
                z_act(e, b, 3)
            elif eng == "dve":
                K_dve1(e, p, j)
                K_dve2(e, p, j)
                Y_dve(e, p, NP - UN, b * NB + NB - 1)

        def z_pe(e, b, f):
            a_tw.wait(e, 2 * (b + 1))
            if f >= 2:
                e_sz.wait(e, KI * b + f - 1)
            for k in range(KD):
                ins = e.matmul(XBANK[f % 2][:, :], wz_sb[:, k, f * P:(f + 1) * P], xn[:, k, 0:SEQ], start=k == 0, stop=k == KD - 1)
            e_z.mark(ins)

        def z_act(e, b, f):
            e_sql.wait(e, 2 * (b + 1) * NP)
            e_z.wait(e, KI * b + f + 1)
            e_sz.mark(e.activation(silu_z[f], XBANK[f % 2][:, :], ACT.Silu))

        def tail_pe(e, b):
            e_sz.wait(e, KI * (b + 1))
            e_yev.wait(e, (b + 1) * (NP // UN))
            for f in range(KI):
                for t in range(TT):
                    ins = e.transpose(bank[f][:, t * P:(t + 1) * P], ysb[:, t, f * P:(f + 1) * P], ident[:, :])
                e_yT.mark(ins)
            e_gt.wait(e, KI * (b + 1))
            for m in range(KD):
                for f in range(KI):
                    ins = e.matmul(bank[4 + m][:, :], wo_sb[:, f, m * P:(m + 1) * P], gated[:, f, :], start=f == 0, stop=f == KI - 1)
                e_o.mark(ins)

        def tail_dve(e, b, s):
            e_Y.wait(e, (b + 1) * NP)
            for f in range(KI):
                e_sz.wait(e, KI * b + f + 1)
                e_yT.wait(e, KI * b + f + 1)
                e_gt.mark(e.tensor_tensor(gated[:, f, :], silu_z[f], bank[f][:, :], ALU.mult))
            for m in range(KD):
                e_o.wait(e, KD * b + m + 1)
                e.tensor_tensor(stream(s)(m), stream(s)(m), bank[4 + m][:, :], ALU.add)

        NCONST = 4
        LNS = 3 * SG
        seq_of = lambda a, n: a[bass.ds(n, 1), :, :, :].rearrange("a p k t -> (a p) k t")
        block = ctx.enter_context(nc.Block())

        def give_ahead(e, n):
            for v in events[n::5]:
                v.give_ahead(e)

        @block.tensor
        def _(e):
            give_ahead(e, 0)
            a_const.wait(e, NCONST)
            e_init.wait(e, 3)
            with e.Fori(0, BATCH // SG) as bp:
                a_x.wait(e, SG * (bp + 1))
                ffn_start("pe", e, 2 * bp, LNS * bp)
                ffn_pe(e, 2 * bp)
                end_phase(e, PHASES * bp)
                with e.Fori(0, SG) as s:
                    b = bp * SG + s
                    layernorm("pe", e, LNS * bp + SG + s, [stream(s)], None)
                    e_xn.wait(e, KD * (LNS * bp + SG + s + 1))
                    prep_pe(e, b, LNS * bp + SG + s)
                    pairs("pe", e, b)
                    tail_pe(e, b)
                    end_phase(e, PHASES * bp + 1 + s)
                ffn_start("pe", e, 2 * bp + 1, LNS * bp + 2 * SG)
                ffn_pe(e, 2 * bp + 1)
                end_phase(e, PHASES * bp + PHASES - 1)

        @block.scalar
        def _(e):
            give_ahead(e, 1)
            a_const.wait(e, NCONST)
            e.activation(sel[:, :, :], sel_raw[:, :, :], ACT.Copy)
            e.activation(one_hot[:, :], constant("one_hot"), ACT.Copy)
            e_init.mark(e.activation(row_sel[:, :], constant("row_sel"), ACT.Copy))
            e_init.wait(e, 3)
            with e.Fori(0, BATCH // SG) as bp:
                ffn_start("act", e, 2 * bp, LNS * bp)
                router_act(e, 2 * bp)
                ffn_act(e, 2 * bp)
                end_phase(e, PHASES * bp)
                with e.Fori(0, SG) as s:
                    b = bp * SG + s
                    layernorm("act", e, LNS * bp + SG + s, [stream(s)], lambda: attn_start_act(e, b))
                    prep_act(e, b)
                    pairs("act", e, b)
                    end_phase(e, PHASES * bp + 1 + s)
                ffn_start("act", e, 2 * bp + 1, LNS * bp + 2 * SG)
                router_act(e, 2 * bp + 1)
                ffn_act(e, 2 * bp + 1)
                end_phase(e, PHASES * bp + PHASES - 1)

        @block.gpsimd
        def _(e):
            give_ahead(e, 2)
            e.memset(zero_w[:, :].bitcast(F32), 0.0)
            e.memset(mean_w[:, :], 1.0 / D)
            e.memset(xn[:, :, SEQ:], 0.0)
            e.memset(eps_nm[:, :], EPS_NORM)
            e.memset(magic[:, :], MAGIC)
            e.memset(half_pi[:, :], float(np.pi / 2))
            e_init.mark(e.memset(eps_ln[:, :], EPS_LN))
            with e.Fori(0, BATCH // SG) as bp:
                ffn_pool(e, 2 * bp)
                end_phase(e, PHASES * bp)
                with e.Fori(0, SG) as s:
                    b = bp * SG + s
                    pairs("pool", e, b)
                    end_phase(e, PHASES * bp + 1 + s)
                ffn_pool(e, 2 * bp + 1)
                end_phase(e, PHASES * bp + PHASES - 1)

        @block.vector
        def _(e):
            give_ahead(e, 3)
            e_init.mark(e.memset(top[:, :, :], 0.0))
            with e.Fori(0, BATCH // SG) as bp:
                ffn_start("dve", e, 2 * bp, LNS * bp)
                router_dve(e, 2 * bp)
                ffn_dve(e, 2 * bp)
                end_phase(e, PHASES * bp)
                with e.Fori(0, SG) as s:
                    b = bp * SG + s
                    layernorm("dve", e, LNS * bp + SG + s, [stream(s)], lambda: None)
                    a_aw.wait(e, 6 * (b + 1))
                    prep_dve(e, b)
                    pairs("dve", e, b)
                    tail_dve(e, b, s)
                    end_phase(e, PHASES * bp + 1 + s)
                ffn_start("dve", e, 2 * bp + 1, LNS * bp + 2 * SG)
                router_dve(e, 2 * bp + 1)
                ffn_dve(e, 2 * bp + 1)
                end_phase(e, PHASES * bp + PHASES - 1)

        @block.sync
        def _(e):
            give_ahead(e, 4)
            a_const.mark(e.dma_start(sel_raw[:, :, :], sel_ffn_in))
            a_const.mark(e.dma_start(ident[:, :], ident_in))
            a_const.mark(e.dma_start(wr_sb[:, :, :], w_router))
            a_const.mark(e.dma_start(cst[:, :], cst_in))
            with e.Fori(0, BATCH // SG) as bp:
                for s in range(SG):
                    a_x.mark(e.dma_start(xs[:, s], seq_of(x_in, bp * SG + s)))
                ffn_load_sp(e, 2 * bp)
                router_sp(e, 2 * bp)
                ffn_sp(e, 2 * bp)
                end_phase(e, PHASES * bp)
                with e.Fori(0, SG) as s:
                    b = bp * SG + s
                    attn_load_sp(e, b)
                    early_sp(e, b)
                    prep_sp(e, b)
                    pairs("sp", e, b)
                    end_phase(e, PHASES * bp + 1 + s)
                ffn_load_sp(e, 2 * bp + 1)
                router_sp(e, 2 * bp + 1)
                ffn_sp(e, 2 * bp + 1)
                for s in range(SG):
                    e_xo.hold(e, (2 * bp + 1) * SG + s + 1)
                    a_out.mark(e.dma_start(seq_of(out, bp * SG + s), xs[:, s]))
                a_out.hold(e, SG * (bp + 1))
                end_phase(e, PHASES * bp + PHASES - 1)


def feature_major(w):
    return np.ascontiguousarray(w.reshape(-1, P, w.shape[1]).transpose(1, 0, 2))


def arrays_of(a):
    x = a["L0_attn_x"].transpose(0, 2, 1).reshape(BATCH, KD, P, SEQ).transpose(0, 2, 1, 3)
    groups = []
    for n in range(NG):
        s = slice(n * GE, (n + 1) * GE)
        g, u = (a[w][s].transpose(1, 0, 2).reshape(KD, P, GT * P).transpose(1, 0, 2).reshape(P, -1)
                for w in ("L0_ffn_Wg", "L0_ffn_Wu"))
        d = a["L0_ffn_Wd"][s].reshape(GT, P, D).transpose(1, 0, 2).reshape(P, -1)
        groups.append(np.concatenate([g, u, d], axis=1))
    def tiles(w, eo):
        w = w.reshape(NP, 2, -1, eo, D).transpose(0, 3, 4, 1, 2).reshape(NP, eo, KD, P, P)
        return w.transpose(0, 3, 1, 2, 4)
    bc = np.concatenate([tiles(a["L0_attn_WB"], 2), tiles(a["L0_attn_WC"], 2)], axis=2).reshape(NP, P, BCW)
    th = tiles(a["L0_attn_Wth"], 1).reshape(NP, P, THW)
    per_row = lambda v: v.reshape(NP, 2, NS // 2, 2).transpose(1, 2, 0, 3).reshape(P, NP, 2)
    bias = np.concatenate([per_row(a["L0_attn_B_bias"]), per_row(a["L0_attn_C_bias"])], axis=2)
    nw = np.concatenate([np.tile(a[w].reshape(NS // 2, 2), (2, 1)) for w in ("L0_attn_Bn_w", "L0_attn_Cn_w")], axis=1)
    by_parity = lambda v: v.reshape(NP, 2, -1).transpose(1, 0, 2).reshape(NH, -1)
    sel = np.zeros((2 * GE, GT, P), np.float32)
    for i in range(GT):
        for p in range(P):
            n = (i * P + p) // NI
            sel[2 * n:2 * n + 2, i, p] = 1.0
    p = np.arange(P)
    t = np.arange(SEQ) % CL
    shift = (t[None] == p[:, None] % CL + 1).astype(np.float32)
    diag = (t[None] == p[:, None] % CL).astype(np.float32)
    last = (p % CL == CL - 1).astype(np.float32)[:, None]
    head = (p[:, None, None, None, None] // CL == np.arange(2)[None, None, :, None, None]) * np.ones((P, 2, 2, HP, NC - 1))
    chunk = (p[:, None, None, None] // CL == np.arange(2)[None, None, :, None]) * np.ones((P, 2 * TT, 2, HP))
    row_sel = ((p[:, None] % 32) // 2 == p[None] // CL) * np.ones((P, P))
    one_hot = np.zeros((P, P + 6))
    one_hot[p, 6 + p // CL] = 1.0
    cst = np.concatenate([v.reshape(P, -1) for v in (shift, diag, last, head, chunk, row_sel, one_hot)], axis=1)
    arrays = {
        "x_in": x,
        "w_ffn": np.stack(groups),
        "w_router": feature_major(a["L0_ffn_Wr"].T),
        "w_bc": bc,
        "w_th": th,
        "w_x": feature_major(a["L0_attn_Wx"].T),
        "w_z": feature_major(a["L0_attn_Wz"].T),
        "w_dtl": feature_major(np.concatenate([a["L0_attn_Wdt"], a["L0_attn_Wlam"]]).T),
        "w_dth": feature_major(by_parity(a["L0_attn_Wdt"]).T),
        "a_log": by_parity(a["L0_attn_A_log"]),
        "w_out": feature_major(a["L0_attn_Wout"].T),
        "bias_in": bias,
        "norm_w_in": nw,
        "sel_ffn_in": sel,
        "ident_in": np.eye(P, dtype=np.float32),
        "cst_in": cst.astype(np.float32),
    }
    return {k: np.ascontiguousarray(v) for k, v in arrays.items()}


def kernel(**inputs):
    import concourse.bacc as bacc
    from concourse.bass_utils import run_bass_kernel_spmd

    arrays = arrays_of({k: np.asarray(v) for k, v in inputs.items()})
    nc = bacc.Bacc("TRN2", target_bir_lowering=False, num_devices=1)
    args = [nc.dram_tensor(n, v.shape, mybir.dt.from_np(v.dtype), kind="ExternalInput").ap() for n, v in arrays.items()]
    out = nc.dram_tensor("out_x", (BATCH, P, KD, SEQ), F32, kind="ExternalOutput").ap()
    build(nc, *args, out)
    r = run_bass_kernel_spmd(nc, [arrays], core_ids=[0])
    got = r.results[0]["out_x"]
    return np.ascontiguousarray(got.transpose(0, 3, 2, 1).reshape(BATCH, SEQ, D))
```
